# Optimizing a Trainium2 kernel written in Bass

```python
import numpy as np
import jax
import jax.numpy as jnp

def _softmax(x, axis=-1):
    return jax.nn.softmax(x, axis=axis)

def _gelu(x):
    return jax.nn.gelu(x, approximate=True)

def _silu(x):
    return jax.nn.silu(x)

def _sigmoid(x):
    return jax.nn.sigmoid(x)

def _layernorm(x, axis=-1, eps=1e-05):
    m = jnp.mean(x, axis=axis, keepdims=True)
    v = jnp.var(x, axis=axis, keepdims=True)
    return (x - m) / jnp.sqrt(v + eps)

def _scatter_add(tgt, idx, src, axis=0):
    return tgt.at[idx].add(src)

def _segment_sum(src, seg, n):
    return jax.ops.segment_sum(src, seg, n)
kernel_name = 'mk_early_fusion_d1_tok_img1024_r4_c85035'

def setup_inputs(seed: int=0):
    np.random.seed(seed)
    _w = jnp.asarray

    def _rec_inputs():
        import jax
        import jax.numpy as jnp
        _rk = jax.random.key(seed)
        x = -0.00016672 + 0.999947 * jax.random.normal(jax.random.fold_in(_rk, 1), (8, 3, 96, 96), jnp.float32)
        txt = 0.501581 + 0.625929 * jax.random.normal(jax.random.fold_in(_rk, 2), (8, 128, 256), jnp.float32)
        return (x, txt)
    x, txt = _rec_inputs()

    def _L0_tok_setup():
        import jax, jax.numpy as jnp
        import numpy as np
        key = jax.random.key(seed)
        kx, kw, kpos = jax.random.split(key, 3)
        B, C, H, W = (64, 3, 96, 96)
        p, dim = (16, 256)
        n_patches = H // p * (W // p)
        x = jax.random.normal(kx, (B, C, H, W), dtype=jnp.float32)
        w = jax.random.normal(kw, (dim, C * p * p), dtype=jnp.float32) * 0.02
        b = jnp.zeros((dim,), dtype=jnp.float32)
        cls_token = jnp.ones((dim,), dtype=jnp.float32)
        pos = jax.random.uniform(kpos, (n_patches + 1, dim), dtype=jnp.float32)
        return {'x': x, 'w': w, 'b': b, 'cls_token': cls_token, 'pos': pos, 'patch_size': p}
    _L0_tok_all = _L0_tok_setup()
    _L0_tok_in = {k: v for k, v in _L0_tok_all.items() if k in ('w', 'b', 'cls_token', 'pos')}
    del _L0_tok_all

    def _L0_attn_setup():
        import jax, jax.numpy as jnp
        import numpy as np
        D_MODEL = 256
        NUM_HEADS = 16
        HEAD_DIM = D_MODEL // NUM_HEADS
        ROPE_THETA = 10000.0

        def apply_rope(x):
            S, d_k = (x.shape[-2], x.shape[-1])
            inv_freq = ROPE_THETA ** (jnp.arange(0, d_k, 2, dtype=jnp.float32) / d_k)
            ang = jnp.arange(S, dtype=jnp.float32)[:, None] / inv_freq[None, :]
            cos, sin = (jnp.cos(ang), jnp.sin(ang))
            xp = x.reshape(x.shape[:-1] + (d_k // 2, 2))
            x0, x1 = (xp[..., 0], xp[..., 1])
            out = jnp.stack([x0 * cos - x1 * sin, x0 * sin + x1 * cos], axis=-1)
            return out.reshape(x.shape)
        key = jax.random.key(seed)
        k1, k2, k3 = jax.random.split(key, 3)
        B, S = (2, 512)
        std = 2.0 / (D_MODEL + 3 * D_MODEL)
        std_o = 2.0 / (D_MODEL + D_MODEL)
        return {'x': jax.random.normal(k1, (B, S, D_MODEL), dtype=jnp.float32), 'W_qkv': jax.random.normal(k2, (3 * D_MODEL, D_MODEL), dtype=jnp.float32) * std, 'W_o': jax.random.normal(k3, (D_MODEL, D_MODEL), dtype=jnp.float32) * std_o}
    _L0_attn_all = _L0_attn_setup()
    _L0_attn_in = {k: v for k, v in _L0_attn_all.items() if k in ('W_qkv', 'W_o')}
    del _L0_attn_all

    def _L0_ffn_setup():
        import jax, jax.numpy as jnp
        import numpy as np
        DIM = 256
        HIDDEN = 1024
        E = 8
        B, S = (2, 1024)
        key = jax.random.key(seed)
        ks = jax.random.split(key, 8)
        sd = 1.0 / np.sqrt(DIM)
        sh = 1.0 / np.sqrt(HIDDEN)
        return {'x': jax.random.normal(ks[0], (B, S, DIM), dtype=jnp.float32), 'router_w': jax.random.uniform(ks[1], (DIM, E), jnp.float32, -sd, sd), 'router_b': jax.random.uniform(ks[2], (E,), jnp.float32, -sd, sd), 'w1': jax.random.uniform(ks[3], (E, DIM, 2 * HIDDEN), jnp.float32, -sd, sd), 'b1': jax.random.uniform(ks[4], (E, 2 * HIDDEN), jnp.float32, -sd, sd), 'w2': jax.random.uniform(ks[5], (E, HIDDEN, DIM), jnp.float32, -sh, sh), 'b2': jax.random.uniform(ks[6], (E, DIM), jnp.float32, -sh, sh)}
    _L0_ffn_all = _L0_ffn_setup()
    _L0_ffn_in = {k: v for k, v in _L0_ffn_all.items() if k in ('router_w', 'router_b', 'w1', 'b1', 'w2', 'b2')}
    del _L0_ffn_all
    return {'x': x, 'txt': txt, 'L0_tok_w': _L0_tok_in['w'], 'L0_tok_b': _L0_tok_in['b'], 'L0_tok_cls_token': _L0_tok_in['cls_token'], 'L0_tok_pos': _L0_tok_in['pos'], 'L0_attn_W_qkv': _L0_attn_in['W_qkv'], 'L0_attn_W_o': _L0_attn_in['W_o'], 'L0_ffn_router_w': _L0_ffn_in['router_w'], 'L0_ffn_router_b': _L0_ffn_in['router_b'], 'L0_ffn_w1': _L0_ffn_in['w1'], 'L0_ffn_b1': _L0_ffn_in['b1'], 'L0_ffn_w2': _L0_ffn_in['w2'], 'L0_ffn_b2': _L0_ffn_in['b2']}

def reference(x, txt, L0_tok_w, L0_tok_b, L0_tok_cls_token, L0_tok_pos, L0_attn_W_qkv, L0_attn_W_o, L0_ffn_router_w, L0_ffn_router_b, L0_ffn_w1, L0_ffn_b1, L0_ffn_w2, L0_ffn_b2):
    import jax
    import jax.numpy as jnp

    def _L0_tok_ref(x, w, b, cls_token, pos, patch_size):
        import jax, jax.numpy as jnp
        import numpy as np
        B, C, H, W = x.shape
        p = patch_size
        Hp, Wp = (H // p, W // p)
        dim = w.shape[0]
        patches = x.reshape(B, C, Hp, p, Wp, p).transpose(0, 2, 4, 1, 3, 5).reshape(B, Hp * Wp, C * p * p)
        tokens = jnp.einsum('bnf,df->bnd', patches, w) + b
        cls = jnp.broadcast_to(cls_token, (B, 1, dim))
        emb = jnp.concatenate([cls, tokens], axis=1)
        return emb + pos

    def _L0_attn_ref(x, W_qkv, W_o):
        import jax, jax.numpy as jnp
        import numpy as np
        D_MODEL = 256
        NUM_HEADS = 16
        HEAD_DIM = D_MODEL // NUM_HEADS
        ROPE_THETA = 10000.0

        def apply_rope(x):
            S, d_k = (x.shape[-2], x.shape[-1])
            inv_freq = ROPE_THETA ** (jnp.arange(0, d_k, 2, dtype=jnp.float32) / d_k)
            ang = jnp.arange(S, dtype=jnp.float32)[:, None] / inv_freq[None, :]
            cos, sin = (jnp.cos(ang), jnp.sin(ang))
            xp = x.reshape(x.shape[:-1] + (d_k // 2, 2))
            x0, x1 = (xp[..., 0], xp[..., 1])
            out = jnp.stack([x0 * cos - x1 * sin, x0 * sin + x1 * cos], axis=-1)
            return out.reshape(x.shape)
        B, S, d_model = x.shape
        H, d_k = (NUM_HEADS, HEAD_DIM)
        qkv = jnp.einsum('bsi,oi->bso', x, W_qkv)
        Q, K, V = jnp.split(qkv, 3, axis=-1)

        def to_heads(t):
            return t.reshape(B, S, H, d_k).transpose(0, 2, 1, 3)
        Q, K, V = (to_heads(Q), to_heads(K), to_heads(V))
        Q, K = (apply_rope(Q), apply_rope(K))
        scores = jnp.einsum('bhqd,bhkd->bhqk', Q, K) / jnp.sqrt(jnp.float32(d_k))
        causal = jnp.tril(jnp.ones((S, S), dtype=bool))
        scores = jnp.where(causal, scores, -jnp.inf)
        attn = jax.nn.softmax(scores, axis=-1)
        out = jnp.einsum('bhqk,bhkd->bhqd', attn, V)
        out = out.transpose(0, 2, 1, 3).reshape(B, S, d_model)
        return jnp.einsum('bsi,oi->bso', out, W_o)

    def _L0_ffn_ref(x, router_w, router_b, w1, b1, w2, b2):
        import jax, jax.numpy as jnp
        import numpy as np
        DIM = 256
        HIDDEN = 1024
        E = 8
        B, S = (2, 1024)
        logits = jnp.einsum('bsd,de->bse', x, router_w) + router_b
        probs = jax.nn.softmax(logits, axis=-1)
        top1 = jnp.argmax(probs, axis=-1)
        out = jnp.zeros_like(x)
        for i in range(E):
            h = jnp.einsum('bsd,df->bsf', x, w1[i]) + b1[i]
            a, g = jnp.split(h, 2, axis=-1)
            y = jnp.einsum('bsh,hd->bsd', a * jax.nn.sigmoid(g), w2[i]) + b2[i]
            out = out + jnp.where((top1 == i)[..., None], y, 0.0)
        return out
    h = _L0_tok_ref(x, L0_tok_w, L0_tok_b, L0_tok_cls_token, L0_tok_pos, 16)
    h = jnp.concatenate([h, txt], axis=1)
    h = h + _L0_attn_ref(_layernorm(h, axis=-1), L0_attn_W_qkv, L0_attn_W_o)
    h = h + _L0_ffn_ref(_layernorm(h, axis=-1), L0_ffn_router_w, L0_ffn_router_b, L0_ffn_w1, L0_ffn_b1, L0_ffn_w2, L0_ffn_b2)
    return h

_drawn_inputs = setup_inputs


def setup_inputs(seed=0):
    import zlib

    import numpy as np

    out = dict(_drawn_inputs(seed))
    spreads = {'L0_tok_b': (0.0, 0.1), 'L0_tok_cls_token': (1.0, 0.6)}
    factors = {'L0_attn_W_qkv': 8.0, 'L0_attn_W_o': 8.0, 'L0_ffn_b1': 4.246}
    for name, (base, spread) in spreads.items():
        noise = np.random.default_rng([zlib.crc32(name.encode()), seed]).standard_normal(out[name].shape)
        drawn = base * np.exp(spread * noise) if base else spread * noise
        out[name] = jnp.asarray(drawn.astype(out[name].dtype))
    for name, factor in factors.items():
        out[name] = (out[name] * factor).astype(out[name].dtype)
    return out
```

```python
from contextlib import ExitStack

import numpy as np

import concourse.bass as bass
from concourse import mybir

F32 = mybir.dt.float32
F16 = mybir.dt.float16
BF16 = mybir.dt.bfloat16
I32 = mybir.dt.int32
ALU = mybir.AluOpType
ACT = mybir.ActivationFunctionType
AX = mybir.AxisListType.X

B, D, H, DH = 8, 256, 16, 16
NPATCH, EMB, TXT = 36, 37, 128
S = EMB + TXT
MAIN, TAIL = 128, S - 128
PAIRS = B // 2
TAILS = 64
PR = TAILS + TAIL
KP = 6
E, HID = 8, 1024
NTOK = B * S
TT = 208
HT = TT // 2
MAXT = -(-NTOK // TT)
U32 = 3
PIECES = 8
CAP = MAXT * TT
WS = 16.0
EPS = 1e-5
NEG = -1e30

COLS = {}
_at = 0
for _name, _n in (("ident", 128), ("mask_main", MAIN), ("mask_tail", S), ("cos", 4 * 8), ("sin", 4 * 8),
                  ("before", 128), ("head_rows", H), ("expert_m8", E), ("valid", 3), ("pad_place", 3),
                  ("id0", 3), ("list_base", E), ("tile_edges", MAXT - 1), ("lower", E * E), ("emb_rows", PR)):
    COLS[_name] = (_at, _at + _n)
    _at += _n
NCONST = _at


def constants():
    t = np.zeros((128, NCONST), np.float32)

    def put(name, a):
        lo, hi = COLS[name]
        t[:, lo:hi] = np.asarray(a, np.float32).reshape(-1, hi - lo)

    p = np.arange(128)
    put("ident", np.eye(128))
    put("mask_main", np.where(p[None, :] <= p[:, None], 0.0, NEG))
    row = p % TAILS
    real = row < TAIL
    k = np.arange(S)
    put("mask_tail", np.where((k[None, :] <= MAIN + row[:, None]) | ~real[:, None], 0.0, NEG))
    freq = (np.float32(10000.0) ** (np.arange(0, DH, 2, dtype=np.float32) / np.float32(DH))).astype(np.float32)
    pos = np.stack([p, MAIN + row]).astype(np.float32)
    ang = (pos[:, :, None] / freq[None, None, :]).astype(np.float32).transpose(1, 0, 2)
    cos, sin = np.cos(ang), np.sin(ang)
    put("cos", np.stack([cos, cos], 2).reshape(128, -1) / WS)
    put("sin", np.stack([-sin, sin], 2).reshape(128, -1) / WS)
    put("before", p[:, None] < p[None, :])
    r = p % 64
    put("head_rows", (r[:, None] == np.arange(H)) | (r[:, None] == H + np.arange(H)))
    put("expert_m8", np.tile(np.arange(E) - E, (128, 1)))
    put("valid", np.stack([p >= 0, p >= 0, real], 1))
    put("pad_place", np.stack([0 * p, 0 * p, np.where(real, 0, 4 * E * CAP)], 1))
    put("id0", np.stack([p, S + p, MAIN + row + S * (p >= TAILS)], 1))
    put("list_base", np.tile(np.arange(E) * CAP, (128, 1)))
    put("tile_edges", np.tile(np.arange(1, MAXT) * TT, (128, 1)))
    put("lower", np.tile((np.arange(E)[None, :] < np.arange(E)[:, None]).reshape(1, -1), (128, 1)))
    cls = np.zeros((128, PR))
    cls[0, [0, TAILS]] = 1
    cls[1, 1:EMB] = 1
    cls[1, TAILS + 1:TAILS + EMB] = 1
    put("emb_rows", cls)
    return t


class Signal:

    def __init__(self, sem, per_round, unit=1, start=True):
        self.sem, self.per_round, self.unit, self.start = sem, per_round, unit, per_round if start else 0

    def at(self, rnd, k):
        return (rnd * self.per_round + self.start + k) * self.unit

    def before(self, rnd):
        return self.at(rnd, 0)



def build(nc, patches, txt, w_emb, cls_b, pos, w_qkv, w_o, router_w, router_b, w1, b1, w2, b2, consts, out):
    rows_x = nc.dram_tensor("rows_x", (NTOK + 1, 2 * D), F16).ap()
    rows_h = nc.dram_tensor("rows_h", (NTOK + 1, D), F32).ap()
    id_list = nc.dram_tensor("id_list", (E * CAP + (E + MAXT + 1) * TT, 1), I32).ap()

    ctx = ExitStack()
    with ctx:
        def sb(name, shape, dt=F32):
            return ctx.enter_context(nc.sbuf_tensor(name, shape, dt))

        def psum(name, shape):
            return ctx.enter_context(nc.psum_tensor(name, shape, F32))

        def sig(name, per_round, unit=1, start=True):
            return Signal(ctx.enter_context(nc.semaphore(name)), per_round, unit, start)

        X = psum("X", [128, 2, 512])
        SC = [psum("SC0", [128, 2, 512]), psum("SC1", [128, 2, 512])]
        PV = psum("PV", [128, 2, 512])
        turn_banks = [X[:, 0, :], X[:, 1, :], PV[:, 0, :]]
        wo_banks = [PV[:, 1, :], X[:, 0, :], X[:, 1, :]]
        proj = [X, PV, X]
        up_banks = [SC[0][:, 0, :], SC[0][:, 1, :], SC[1][:, 0, :], SC[1][:, 1, :]]
        y_banks = [PV[:, 1, :], X[:, 0, :]]

        C = sb("C", [128, NCONST])

        def const(name, rows=128):
            lo, hi = COLS[name]
            return C[0:rows, lo:hi]

        ident = sb("ident", [128, 128], F16)
        identb = sb("identb", [128, 128], BF16)
        mask_main = sb("mask_main", [128, MAIN], BF16)
        mask_tail = sb("mask_tail", [128, S], BF16)
        before = sb("before", [128, 128], F16)
        ones = sb("ones", [128, 128], F16)
        head_sel = sb("head_sel", [128, H, 128], F16)
        cls_b_sb = sb("cls_b_sb", [2, D])
        pos_sb = sb("pos_sb", [128, D])
        wq_h = sb("wq_h", [128, 2, 3 * D], F16)
        wq_l = sb("wq_l", [128, 2, 3 * D], F16)
        wo_h = sb("wo_h", [128, 2, D], F16)
        wo_l = sb("wo_l", [128, 2, D], F16)
        rw_raw = sb("rw_raw", [128, 2, E])
        rw_h = sb("rw_h", [128, 2, E], F16)
        rw_l = sb("rw_l", [128, 2, E], F16)
        rb_sb = sb("rb_sb", [128, E])

        patch_sb = sb("patch_sb", [128, KP, PR])
        h0 = sb("h0", [128, 3, D])
        h1 = sb("h1", [128, 3, D])
        stats = sb("stats", [128, 3, 6])
        mv = sb("mv", [128, 3, 2])
        rstd = sb("rstd", [128, 3])
        xn = sb("xn", [128, 3, D])
        xn_h = sb("xn_h", [128, 3, D], F16)
        xn_l = sb("xn_l", [128, 3, D], F16)
        xT = sb("xT", [128, 3, 2, 2, 128], F16)
        rope_a = sb("rope_a", [128, 2 * D])
        rope_b = sb("rope_b", [128, 2 * D])
        qk = sb("qk", [128, 2, 2 * D])
        pack = sb("pack", [128, 2, 2, H, 64], F16)
        QT = sb("QT", [128, 2, 8, S], F16)
        KT = sb("KT", [128, 2, 8, S], F16)
        V_h = sb("V_h", [128, 3, H, DH + 1], F16)
        V_l = sb("V_l", [128, 3, H, DH + 1], F16)
        smax = sb("smax", [128, 3, H])
        neg_m = sb("neg_m", [128, 3, 2, 64], F16)
        mT = sb("mT", [128, 2, S], F16)
        P32t = sb("P32t", [128, 2, 8, TAIL])
        Pt_h = sb("Pt_h", [128, H, TAIL], F16)
        Pt_l = sb("Pt_l", [128, H, TAIL], F16)
        rinv = sb("rinv", [128, 3, H])
        O = sb("O", [128, 3, D])
        O_h = sb("O_h", [128, 3, D], F16)
        O_l = sb("O_l", [128, 3, D], F16)
        oT = sb("oT", [128, 3, 2, 2, 128], F16)
        stats2 = sb("stats2", [128, 3, 6])
        mv2 = sb("mv2", [128, 3, 2])
        rstd2 = sb("rstd2", [128, 3])
        xn2 = sb("xn2", [128, 3, D])
        x2_hl = sb("x2_hl", [128, 3, 2, D], F16)
        x2T = sb("x2T", [128, 3, 2, 2, 128], F16)
        logit = sb("logit", [128, 3, E])
        lmax = sb("lmax", [128, 3])
        tie = sb("tie", [128, 3, E])
        pick = sb("pick", [128, 3, E])
        first = sb("first", [128, 3])
        onehot = sb("onehot", [128, 3, E])
        onehot16 = sb("onehot16", [128, 3, E], F16)
        place_e = sb("place_e", [128, 3, E])
        place_f = sb("place_f", [128, 3])
        place = sb("place", [128, 3], I32)
        ids_f = sb("ids_f", [128, 3])
        ids = sb("ids", [128, 3], I32)
        pad_ids = sb("pad_ids", [128, E * CAP // 128], I32)
        zero_row = sb("zero_row", [1, D])
        minus_half = sb("minus_half", [128, 3])
        base = sb("base", [128, E])
        count = sb("count", [128, E])
        above = sb("above", [128, E, MAXT - 1])
        tiles = sb("tiles", [128, E])
        cum_all = sb("cum_all", [128, E, E])
        cum = sb("cum", [128, E])
        table_f = sb("table_f", [128, 2 * E + 1])
        table = sb("table", [128, 2 * E + 1], I32)

        W1N, W2N = 2 * 2 * HID, 8 * D
        WN = W1N + W2N
        PIECE = WN // PIECES
        w_raw = [sb(f"w_raw{u}", [128, WN]) for u in range(2)]
        w1_raw = [w[:, 0:W1N].rearrange("p (k n) -> p k n", k=2) for w in w_raw]
        w2_raw = [w[:, W1N:WN].rearrange("p (k n) -> p k n", k=8) for w in w_raw]
        b1_all = sb("b1_all", [128, E, 16])
        b2_all = sb("b2_all", [128, E, D])
        w_hi, w_lo = ([sb(f"w_{name}{u}", [128, WN], F16) for u in range(2)] for name in ("hi", "lo"))
        w1_h, w1_l = ([w[:, 0:W1N].rearrange("p (k n) -> p k n", k=2) for w in ws] for ws in (w_hi, w_lo))
        w2_h, w2_l = ([w[:, W1N:WN].rearrange("p (k n) -> p k n", k=8) for w in ws] for ws in (w_hi, w_lo))
        b1_lin = [sb(f"b1_lin{u}", [128, 8]) for u in range(2)]
        b1_gate = [sb(f"b1_gate{u}", [128, 8]) for u in range(2)]
        b2_e = [sb(f"b2_e{u}", [128, D]) for u in range(2)]
        idx_in = sb("idx_in", [HT, 2], I32)
        idx_out = sb("idx_out", [HT, 2], I32)
        Xg = sb("Xg", [HT, 2, 2 * D], F16)
        gT = sb("gT", [128, 2, 2, TT], F16)
        sigm = sb("sigm", [128, 2, TT])
        u32 = sb("u32", [128, U32, TT])

        spare = w_raw[1]
        wq_raw = spare[:, 0:6 * D].rearrange("p (k n) -> p k n", k=2)
        wo_raw = spare[:, 6 * D:8 * D].rearrange("p (k n) -> p k n", k=2)
        P32_flat = spare[:, 8 * D:8 * D + 12 * S].rearrange("p (x n) -> p x n", x=2)

        def P32(x, nj):
            return P32_flat[:, x, 0:2 * nj * S].rearrange("p (h q) -> p h q", q=S)

        def P32_par(x, nj):
            return P32(x, nj).rearrange("p (a j) q -> p a j q", a=2)

        w_emb_sb = w2_raw[1][:, 0:KP, :]
        P_h = w_hi[1][:, 0:2 * H * S].rearrange("p (u h q) -> p u h q", u=2, h=H)
        P_l = w_lo[1][:, 0:2 * H * S].rearrange("p (u h q) -> p u h q", u=2, h=H)
        pack_flat = pack[:, :, :, :, :].rearrange("p x m h s -> p (x m h s)")
        u_h = pack_flat[:, 0:8 * TT].rearrange("p (k n) -> p k n", k=8)
        u_l = pack_flat[:, 8 * TT:16 * TT].rearrange("p (k n) -> p k n", k=8)
        Hg, hb, yo = xn2[0:HT, 0:2, :], xn[0:HT, 0:2, :], O[0:HT, 0:2, :]

        passed = sig("passed", 1)
        const_in = sig("const_in", 1, 16)
        w_in = sig("w_in", 10, 16)
        const_ready = sig("const_ready", 10)
        split_h = sig("split_h", 3)
        w_ready = sig("w_ready", 3)
        filled = sig("filled", 9)
        fill_out = sig("fill_out", 1, 16)
        patches_in = sig("patches_in", 1, 16)
        txt_in = sig("txt_in", 4, 16)
        emb_ready = sig("emb_ready", 1)
        emb_added = sig("emb_added", 2)
        ln1 = sig("ln1", 9)
        rsqrt1 = sig("rsqrt1", 2)
        xn_hi = sig("xn_hi", 3)
        xn_lo = sig("xn_lo", 3)
        xn_turned = sig("xn_turned", 3)
        xT_ready = sig("xT_ready", 3)
        qkv_ready = sig("qkv_ready", 3)
        v_hi = sig("v_hi", 3)
        v_lo = sig("v_lo", 3)
        rope = sig("rope", 9)
        qk_ready = sig("qk_ready", 3)
        pack_hi = sig("pack_hi", 6)
        pack_lo = sig("pack_lo", 6)
        pack_turned = sig("pack_turned", 3)
        qT_ready = sig("qT_ready", 3)
        kT_ready = sig("kT_ready", 3)
        s_ready = sig("s_ready", 7)
        max_done = sig("max_done", 7)
        negm_hi = sig("negm_hi", 1)
        negm_ready = sig("negm_ready", 2)
        negm_turned = sig("negm_turned", 1)
        mT_ready = sig("mT_ready", 2)
        st_ready = sig("st_ready", 7)
        exp_done = sig("exp_done", 8)
        p_masked = sig("p_masked", 8)
        p_hi = sig("p_hi", 8)
        p_lo = sig("p_lo", 8)
        pv_ready = sig("pv_ready", 3)
        o_rinv = sig("o_rinv", 4)
        o_ready = sig("o_ready", 4)
        o_hi = sig("o_hi", 3)
        o_lo = sig("o_lo", 3)
        o_turned = sig("o_turned", 3)
        oT_ready = sig("oT_ready", 3)
        wo_ready = sig("wo_ready", 3)
        h1_ready = sig("h1_ready", 3)
        ln2 = sig("ln2", 9)
        rsqrt2 = sig("rsqrt2", 2)
        x2_hi = sig("x2_hi", 3)
        x2_lo = sig("x2_lo", 3)
        x2_turned = sig("x2_turned", 3)
        x2T_ready = sig("x2T_ready", 3)
        rows_out = sig("rows_out", 8, 16)
        logits_ready = sig("logits_ready", 1)
        route = sig("route", 14)
        ranks_ready = sig("ranks_ready", 1)
        ids_out = sig("ids_out", 3, 16, start=False)
        tabled = sig("tabled", 10)
        ew_in = [sig(f"ew_in{u}", 2, 16) for u in range(2)]
        ew_hi = sig("ew_hi", PIECES)
        ew_lo = sig("ew_lo", PIECES)
        bias_ready = sig("bias_ready", 3)
        idx_in_in = sig("idx_in_in", 1, 16)
        idx_out_in = sig("idx_out_in", 1, 16)
        x_in = sig("x_in", 2, 16, start=False)
        h_in = sig("h_in", 2, 16, start=False)
        g_turned = sig("g_turned", 1)
        gT_ready = sig("gT_ready", 1)
        up_ready = sig("up_ready", 8)
        sig_done = sig("sig_done", 8)
        glu_done = sig("glu_done", 8)
        u_hi = sig("u_hi", 8)
        u_lo = sig("u_lo", 8)
        y_ready = sig("y_ready", 2)
        hb_done = sig("hb_done", 1)
        yo_ready = sig("yo_ready", 2)
        out_done = sig("out_done", 2, 16)

        every = {
            "sync": [passed, const_in, w_in, fill_out, patches_in, txt_in, rows_out, *ew_in, idx_in_in, idx_out_in],
            "gpsimd": [rsqrt1, rsqrt2, xn_lo, p_masked, p_lo, o_lo, x2_lo, u_lo],
            "scalar": [xn_hi, xT_ready, v_hi, pack_hi, qT_ready, mT_ready, exp_done, o_hi, oT_ready, x2_hi,
                       x2T_ready, ew_hi, gT_ready, sig_done, split_h],
            "vector": [const_ready, w_ready, emb_added, ln1, v_lo, rope, qk_ready, pack_lo, kT_ready, max_done,
                       negm_hi, negm_ready, p_hi, o_rinv, o_ready, ew_lo, h1_ready, ln2, route, tabled,
                       bias_ready, filled, glu_done, u_hi, hb_done, yo_ready],
            "tensor": [emb_ready, xn_turned, qkv_ready, pack_turned, s_ready, negm_turned, st_ready, pv_ready,
                       o_turned, wo_ready, x2_turned, logits_ready, ranks_ready, g_turned, up_ready, y_ready],
        }

        def start_signals(eng, name):
            for s in every[name]:
                eng.sem_inc(s.sem, s.per_round * s.unit)

        def score_heads(q):
            return 6 * q, min(3, (H - 6 * q) // 2)

        def token_rows(dram, img, lo, n):
            return dram[bass.ds(img * S + lo, n), :]

        block = ctx.enter_context(nc.Block())

        @block.sync
        def _(sp):
            start_signals(sp, "sync")
            sp.dma_start(C[:, :], consts).then_inc(const_in.sem, 16)
            for dst, src in ((w_emb_sb[:, :, :], w_emb), (cls_b_sb[:, :], cls_b), (pos_sb[0:EMB, :], pos),
                             (pos_sb[TAILS:TAILS + EMB, :], pos), (wq_raw[:, :, :], w_qkv),
                             (wo_raw[:, :, :], w_o), (rw_raw[:, :, :], router_w),
                             (rb_sb[:, :], router_b.broadcast_to((128, E))), (b1_all[:, :, :], b1),
                             (b2_all[:, :, :].rearrange("p e d -> p (e d)"), b2.broadcast_to((128, E * D)))):
                sp.dma_start(dst, src).then_inc(w_in.sem, 16)
            sp.wait_ge(filled.sem, filled.at(0, 9))
            sp.dma_start(id_list[0:E * CAP, :].rearrange("(p n) a -> p (n a)", p=128), pad_ids[:, :]).then_inc(fill_out.sem, 16)
            def load_weights(e, u):
                sp.dma_start(w1_raw[u][:, :, :], w1[bass.ds(e, 1)].rearrange("a (k p) n -> p (a k) n", p=128)
                             ).then_inc(ew_in[u].sem, 16)
                sp.dma_start(w2_raw[u][:, :, :], w2[bass.ds(e, 1)].rearrange("a (k p) n -> p (a k) n", p=128)
                             ).then_inc(ew_in[u].sem, 16)

            def pair(i, ahead):
                sp.wait_ge(emb_ready.sem, emb_ready.before(i))
                sp.dma_start(patch_sb[:, :, :], patches[bass.ds(i, 1)].rearrange("a p k n -> p (a k) n")
                             ).then_inc(patches_in.sem, 16)
                sp.wait_ge(h1_ready.sem, h1_ready.before(i))
                for u in range(2):
                    img = txt[bass.ds(2 * i + u, 1)].rearrange("a t d -> (a t) d")
                    sp.dma_start(h0[EMB:128, u, :], img[0:MAIN - EMB, :]).then_inc(txt_in.sem, 16)
                    sp.dma_start(h0[TAILS * u:TAILS * u + TAIL, 2, :], img[MAIN - EMB:TXT, :]).then_inc(txt_in.sem, 16)
                ahead()
                sp.wait_ge(h1_ready.sem, h1_ready.at(i, 3))
                for u in range(2):
                    sp.dma_start(token_rows(rows_h, 2 * i + u, 0, MAIN), h1[:, u, :]).then_inc(rows_out.sem, 16)
                    sp.dma_start(token_rows(rows_h, 2 * i + u, MAIN, TAIL), h1[TAILS * u:TAILS * u + TAIL, 2, :]
                                 ).then_inc(rows_out.sem, 16)
                sp.wait_ge(x2_hi.sem, x2_hi.at(i, 3))
                sp.wait_ge(x2_lo.sem, x2_lo.at(i, 3))
                for u in range(2):
                    sp.dma_start(token_rows(rows_x, 2 * i + u, 0, MAIN),
                                 x2_hl[:, u, :, :].rearrange("p a b -> p (a b)")).then_inc(rows_out.sem, 16)
                    sp.dma_start(token_rows(rows_x, 2 * i + u, MAIN, TAIL),
                                 x2_hl[TAILS * u:TAILS * u + TAIL, 2, :, :].rearrange("p a b -> p (a b)")
                                 ).then_inc(rows_out.sem, 16)

            pair(0, lambda: load_weights(0, 0))
            with sp.Fori(1, PAIRS - 1) as i:
                pair(i, lambda: None)

            def second_expert():
                sp.wait_ge(emb_ready.sem, emb_ready.at(PAIRS - 1, 1))
                sp.wait_ge(p_hi.sem, p_hi.at(PAIRS - 1, 8))
                sp.wait_ge(p_lo.sem, p_lo.at(PAIRS - 1, 8))
                load_weights(1, 1)

            pair(PAIRS - 1, second_expert)

            def tile_ids(e):
                lo = sp.value_load(table[0:1, bass.ds(e, 1)], min_val=0, max_val=E + MAXT)
                hi = sp.value_load(table[0:1, bass.ds(e + 1, 1)], min_val=1, max_val=E + MAXT)
                off = sp.value_load(table[0:1, bass.ds(e + E + 1, 1)], min_val=0, max_val=E * CAP)
                with sp.Fori(lo, hi) as g:
                    places = id_list[bass.ds(g * TT + off, TT), :].rearrange("(s p) a -> p (s a)", s=2)
                    with nc.allow_non_contiguous_dma(reason="ids, one to a partition"):
                        sp.wait_ge(g_turned.sem, g_turned.before(g))
                        sp.wait_ge(hb_done.sem, hb_done.before(g))
                        sp.dma_start(idx_in[:, :], places).then_inc(idx_in_in.sem, 16)
                        sp.wait_ge(out_done.sem, out_done.before(g))
                        sp.dma_start(idx_out[:, :], places).then_inc(idx_out_in.sem, 16)

            sp.wait_ge(tabled.sem, tabled.at(0, 10))
            sp.wait_ge(ids_out.sem, ids_out.at(PAIRS - 1, 3))
            with sp.Fori(0, E) as e:
                tile_ids(e)
            last = sp.value_load(table[0:1, E:E + 1], min_val=E, max_val=E + MAXT)
            sp.wait_ge(g_turned.sem, g_turned.before(last))
            sp.wait_ge(hb_done.sem, hb_done.before(last))
            with nc.allow_non_contiguous_dma(reason="ids, one to a partition"):
                sp.dma_start(idx_in[:, :], id_list[0:TT, :].rearrange("(s p) a -> p (s a)", s=2)
                             ).then_inc(idx_in_in.sem, 16)
            sp.wait_ge(out_done.sem, out_done.before(last))
            sp.sem_inc(passed.sem, 1)

        @block.gpsimd
        def _(pool):
            start_signals(pool, "gpsimd")
            def inverse_deviation(i, mvt, rs, moments, rsqrt):
                pool.wait_ge(moments.sem, moments.at(i, 6))
                pool.sem_inc(passed.sem, 1)
                pool.tensor_scalar(rs[:, :], mvt[:, :, 1], EPS, None, ALU.add).then_inc(rsqrt.sem, 1)
                pool.wait_ge(rsqrt.sem, rsqrt.at(i, 1))
                pool.tensor_tensor(rs[:, :], rs[:, :], minus_half[:, :], ALU.pow).then_inc(rsqrt.sem, 1)

            pool.wait_ge(filled.sem, filled.at(0, 9))
            pool.dma_start(rows_x[NTOK:NTOK + 1, :], zero_row[0:1, :].bitcast(F16)).then_inc(out_done.sem, 16)
            pool.dma_start(rows_h[NTOK:NTOK + 1, :], zero_row[0:1, :]).then_inc(out_done.sem, 16)
            pool.wait_ge(out_done.sem, out_done.before(0))
            pool.wait_ge(fill_out.sem, fill_out.at(0, 1))
            with pool.Fori(0, PAIRS) as i:
                inverse_deviation(i, mv, rstd, ln1, rsqrt1)
                for t in range(3):
                    pool.wait_ge(xn_hi.sem, xn_hi.at(i, t + 1))
                    pool.tensor_tensor(xn_l[:, t, :], xn[:, t, :], xn_h[:, t, :], ALU.subtract).then_inc(xn_lo.sem, 1)
                n = 0
                for u in range(2):
                    for q in range(3):
                        h, nj = score_heads(q)
                        pool.wait_ge(exp_done.sem, exp_done.at(i, n + 1))
                        pool.sem_inc(passed.sem, 1)
                        diag = P32(n % 2, nj)[:, :, 0:MAIN]
                        pool.affine_select(out=diag, in_=diag, compare_op=ALU.is_ge, fill=0.0, base=0,
                                           pattern=[[0, 2 * nj], [1, MAIN]], channel_multiplier=-1
                                           ).then_inc(p_masked.sem, 1)
                        pool.wait_ge(p_hi.sem, p_hi.at(i, n + 1))
                        pool.tensor_tensor(by_parity(P_l[:, u, h:h + 2 * nj, :]), P32_par(n % 2, nj),
                                           by_parity(P_h[:, u, h:h + 2 * nj, :]), ALU.subtract).then_inc(p_lo.sem, 1)
                        n += 1
                for u in range(2):
                    rows = slice(TAILS * u, TAILS * u + TAIL)
                    pool.wait_ge(exp_done.sem, exp_done.at(i, n + 1))
                    pool.sem_inc(passed.sem, 1)
                    pool.wait_ge(p_lo.sem, p_lo.at(i, n))
                    pool.sem_inc(passed.sem, 1)
                    pt = P32t[rows, :, :, :].rearrange("p a b q -> p (a b) q")
                    pool.affine_select(out=pt, in_=pt, compare_op=ALU.is_ge, fill=0.0, base=0,
                                       pattern=[[0, H], [1, TAIL]], channel_multiplier=-1).then_inc(p_masked.sem, 1)
                    pool.wait_ge(p_hi.sem, p_hi.at(i, n + 1))
                    pool.tensor_tensor(by_parity(Pt_l[rows]), P32t[rows], by_parity(Pt_h[rows]), ALU.subtract
                                       ).then_inc(p_lo.sem, 1)
                    n += 1
                pool.wait_ge(p_lo.sem, p_lo.at(i, 8))
                for t in range(3):
                    pool.wait_ge(o_hi.sem, o_hi.at(i, t + 1))
                    pool.tensor_tensor(O_l[:, t, :], O[:, t, :], O_h[:, t, :], ALU.subtract).then_inc(o_lo.sem, 1)
                inverse_deviation(i, mv2, rstd2, ln2, rsqrt2)
                for t in range(3):
                    pool.wait_ge(x2_hi.sem, x2_hi.at(i, t + 1))
                    pool.tensor_tensor(x2_hl[:, t, 1, :], xn2[:, t, :], x2_hl[:, t, 0, :], ALU.subtract
                                       ).then_inc(x2_lo.sem, 1)
                pool.wait_ge(route.sem, route.at(i, 14))
                pool.sem_inc(passed.sem, 1)
                for t in range(3):
                    pool.indirect_dma_start(
                        out=id_list[:, :], out_offset=bass.IndirectOffsetOnAxis(ap=place[:, t:t + 1], axis=0),
                        in_=ids[:, t:t + 1], in_offset=None, bounds_check=E * CAP - 1, oob_is_err=False,
                    ).then_inc(ids_out.sem, 16)
                pool.wait_ge(ids_out.sem, ids_out.at(i, 3))

            pool.wait_ge(tabled.sem, tabled.at(0, 10))
            pool.wait_ge(rows_out.sem, rows_out.at(PAIRS - 1, 8))

            def gather_x(g, s):
                if s == 0:
                    pool.wait_ge(idx_in_in.sem, idx_in_in.at(g, 1))
                    pool.sem_inc(passed.sem, 1)
                    pool.wait_ge(g_turned.sem, g_turned.before(g))
                    pool.sem_inc(passed.sem, 1)
                pool.indirect_dma_start(
                    out=Xg[:, s, :], out_offset=None, in_=rows_x[:, :],
                    in_offset=bass.IndirectOffsetOnAxis(ap=idx_in[:, s:s + 1], axis=0),
                    bounds_check=NTOK, oob_is_err=False).then_inc(x_in.sem, 16)

            def gather_h(g):
                pool.wait_ge(hb_done.sem, hb_done.before(g))
                pool.sem_inc(passed.sem, 1)
                for s in range(2):
                    pool.indirect_dma_start(
                        out=Hg[:, s, :], out_offset=None, in_=rows_h[:, :],
                        in_offset=bass.IndirectOffsetOnAxis(ap=idx_in[:, s:s + 1], axis=0),
                        bounds_check=NTOK, oob_is_err=False).then_inc(h_in.sem, 16)

            gather_x(0, 0)
            gather_x(0, 1)
            gather_h(0)
            last = pool.value_load(table[0:1, E:E + 1], min_val=E, max_val=E + MAXT)
            with pool.Fori(0, last) as g:
                for k in range(8):
                    pool.wait_ge(u_hi.sem, u_hi.at(g, k + 1))
                    pool.tensor_tensor(u_l[:, k, :], u32[:, k % U32, :], u_h[:, k, :], ALU.subtract
                                       ).then_inc(u_lo.sem, 1)
                    if k in (3, 5):
                        gather_x(g + 1, k // 4)
                gather_h(g + 1)
                pool.wait_ge(idx_out_in.sem, idx_out_in.at(g, 1))
                for s in range(2):
                    pool.wait_ge(yo_ready.sem, yo_ready.at(g, s + 1))
                    pool.sem_inc(passed.sem, 1)
                    pool.indirect_dma_start(
                        out=out[:, :], out_offset=bass.IndirectOffsetOnAxis(ap=idx_out[:, s:s + 1], axis=0),
                        in_=yo[:, s, :], in_offset=None, bounds_check=NTOK - 1, oob_is_err=False,
                    ).then_inc(out_done.sem, 16)
            pool.wait_ge(x_in.sem, x_in.at(last, 2))
            pool.wait_ge(h_in.sem, h_in.at(last, 2))

        @block.scalar
        def _(act):
            start_signals(act, "scalar")
            act.wait_ge(w_in.sem, w_in.at(0, 10))
            for raw, hi_ in ((wq_raw, wq_h), (wo_raw, wo_h), (rw_raw, rw_h)):
                act.activation(hi_[:, :, :], raw[:, :, :], ACT.Copy, scale=WS).then_inc(split_h.sem, 1)
            with act.Fori(0, PAIRS) as i:
                for t in range(3):
                    act.wait_ge(ln1.sem, ln1.at(i, 7 + t))
                    act.wait_ge(xn_turned.sem, xn_turned.before(i))
                    act.activation(xn_h[:, t, :], xn[:, t, :], ACT.Copy).then_inc(xn_hi.sem, 1)
                for t in range(3):
                    act.wait_ge(xn_turned.sem, xn_turned.at(i, t + 1))
                    act.activation(xT[:, t].rearrange("p a b c -> p (a b c)"), turn_banks[t].bitcast(F16)[:, 0:512], ACT.Copy
                                   ).then_inc(xT_ready.sem, 1)
                def turned_q(t):
                    act.wait_ge(pack_turned.sem, pack_turned.at(i, t + 1))
                    src = halves(SC[t % 2][:, 0, :])
                    if t < 2:
                        act.activation(QT[:, t, :, 0:MAIN], src, ACT.Copy).then_inc(qT_ready.sem, 1)
                    else:
                        act.activation(QT[:, :, :, MAIN:S], tail_cols(src), ACT.Copy).then_inc(qT_ready.sem, 1)

                for t in range(3):
                    act.wait_ge(qkv_ready.sem, qkv_ready.at(i, t + 1))
                    act.activation(V_h[:, t, :, 0:DH], proj[t][:, 1, 0:D].rearrange("p (h d) -> p h d", h=H), ACT.Copy,
                                   scale=1 / WS).then_inc(v_hi.sem, 1)
                    act.wait_ge(qk_ready.sem, qk_ready.at(i, t + 1))
                    if t >= 2:
                        act.wait_ge(pack_turned.sem, pack_turned.at(i, t - 1))
                    else:
                        act.wait_ge(pack_turned.sem, pack_turned.before(i))
                    for m in range(2):
                        src = qk[:, t % 2, D * m:D * m + D].rearrange("p (h a d) -> p h a d", h=H, a=1
                                                                      ).broadcast_to((128, H, 2, DH))
                        dst = pack[:, t % 2, m, :, :].rearrange("p h (s d) -> p h s d", d=DH)
                        dst = dst[:, :, 0:2, :] if m == 0 else dst[:, :, 0:3:2, :]
                        act.activation(dst, src, ACT.Copy).then_inc(pack_hi.sem, 1)
                    if t:
                        turned_q(t - 1)
                turned_q(2)
                act.wait_ge(negm_turned.sem, negm_turned.at(i, 1))
                mt = X[:, 0, :].bitcast(F16)[:, 0:384].rearrange("p (t n) -> p t n", t=3)
                act.activation(mT[:, :, 0:MAIN], mt[:, 0:2, :], ACT.Copy).then_inc(mT_ready.sem, 1)
                act.activation(mT[:, :, MAIN:S], mt[:, 2, :].rearrange("p (u n) -> p u n", u=2)[:, :, 0:TAIL], ACT.Copy
                               ).then_inc(mT_ready.sem, 1)
                n = 0
                for u in range(2):
                    for q in range(3):
                        _, nj = score_heads(q)
                        act.wait_ge(st_ready.sem, st_ready.at(i, n + 1))
                        if n >= 2:
                            act.wait_ge(p_lo.sem, p_lo.at(i, n - 1))
                        else:
                            act.wait_ge(p_lo.sem, p_lo.before(i))
                        act.activation(P32_par(n % 2, nj),
                                       SC[(n + 7) % 2][:, :, 0:nj * S].rearrange("p a (b q) -> p a b q", b=nj),
                                       ACT.Exp, scale=DH ** -0.5).then_inc(exp_done.sem, 1)
                        n += 1
                act.wait_ge(st_ready.sem, st_ready.at(i, n + 1))
                for u in range(2):
                    rows = slice(TAILS * u, TAILS * u + TAIL)
                    act.activation(P32t[rows], SC[(n + 7) % 2][rows, :, 0:8 * TAIL].rearrange("p a (b q) -> p a b q", b=8),
                                   ACT.Exp, scale=DH ** -0.5).then_inc(exp_done.sem, 1)
                for c in range(2):
                    if c == 0:
                        act.wait_ge(ew_in[0].sem, ew_in[0].at(0, 2))
                    piece = bass.ds((2 * i + c) * PIECE, PIECE)
                    act.activation(w_hi[0][:, piece], w_raw[0][:, piece], ACT.Copy, scale=WS).then_inc(ew_hi.sem, 1)
                for t in range(3):
                    act.wait_ge(o_ready.sem, o_ready.at(i, t + 1 if t < 2 else 4))
                    act.activation(O_h[:, t, :], O[:, t, :], ACT.Copy).then_inc(o_hi.sem, 1)
                for t in range(3):
                    act.wait_ge(o_turned.sem, o_turned.at(i, t + 1))
                    act.activation(oT[:, t].rearrange("p a b c -> p (a b c)"), turn_banks[t].bitcast(F16)[:, 0:512], ACT.Copy
                                   ).then_inc(oT_ready.sem, 1)
                for t in range(3):
                    act.wait_ge(ln2.sem, ln2.at(i, 7 + t))
                    act.wait_ge(x2_turned.sem, x2_turned.before(i))
                    act.wait_ge(rows_out.sem, rows_out.before(i))
                    act.activation(x2_hl[:, t, 0, :], xn2[:, t, :], ACT.Copy).then_inc(x2_hi.sem, 1)
                for t in range(3):
                    act.wait_ge(x2_turned.sem, x2_turned.at(i, t + 1))
                    act.activation(x2T[:, t].rearrange("p a b c -> p (a b c)"), turn_banks[t].bitcast(F16)[:, 0:512], ACT.Copy
                                   ).then_inc(x2T_ready.sem, 1)

            def turned_x(g):
                act.wait_ge(g_turned.sem, g_turned.at(g, 1))
                act.activation(gT[:, :, :, :].rearrange("p a b c -> p (a b c)"),
                               PV[:, 0, :].bitcast(F16)[:, 0:4 * TT], ACT.Copy).then_inc(gT_ready.sem, 1)

            def tile(g, u, split_piece):
                for k in range(8):
                    act.wait_ge(up_ready.sem, up_ready.at(g, k + 1))
                    if k >= 2:
                        act.wait_ge(glu_done.sem, glu_done.at(g, k - 1))
                    else:
                        act.wait_ge(glu_done.sem, glu_done.before(g))
                    act.activation(sigm[:, k % 2, :], up_banks[k % 4][:, TT:2 * TT], ACT.Sigmoid,
                                   scale=1 / WS, bias=b1_gate[u][:, k:k + 1]).then_inc(sig_done.sem, 1)
                    if k % 2:
                        split_piece(k // 2)
                for n in range(4, PIECES):
                    split_piece(n)
                turned_x(g + 1)

            def expert(j, u, load, split):
                e = 2 * j + u
                lo = act.value_load(table[0:1, bass.ds(e, 1)], min_val=0, max_val=E + MAXT)
                hi = act.value_load(table[0:1, bass.ds(e + 1, 1)], min_val=1, max_val=E + MAXT)

                def split_piece(n):
                    if n == 0:
                        act.wait_ge(ew_in[1 - u].sem, ew_in[1 - u].at(j + u, 2))
                        act.wait_ge(y_ready.sem, y_ready.before(lo))
                    piece = slice(n * PIECE, (n + 1) * PIECE)
                    act.activation(w_hi[1 - u][:, piece], w_raw[1 - u][:, piece], ACT.Copy, scale=WS
                                   ).then_inc(ew_hi.sem, 1)

                if load:
                    act.wait_ge(ew_lo.sem, ew_lo.at(e, PIECES))
                    for dst, w in ((w1_raw[u], w1), (w2_raw[u], w2)):
                        act.dma_start(dst, w[bass.ds(e + 2, 1)].rearrange("a (k p) n -> p (a k) n", p=128)
                                      ).then_inc(ew_in[u].sem, 16)
                act.wait_ge(bias_ready.sem, bias_ready.at(e, 3))
                tile(lo, u, split_piece if split else lambda n: None)
                with act.If(lo + 1 < hi):
                    with act.Fori(lo + 1, hi) as g:
                        tile(g, u, lambda n: None)

            act.wait_ge(tabled.sem, tabled.at(0, 10))
            turned_x(0)
            with act.Fori(0, E // 2 - 1) as j:
                for u in range(2):
                    expert(j, u, True, True)
            for u in range(2):
                expert(E // 2 - 1, u, False, u == 0)

        @block.vector
        def _(dve):
            start_signals(dve, "vector")
            for dst, value in ((h0[:, :, :], 0.0), (pack[:, :, :, :, :], 0.0), (neg_m[:, :, :, :], 0.0),
                               (O[:, :, :], 0.0), (V_l[:, :, :, :], 0.0), (V_h[:, :, :, :], 1.0),
                               (pad_ids[:, :], NTOK), (zero_row[:, :], 0.0), (minus_half[:, :], -0.5)):
                dve.memset(dst, value).then_inc(filled.sem, 1)
            dve.wait_ge(const_in.sem, const_in.at(0, 1))
            dve.memset(ones[:, :], 1.0).then_inc(const_ready.sem, 1)
            for dst, name in ((ident, "ident"), (identb, "ident"), (mask_main, "mask_main"), (mask_tail, "mask_tail"),
                              (before, "before"), (base, "list_base"), (ids_f, "id0")):
                dve.tensor_copy(dst[:, :], const(name)).then_inc(const_ready.sem, 1)
            dve.tensor_copy(head_sel[:, :, :], const("head_rows").rearrange("p (h a) -> p h a", a=1
                                                                            ).broadcast_to((128, H, 128))
                            ).then_inc(const_ready.sem, 1)
            dve.tensor_copy(rstd[:, :], const("valid")).then_inc(const_ready.sem, 1)
            dve.wait_ge(w_in.sem, w_in.at(0, 10))
            for n, (raw, hi_, lo_) in enumerate(((wq_raw, wq_h, wq_l), (wo_raw, wo_h, wo_l), (rw_raw, rw_h, rw_l))):
                dve.wait_ge(split_h.sem, split_h.at(0, n + 1))
                dve.scalar_tensor_tensor(out=lo_[:, :, :], in0=raw[:, :, :], scalar=WS, in1=hi_[:, :, :],
                                         op0=ALU.mult, op1=ALU.subtract).then_inc(w_ready.sem, 1)

            def layer_norm(i, src, dst, st, mvt, rs, signal, rsqrt):
                for t in range(3):
                    dve.bn_stats(st[:, t, :], src[:, t, :]).then_inc(signal.sem, 1)
                for t in range(3):
                    dve.wait_ge(signal.sem, signal.at(i, t + 1))
                    dve.sem_inc(passed.sem, 1)
                    dve.bn_aggr(mvt[:, t, :], st[:, t, :]).then_inc(signal.sem, 1)
                dve.wait_ge(rsqrt.sem, rsqrt.at(i, 2))
                for t in range(3):
                    dve.tensor_scalar(dst[:, t, :], src[:, t, :], mvt[:, t, 0:1], rs[:, t:t + 1],
                                      ALU.subtract, ALU.mult).then_inc(signal.sem, 1)

            with dve.Fori(0, PAIRS) as i:
                dve.wait_ge(emb_ready.sem, emb_ready.at(i, 1))
                dve.wait_ge(txt_in.sem, txt_in.at(i, 4))
                for u in range(2):
                    rows = slice(TAILS * u, TAILS * u + EMB)
                    dve.tensor_tensor(h0[0:EMB, u, :], X[rows, 0, 0:D], pos_sb[rows, :], ALU.add
                                      ).then_inc(emb_added.sem, 1)
                dve.wait_ge(emb_added.sem, emb_added.at(i, 2))
                dve.wait_ge(xn_lo.sem, xn_lo.before(i))
                layer_norm(i, h0, xn, stats, mv, rstd, ln1, rsqrt1)

                def low_pack(t):
                    for m in range(2):
                        dve.wait_ge(pack_hi.sem, pack_hi.at(i, 2 * t + m + 1))
                        src = qk[:, t % 2, D * m:D * m + D].rearrange("p (h d) -> p h d", h=H)
                        dst = pack[:, t % 2, m, :, :]
                        at = DH * (2 - m)
                        dve.tensor_tensor(dst[:, :, at:at + DH], src, dst[:, :, 0:DH], ALU.subtract
                                          ).then_inc(pack_lo.sem, 1)

                def turned_k(t):
                    dve.wait_ge(pack_turned.sem, pack_turned.at(i, t + 1))
                    src = halves(SC[t % 2][:, 1, :])
                    if t < 2:
                        dve.tensor_copy(KT[:, t, :, 0:MAIN], src).then_inc(kT_ready.sem, 1)
                    else:
                        dve.tensor_copy(KT[:, :, :, MAIN:S], tail_cols(src)).then_inc(kT_ready.sem, 1)

                for t in range(3):
                    dve.wait_ge(qkv_ready.sem, qkv_ready.at(i, t + 1))
                    ty = t // 2
                    pair_of = proj[t][:, 0, :].rearrange("p (n a d) -> p n a d", a=2, d=8)
                    a_of = rope_a[:, :].rearrange("p (n a d) -> p n a d", a=2, d=8)
                    b_of = rope_b[:, :].rearrange("p (n a d) -> p n a d", a=2, d=8)
                    cos = const("cos").rearrange("p (t n a d) -> p t n a d", t=2, n=1, a=2)[:, ty]
                    sin = const("sin").rearrange("p (t n a d) -> p t n a d", t=2, n=1, a=2)[:, ty]
                    if t:
                        dve.wait_ge(qk_ready.sem, qk_ready.at(i, t))
                    else:
                        dve.wait_ge(qk_ready.sem, qk_ready.before(i))
                    dve.tensor_tensor(a_of, pair_of, cos.broadcast_to((128, 2 * H, 2, 8)), ALU.mult
                                      ).then_inc(rope.sem, 1)
                    for half in range(2):
                        dve.tensor_tensor(b_of[:, :, half, :], pair_of[:, :, 1 - half, :],
                                          sin[:, :, half, :].broadcast_to((128, 2 * H, 8)), ALU.mult
                                          ).then_inc(rope.sem, 1)
                    dve.wait_ge(v_hi.sem, v_hi.at(i, t + 1))
                    dve.scalar_tensor_tensor(out=V_l[:, t, :, 0:DH],
                                             in0=proj[t][:, 1, 0:D].rearrange("p (h d) -> p h d", h=H),
                                             scalar=1 / WS, in1=V_h[:, t, :, 0:DH], op0=ALU.mult, op1=ALU.subtract
                                             ).then_inc(v_lo.sem, 1)
                    if t >= 2:
                        dve.wait_ge(pack_hi.sem, pack_hi.at(i, 2))
                    elif t == 0:
                        dve.wait_ge(pack_hi.sem, pack_hi.before(i))
                    dve.wait_ge(rope.sem, rope.at(i, 3 * t + 3))
                    dve.tensor_tensor(qk[:, t % 2, :], rope_a[:, :], rope_b[:, :], ALU.add).then_inc(qk_ready.sem, 1)
                    low_pack(t)
                    if t:
                        turned_k(t - 1)
                turned_k(2)

                for n in range(7):
                    dve.wait_ge(s_ready.sem, s_ready.at(i, n + 1))
                    if n < 4:
                        tile, h, nj, width = n // 2, 8 * (n % 2), 4, MAIN
                    else:
                        (h, nj), tile, width = score_heads(n - 4), 2, S
                    dve.tensor_reduce(smax[:, tile, h:h + 2 * nj].rearrange("p (j a) -> p a j", a=2),
                                      SC[n % 2][:, :, 0:nj * width].rearrange("p a (j k) -> p a j k", j=nj),
                                      AX, ALU.max).then_inc(max_done.sem, 1)
                dve.wait_ge(max_done.sem, max_done.at(i, 7))
                nm = neg_m[:, :, :, 0:H]
                dve.tensor_scalar(nm, smax[:, :, :].rearrange("p t (a h) -> p t a h", a=1
                                                              ).broadcast_to((128, 3, 2, H)), -1.0, None, ALU.mult
                                  ).then_inc(negm_hi.sem, 1)
                dve.wait_ge(negm_hi.sem, negm_hi.at(i, 1))
                for d in range(2):
                    ins = dve.scalar_tensor_tensor(out=neg_m[:, :, d, H:2 * H], in0=smax[:, :, :], scalar=-1.0,
                                                   in1=neg_m[:, :, d, 0:H], op0=ALU.mult, op1=ALU.subtract)
                    ins.then_inc(negm_ready.sem, 1)

                for n in range(8):
                    dve.wait_ge(p_masked.sem, p_masked.at(i, n + 1))
                    if n < 6:
                        u = n // 3
                        h, nj = score_heads(n % 3)
                        dve.tensor_copy(by_parity(P_h[:, u, h:h + 2 * nj, :]), P32_par(n % 2, nj)
                                        ).then_inc(p_hi.sem, 1)
                    else:
                        rows = slice(TAILS * (n - 6), TAILS * (n - 6) + TAIL)
                        dve.tensor_copy(by_parity(Pt_h[rows]), P32t[rows]).then_inc(p_hi.sem, 1)

                for c in range(2):
                    dve.wait_ge(ew_hi.sem, ew_hi.at(0, 2 * i + c + 1))
                    piece = bass.ds((2 * i + c) * PIECE, PIECE)
                    dve.scalar_tensor_tensor(out=w_lo[0][:, piece], in0=w_raw[0][:, piece], scalar=WS,
                                             in1=w_hi[0][:, piece], op0=ALU.mult, op1=ALU.subtract
                                             ).then_inc(ew_lo.sem, 1)

                dve.wait_ge(o_lo.sem, o_lo.before(i))
                for n in range(4):
                    dve.wait_ge(pv_ready.sem, pv_ready.at(i, min(n, 2) + 1))
                    t = min(n, 2)
                    rows = slice(0, 128) if n < 2 else slice(TAILS * (n - 2), TAILS * (n - 2) + TAIL)
                    src = (PV[:, t, :] if n < 2 else X[:, 0, :])[rows, 0:H * (DH + 1)].rearrange("p (h d) -> p h d", h=H)
                    dve.reciprocal(rinv[rows, t, :], src[:, :, DH]).then_inc(o_rinv.sem, 1)
                    dve.wait_ge(o_rinv.sem, o_rinv.at(i, n + 1))
                    n_rows = rows.stop - rows.start
                    dve.tensor_tensor(O[rows, t, :].rearrange("p (h d) -> p h d", h=H), src[:, :, 0:DH],
                                      rinv[rows, t, :].rearrange("p (h a) -> p h a", a=1
                                                                 ).broadcast_to((n_rows, H, DH)), ALU.mult
                                      ).then_inc(o_ready.sem, 1)

                dve.wait_ge(rows_out.sem, rows_out.before(i))
                for t in range(3):
                    dve.wait_ge(wo_ready.sem, wo_ready.at(i, t + 1))
                    dve.scalar_tensor_tensor(out=h1[:, t, :], in0=wo_banks[t][:, 0:D], scalar=1 / WS, in1=h0[:, t, :],
                                             op0=ALU.mult, op1=ALU.add).then_inc(h1_ready.sem, 1)
                dve.wait_ge(h1_ready.sem, h1_ready.at(i, 3))
                dve.wait_ge(x2_lo.sem, x2_lo.before(i))
                layer_norm(i, h1, xn2, stats2, mv2, rstd2, ln2, rsqrt2)

                def by_tile(ap):
                    return ap.rearrange("p (t e) -> p t e", t=1).broadcast_to((128, 3, E))

                def by_expert(ap):
                    return ap.rearrange("p (t e) -> p t e", e=1).broadcast_to((128, 3, E))

                dve.wait_ge(logits_ready.sem, logits_ready.at(i, 1))
                dve.scalar_tensor_tensor(out=logit[:, :, :], in0=PV[:, 1, 0:3 * E].rearrange("p (t e) -> p t e", t=3),
                                         scalar=1 / WS, in1=by_tile(rb_sb[:, :]), op0=ALU.mult, op1=ALU.add
                                         ).then_inc(route.sem, 1)
                dve.wait_ge(route.sem, route.at(i, 1))
                dve.tensor_reduce(lmax[:, :], logit[:, :, :], AX, ALU.max).then_inc(route.sem, 1)
                dve.wait_ge(route.sem, route.at(i, 2))
                dve.tensor_tensor(tie[:, :, :], logit[:, :, :], by_expert(lmax[:, :]), ALU.is_equal).then_inc(route.sem, 1)
                dve.wait_ge(route.sem, route.at(i, 3))
                dve.tensor_tensor(pick[:, :, :], tie[:, :, :], by_tile(const("expert_m8")), ALU.mult).then_inc(route.sem, 1)
                dve.wait_ge(route.sem, route.at(i, 4))
                dve.tensor_reduce(first[:, :], pick[:, :, :], AX, ALU.min).then_inc(route.sem, 1)
                dve.wait_ge(route.sem, route.at(i, 5))
                dve.tensor_tensor(onehot[:, :, :], by_tile(const("expert_m8")), by_expert(first[:, :]), ALU.is_equal
                                  ).then_inc(route.sem, 1)
                dve.wait_ge(route.sem, route.at(i, 6))
                dve.tensor_tensor(onehot16[:, :, :], onehot[:, :, :], by_expert(const("valid")), ALU.mult
                                  ).then_inc(route.sem, 1)
                dve.wait_ge(ranks_ready.sem, ranks_ready.at(i, 1))
                dve.wait_ge(route.sem, route.at(i, 7))
                dve.tensor_tensor(place_e[:, :, :], X[:, 0, 0:3 * E].rearrange("p (t e) -> p t e", t=3),
                                  by_tile(base[:, :]), ALU.add).then_inc(route.sem, 1)
                dve.wait_ge(route.sem, route.at(i, 8))
                dve.tensor_tensor(place_e[:, :, :], place_e[:, :, :], onehot16[:, :, :], ALU.mult).then_inc(route.sem, 1)
                dve.wait_ge(route.sem, route.at(i, 9))
                dve.tensor_reduce(place_f[:, :], place_e[:, :, :], AX, ALU.add).then_inc(route.sem, 1)
                dve.wait_ge(route.sem, route.at(i, 10))
                dve.tensor_tensor(place[:, :], place_f[:, :], const("pad_place"), ALU.add).then_inc(route.sem, 1)
                dve.tensor_tensor(base[:, :], base[:, :], X[:, 0, 3 * E:4 * E], ALU.add).then_inc(route.sem, 1)
                dve.tensor_copy(ids[:, :], ids_f[:, :]).then_inc(route.sem, 1)
                dve.tensor_scalar(ids_f[:, :], ids_f[:, :], float(2 * S), None, ALU.add).then_inc(route.sem, 1)

            steps = [0]

            def step(ins):
                steps[0] += 1
                ins.then_inc(tabled.sem, 1)
                dve.wait_ge(tabled.sem, tabled.at(0, steps[0]))

            dve.wait_ge(route.sem, route.at(PAIRS - 1, 14))
            step(dve.tensor_tensor(count[:, :], base[:, :], const("list_base"), ALU.subtract))
            step(dve.tensor_tensor(above[:, :, :], count[:, :].rearrange("p (e a) -> p e a", a=1
                                                                         ).broadcast_to((128, E, MAXT - 1)),
                                   const("tile_edges").rearrange("p (a n) -> p a n", a=1
                                                                 ).broadcast_to((128, E, MAXT - 1)), ALU.is_gt))
            step(dve.tensor_reduce(tiles[:, :], above[:, :, :], AX, ALU.add))
            step(dve.tensor_scalar(tiles[:, :], tiles[:, :], 1.0, None, ALU.add))
            step(dve.tensor_tensor(cum_all[:, :, :], const("lower").rearrange("p (e n) -> p e n", e=E),
                                   tiles[:, :].rearrange("p (a n) -> p a n", a=1).broadcast_to((128, E, E)), ALU.mult))
            step(dve.tensor_reduce(cum[:, :], cum_all[:, :, :], AX, ALU.add))
            step(dve.tensor_copy(table_f[:, 0:E], cum[:, :]))
            step(dve.tensor_tensor(table_f[:, E:E + 1], cum[:, E - 1:E], tiles[:, E - 1:E], ALU.add))
            step(dve.scalar_tensor_tensor(out=table_f[:, E + 1:2 * E + 1], in0=cum[:, :], scalar=-float(TT),
                                          in1=const("list_base"), op0=ALU.mult, op1=ALU.add))
            step(dve.tensor_copy(table[:, :], table_f[:, :]))

            def tile(g, u, split_piece):
                dve.wait_ge(h_in.sem, h_in.at(g, 2))
                dve.wait_ge(yo_ready.sem, yo_ready.before(g))
                dve.tensor_tensor(hb[:, :, :], Hg[:, :, :], b2_e[u][0:HT, :].rearrange("p (a d) -> p a d", a=1
                                                                               ).broadcast_to((HT, 2, D)),
                                  ALU.add).then_inc(hb_done.sem, 1)
                for k in range(8):
                    dve.wait_ge(sig_done.sem, sig_done.at(g, k + 1))
                    if k >= U32:
                        dve.wait_ge(u_lo.sem, u_lo.at(g, k - U32 + 1))
                    elif k == 0:
                        dve.wait_ge(u_lo.sem, u_lo.before(g))
                    dve.scalar_tensor_tensor(out=u32[:, k % U32, :], in0=up_banks[k % 4][:, 0:TT],
                                             scalar=b1_lin[u][:, k:k + 1], in1=sigm[:, k % 2, :],
                                             op0=ALU.add, op1=ALU.mult).then_inc(glu_done.sem, 1)
                    dve.wait_ge(glu_done.sem, glu_done.at(g, k + 1))
                    dve.tensor_copy(u_h[:, k, :], u32[:, k % U32, :]).then_inc(u_hi.sem, 1)
                    if k % 2:
                        split_piece(k // 2)
                for n in range(4, PIECES):
                    split_piece(n)
                dve.wait_ge(hb_done.sem, hb_done.at(g, 1))
                dve.wait_ge(out_done.sem, out_done.before(g))
                for s in range(2):
                    dve.wait_ge(y_ready.sem, y_ready.at(g, s + 1))
                    dve.scalar_tensor_tensor(out=yo[:, s, :], in0=y_banks[s][0:HT, 0:D], scalar=1 / (WS * WS),
                                             in1=hb[:, s, :], op0=ALU.mult, op1=ALU.add
                                             ).then_inc(yo_ready.sem, 1)

            def expert(j, u, split):
                e = 2 * j + u
                lo = dve.value_load(table[0:1, bass.ds(e, 1)], min_val=0, max_val=E + MAXT)
                hi = dve.value_load(table[0:1, bass.ds(e + 1, 1)], min_val=1, max_val=E + MAXT)

                def split_piece(n):
                    dve.wait_ge(ew_hi.sem, ew_hi.at(e + 1, n + 1))
                    piece = slice(n * PIECE, (n + 1) * PIECE)
                    dve.scalar_tensor_tensor(out=w_lo[1 - u][:, piece], in0=w_raw[1 - u][:, piece], scalar=WS,
                                             in1=w_hi[1 - u][:, piece], op0=ALU.mult, op1=ALU.subtract
                                             ).then_inc(ew_lo.sem, 1)

                b1_of = b1_all[:, bass.ds(e, 1), :].rearrange("p a c -> p (a c)")
                dve.tensor_scalar(b1_lin[u][:, :], b1_of[:, 0:8], WS, None, ALU.mult).then_inc(bias_ready.sem, 1)
                dve.tensor_copy(b1_gate[u][:, :], b1_of[:, 8:16]).then_inc(bias_ready.sem, 1)
                dve.tensor_copy(b2_e[u][:, :], b2_all[:, bass.ds(e, 1), :].rearrange("p a d -> p (a d)")
                                ).then_inc(bias_ready.sem, 1)
                dve.wait_ge(bias_ready.sem, bias_ready.at(e, 3))
                dve.sem_inc(passed.sem, 1)
                tile(lo, u, split_piece if split else lambda n: None)
                with dve.If(lo + 1 < hi):
                    with dve.Fori(lo + 1, hi) as g:
                        tile(g, u, lambda n: None)

            with dve.Fori(0, E // 2 - 1) as j:
                for u in range(2):
                    expert(j, u, True)
            for u in range(2):
                expert(E // 2 - 1, u, u == 0)

        @block.tensor
        def _(pe):
            start_signals(pe, "tensor")
            pe.wait_ge(const_ready.sem, const_ready.at(0, 10))
            pe.wait_ge(w_ready.sem, w_ready.at(0, 3))
            pe.wait_ge(filled.sem, filled.at(0, 9))

            def split_product(dst, pairs_h, pairs_l, done=None):
                terms = []
                for (ah, al), (bh, bl) in zip(pairs_h, pairs_l):
                    terms += [(ah, bh), (ah, bl), (al, bh)]
                for n, (a, b) in enumerate(terms):
                    ins = pe.matmul(dst, a, b, start=(n == 0), stop=(n == len(terms) - 1))
                return ins

            def turn(t, hl_of, src_ready, rnd, signal):
                dst = turn_banks[t].bitcast(F16)
                for hl in range(2):
                    pe.wait_ge(src_ready[hl].sem, src_ready[hl].at(rnd, t + 1))
                    for c in range(2):
                        n = 2 * hl + c
                        ins = pe.transpose(dst[:, 128 * n:128 * n + 128], hl_of(hl)[:, 128 * c:128 * c + 128], ident[:, :])
                ins.then_inc(signal.sem, 1)

            def tokens(buf, t):
                return [(buf[:, t, 0, c, :], buf[:, t, 1, c, :]) for c in range(2)]

            with pe.Fori(0, PAIRS) as i:
                pe.wait_ge(route.sem, route.before(i))
                pe.wait_ge(patches_in.sem, patches_in.at(i, 1))
                for c in range(KP):
                    pe.matmul(X[0:PR, 0, 0:D], patch_sb[:, c, :], w_emb_sb[:, c, :], start=(c == 0), stop=False)
                pe.matmul(X[0:PR, 0, 0:D], const("emb_rows", 2), cls_b_sb[:, :], start=False, stop=True
                          ).then_inc(emb_ready.sem, 1)
                for t in range(3):
                    if t == 0:
                        pe.wait_ge(emb_added.sem, emb_added.at(i, 2))
                    turn(t, lambda hl: (xn_h, xn_l)[hl][:, t, :], (xn_hi, xn_lo), i, xn_turned)
                for t in range(3):
                    pe.wait_ge(xT_ready.sem, xT_ready.at(i, 3 if t < 2 else 3))
                    if t == 2:
                        pe.wait_ge(v_lo.sem, v_lo.at(i, 1))
                        pe.wait_ge(rope.sem, rope.at(i, 3))
                    split_product(proj[t][:, 0, :], tokens(xT, t),
                                  [(wq_h[:, c, 0:2 * D], wq_l[:, c, 0:2 * D]) for c in range(2)])
                    split_product(proj[t][:, 1, 0:D], tokens(xT, t),
                                  [(wq_h[:, c, 2 * D:3 * D], wq_l[:, c, 2 * D:3 * D]) for c in range(2)]
                                  ).then_inc(qkv_ready.sem, 1)
                for t in range(3):
                    pe.wait_ge(pack_hi.sem, pack_hi.at(i, 2 * t + 2))
                    pe.wait_ge(pack_lo.sem, pack_lo.at(i, 2 * t + 2))
                    if t == 2:
                        pe.wait_ge(qT_ready.sem, qT_ready.at(i, 1))
                        pe.wait_ge(kT_ready.sem, kT_ready.at(i, 1))
                    for m in range(2):
                        src = pack[:, t % 2, m, :, :].rearrange("p h s -> p (h s)")
                        dst = halves(SC[t % 2][:, m, :])
                        for b in range(8):
                            ins = pe.transpose(dst[:, b, :], src[:, 128 * b:128 * b + 128], ident[:, :])
                    ins.then_inc(pack_turned.sem, 1)
                pe.wait_ge(qT_ready.sem, qT_ready.at(i, 3))
                pe.wait_ge(kT_ready.sem, kT_ready.at(i, 3))

                for n in range(7):
                    if n >= 2:
                        pe.wait_ge(max_done.sem, max_done.at(i, n - 1))
                    dst = SC[n % 2]
                    for par in range(2):
                        rows = slice(64 * par, 64 * par + 64)
                        if n < 4:
                            u, q = n // 2, n % 2
                            pe.matmul(dst[:, par, :], identb[:, :], mask_main[:, :].rearrange("p (a k) -> p a k", a=1
                                                                        ).broadcast_to((128, 4, MAIN)),
                                      start=True, stop=False, skip_group_check=True)
                            for j in range(4):
                                ins = pe.matmul(dst[:, par, MAIN * j:MAIN * j + MAIN], QT[rows, u, 4 * q + j, 0:MAIN],
                                                KT[rows, u, 4 * q + j, 0:MAIN], start=False, stop=True,
                                                skip_group_check=True)
                        else:
                            h, nj = score_heads(n - 4)
                            pe.matmul(dst[:, par, 0:nj * S], identb[:, :], mask_tail[:, :].rearrange("p (a k) -> p a k", a=1
                                                                        ).broadcast_to((128, nj, S)),
                                      start=True, stop=False, skip_group_check=True)
                            for u in range(2):
                                for j in range(nj):
                                    ins = pe.matmul(dst[TAILS * u:TAILS * u + TAIL, par, S * j:S * j + S],
                                                    QT[rows, u, h // 2 + j, MAIN:S], KT[rows, u, h // 2 + j, :],
                                                    start=False, stop=True, skip_group_check=True)
                    ins.then_inc(s_ready.sem, 1)
                pe.wait_ge(negm_ready.sem, negm_ready.at(i, 2))
                for t in range(3):
                    ins = pe.transpose(X[:, 0, :].bitcast(F16)[:, 128 * t:128 * t + 128],
                                       neg_m[:, t, :, :].rearrange("p a b -> p (a b)"), ident[:, :])
                ins.then_inc(negm_turned.sem, 1)
                pe.wait_ge(mT_ready.sem, mT_ready.at(i, 2))

                for n in range(7):
                    if n < 2:
                        pe.wait_ge(max_done.sem, max_done.at(i, 6 + n))
                    else:
                        pe.wait_ge(exp_done.sem, exp_done.at(i, n - 1))
                    pe.sem_inc(passed.sem, 1)
                    dst = SC[(n + 7) % 2]
                    if n < 6:
                        (h, nj), us, keys, queries, width = score_heads(n % 3), [n // 3], slice(0, MAIN), slice(0, S), S
                    else:
                        h, nj, us, keys, queries, width = 0, 8, [0, 1], slice(MAIN, S), slice(MAIN, S), TAIL
                    nk = keys.stop - keys.start
                    for u in us:
                        at = 0 if n < 6 else TAILS * u
                        for par in range(2):
                            rows = slice(64 * par, 64 * par + 64)
                            for j in range(nj):
                                to = dst[at:at + nk, par, width * j:width * j + width]
                                pe.matmul(to, head_sel[rows, h + 2 * j + par, 0:nk], mT[rows, u, queries],
                                          start=True, stop=False)
                                ins = pe.matmul(to, KT[rows, u, h // 2 + j, keys], QT[rows, u, h // 2 + j, queries],
                                                start=False, stop=True)
                    ins.then_inc(st_ready.sem, 1)

                for u in range(2):
                    pe.wait_ge(p_lo.sem, p_lo.at(i, 3 * u + 3))
                    for h in range(H):
                        ins = split_product(PV[:, u, (DH + 1) * h:(DH + 1) * (h + 1)],
                                            [(P_h[:, u, h, 0:MAIN], P_l[:, u, h, 0:MAIN])],
                                            [(V_h[:, u, h, :], V_l[:, u, h, :])])
                    ins.then_inc(pv_ready.sem, 1)
                for u in range(2):
                    pe.wait_ge(p_lo.sem, p_lo.at(i, 7 + u))
                    rows = slice(TAILS * u, TAILS * u + TAIL)
                    for h in range(H):
                        ins = split_product(X[rows, 0, (DH + 1) * h:(DH + 1) * (h + 1)],
                                            [(P_h[:, u, h, MAIN:S], P_l[:, u, h, MAIN:S]), (Pt_h[rows, h, :], Pt_l[rows, h, :])],
                                            [(V_h[:, u, h, :], V_l[:, u, h, :]), (V_h[rows, 2, h, :], V_l[rows, 2, h, :])])
                ins.then_inc(pv_ready.sem, 1)

                pe.wait_ge(o_ready.sem, o_ready.at(i, 4))
                for t in range(3):
                    turn(t, lambda hl: (O_h, O_l)[hl][:, t, :], (o_hi, o_lo), i, o_turned)
                for t in range(3):
                    pe.wait_ge(oT_ready.sem, oT_ready.at(i, t + 1))
                    split_product(wo_banks[t][:, 0:D], tokens(oT, t),
                                  [(wo_h[:, c, :], wo_l[:, c, :]) for c in range(2)]).then_inc(wo_ready.sem, 1)

                for t in range(3):
                    if t == 0:
                        pe.wait_ge(h1_ready.sem, h1_ready.at(i, 3))
                    turn(t, lambda hl: x2_hl[:, t, hl, :], (x2_hi, x2_lo), i, x2_turned)
                for t in range(3):
                    pe.wait_ge(x2T_ready.sem, x2T_ready.at(i, t + 1))
                    ins = split_product(PV[:, 1, E * t:E * t + E], tokens(x2T, t),
                                        [(rw_h[:, c, :], rw_l[:, c, :]) for c in range(2)])
                ins.then_inc(logits_ready.sem, 1)
                pe.wait_ge(route.sem, route.at(i, 7))
                for t in range(4):
                    terms = [(ones, s) for s in range(min(t, 3))] + ([(before, t)] if t < 3 else [])
                    for n, (a, s) in enumerate(terms):
                        ins = pe.matmul(X[:, 0, E * t:E * t + E], a[:, :], onehot16[:, s, :], start=(n == 0),
                                        stop=(n == len(terms) - 1))
                ins.then_inc(ranks_ready.sem, 1)

            def turn_x(g):
                pe.wait_ge(x_in.sem, x_in.at(g, 2))
                for n in range(8):
                    hl, c, s = n // 4, n // 2 % 2, n % 2
                    ins = pe.transpose(PV[:, 0, :].bitcast(F16)[:, HT * n:HT * n + HT],
                                       Xg[:, s, D * hl + 128 * c:D * hl + 128 * c + 128], ident[0:HT, 0:HT])
                ins.then_inc(g_turned.sem, 1)

            pe.wait_ge(tabled.sem, tabled.at(0, 10))
            turn_x(0)
            with pe.Fori(0, E // 2) as j:
                for u in range(2):
                    e = 2 * j + u
                    lo = pe.value_load(table[0:1, bass.ds(e, 1)], min_val=0, max_val=E + MAXT)
                    hi = pe.value_load(table[0:1, bass.ds(e + 1, 1)], min_val=1, max_val=E + MAXT)
                    pe.wait_ge(ew_lo.sem, ew_lo.at(e, PIECES))
                    pe.sem_inc(passed.sem, 1)
                    with pe.Fori(lo, hi) as g:
                        pe.wait_ge(gT_ready.sem, gT_ready.at(g, 1))
                        for k in range(8):
                            if k >= 4:
                                pe.wait_ge(glu_done.sem, glu_done.at(g, k - 3))
                            else:
                                pe.wait_ge(glu_done.sem, glu_done.at(g - 1, k + 5))
                            for part in range(2):
                                at = HID * part + 128 * k
                                ins = split_product(up_banks[k % 4][:, TT * part:TT * part + TT],
                                                    [(w1_h[u][:, c, at:at + 128], w1_l[u][:, c, at:at + 128]) for c in range(2)],
                                                    [(gT[:, 0, c, :], gT[:, 1, c, :]) for c in range(2)])
                            ins.then_inc(up_ready.sem, 1)
                        pe.wait_ge(yo_ready.sem, yo_ready.before(g))
                        for k in range(8):
                            pe.wait_ge(u_lo.sem, u_lo.at(g, k + 1))
                            for s in range(2):
                                uh, ul = (x[:, k, HT * s:HT * s + HT] for x in (u_h, u_l))
                                wh, wl = w2_h[u][:, k, :], w2_l[u][:, k, :]
                                for n, (a, b) in enumerate(((uh, wh), (uh, wl), (ul, wh))):
                                    ins = pe.matmul(y_banks[s][0:HT, 0:D], a, b, start=(k == 0 and n == 0),
                                                    stop=(k == 7 and n == 2))
                                if k == 7:
                                    ins.then_inc(y_ready.sem, 1)
                            if k == 3:
                                turn_x(g + 1)


def by_parity(ap):
    return ap.rearrange("p (j a) n -> p a j n", a=2)


def halves(bank):
    return bank.bitcast(F16).rearrange("p (b n) -> p b n", b=8)


def tail_cols(blocks):
    return blocks.rearrange("p b (u n) -> p u b n", u=2)[:, :, :, 0:TAIL]


def kernel(**inputs):
    import concourse.bacc as bacc
    from concourse.bass_utils import run_bass_kernel_spmd

    def get(name):
        return np.ascontiguousarray(inputs[name])

    x = get("x").reshape(PAIRS, 2, 3, 6, 16, 6, 16).transpose(0, 2, 4, 6, 1, 3, 5).reshape(PAIRS, KP, 128, 2, NPATCH)
    patches = np.zeros((PAIRS, 128, KP, PR), x.dtype)
    for u in range(2):
        patches[:, :, :, TAILS * u + 1:TAILS * u + EMB] = x[:, :, :, u].transpose(0, 2, 1, 3)
    qkv = get("L0_attn_W_qkv")
    turned = qkv[:2 * D].reshape(2 * H, DH // 2, 2, D).transpose(0, 2, 1, 3).reshape(2 * D, D)
    qkv = np.concatenate([turned, qkv[2 * D:]], 0)

    def chunks(w):
        return np.ascontiguousarray(w.reshape(-1, 128, w.shape[1]).transpose(1, 0, 2))

    arrays = {
        "patches": patches,
        "txt": get("txt"),
        "w_emb": chunks(get("L0_tok_w").T),
        "cls_b": np.stack([get("L0_tok_cls_token"), get("L0_tok_b")]),
        "pos": get("L0_tok_pos"),
        "w_qkv": chunks(qkv.T),
        "w_o": chunks(get("L0_attn_W_o").T),
        "router_w": chunks(get("L0_ffn_router_w")),
        "router_b": get("L0_ffn_router_b").reshape(1, E),
        "w1": get("L0_ffn_w1"),
        "b1": np.ascontiguousarray(get("L0_ffn_b1").reshape(E, 16, 128).transpose(2, 0, 1)),
        "w2": get("L0_ffn_w2"),
        "b2": get("L0_ffn_b2").reshape(1, E * D),
        "consts": constants(),
    }
    nc = bacc.Bacc("TRN2", target_bir_lowering=False, num_devices=1)
    args = [nc.dram_tensor(f"in_{n}", a.shape, mybir.dt.from_np(a.dtype), kind="ExternalInput").ap()
            for n, a in arrays.items()]
    out = nc.dram_tensor("out", (NTOK, D), F32, kind="ExternalOutput").ap()
    build(nc, *args, out)
    r = run_bass_kernel_spmd(nc, [{f"in_{n}": a for n, a in arrays.items()}], core_ids=[0])
    return r.results[0]["out"].reshape(B, S, D)
```

```python
from contextlib import ExitStack

import numpy as np

import concourse.bass as bass
from concourse import mybir

F32 = mybir.dt.float32
F16 = mybir.dt.float16
BF16 = mybir.dt.bfloat16
I32 = mybir.dt.int32
ALU = mybir.AluOpType
ACT = mybir.ActivationFunctionType
AX = mybir.AxisListType.X

B, D, H, DH = 8, 256, 16, 16
NPATCH, EMB, TXT = 36, 37, 128
S = EMB + TXT
MAIN, TAIL = 128, S - 128
PAIRS = B // 2
TAILS = 64
PR = TAILS + TAIL
KP = 6
E, HID = 8, 1024
NTOK = B * S
TT = 208
HT = TT // 2
MAXT = -(-NTOK // TT)
U32 = 3
LOADS = 12
PIECES = 8
CAP = MAXT * TT
WS = 16.0
EPS = 1e-5
NEG = -1e30

COLS = {}
_at = 0
for _name, _n in (("ident", 128), ("mask_main", MAIN), ("mask_tail", S), ("mask_t_main", S), ("mask_t_tail", TAIL), ("cos", 4 * 8), ("sin", 4 * 8),
                  ("before", 128), ("head_rows", H), ("expert_m8", E), ("valid", 3), ("pad_place", 3),
                  ("id0", 3), ("list_base", E), ("tile_edges", MAXT - 1), ("lower", E * E), ("emb_rows", PR)):
    COLS[_name] = (_at, _at + _n)
    _at += _n
NCONST = _at


def constants():
    t = np.zeros((128, NCONST), np.float32)

    def put(name, a):
        lo, hi = COLS[name]
        t[:, lo:hi] = np.asarray(a, np.float32).reshape(-1, hi - lo)

    p = np.arange(128)
    put("ident", np.eye(128))
    put("mask_main", np.where(p[None, :] <= p[:, None], 0.0, NEG))
    row = p % TAILS
    real = row < TAIL
    k = np.arange(S)
    put("mask_tail", np.where((k[None, :] <= MAIN + row[:, None]) | ~real[:, None], 0.0, NEG))
    put("mask_t_main", np.where(k[None, :] >= p[:, None], 0.0, NEG))
    put("mask_t_tail", np.where((np.arange(TAIL)[None, :] >= row[:, None]) | ~real[:, None], 0.0, NEG))
    freq = (np.float32(10000.0) ** (np.arange(0, DH, 2, dtype=np.float32) / np.float32(DH))).astype(np.float32)
    pos = np.stack([p, MAIN + row]).astype(np.float32)
    ang = (pos[:, :, None] / freq[None, None, :]).astype(np.float32).transpose(1, 0, 2)
    cos, sin = np.cos(ang), np.sin(ang)
    put("cos", np.stack([cos, cos], 2).reshape(128, -1) / WS)
    put("sin", np.stack([-sin, sin], 2).reshape(128, -1) / WS)
    put("before", p[:, None] < p[None, :])
    r = p % 64
    put("head_rows", (r[:, None] == np.arange(H)) | (r[:, None] == H + np.arange(H)))
    put("expert_m8", np.tile(np.arange(E) - E, (128, 1)))
    put("valid", np.stack([p >= 0, p >= 0, real], 1))
    put("pad_place", np.stack([0 * p, 0 * p, np.where(real, 0, 4 * E * CAP)], 1))
    put("id0", np.stack([p, S + p, MAIN + row + S * (p >= TAILS)], 1))
    put("list_base", np.tile(np.arange(E) * CAP, (128, 1)))
    put("tile_edges", np.tile(np.arange(1, MAXT) * TT, (128, 1)))
    put("lower", np.tile((np.arange(E)[None, :] < np.arange(E)[:, None]).reshape(1, -1), (128, 1)))
    cls = np.zeros((128, PR))
    cls[0, [0, TAILS]] = 1
    cls[1, 1:EMB] = 1
    cls[1, TAILS + 1:TAILS + EMB] = 1
    put("emb_rows", cls)
    return t


class Signal:

    def __init__(self, sem, per_round, unit=1, start=True):
        self.sem, self.per_round, self.unit, self.start = sem, per_round, unit, per_round if start else 0

    def at(self, rnd, k):
        return (rnd * self.per_round + self.start + k) * self.unit

    def before(self, rnd):
        return self.at(rnd, 0)



def build(nc, patches, txt, w_emb, cls_b, pos, w_qkv, w_o, router_w, router_b, w1, b1, w2, b2, consts, out):
    rows_x = nc.dram_tensor("rows_x", (NTOK + 1, 2 * D), F16).ap()
    rows_h = nc.dram_tensor("rows_h", (NTOK + 1, D), F32).ap()
    id_list = nc.dram_tensor("id_list", (E * CAP + (E + MAXT + 1) * TT, 1), I32).ap()

    ctx = ExitStack()
    with ctx:
        def sb(name, shape, dt=F32):
            return ctx.enter_context(nc.sbuf_tensor(name, shape, dt))

        def psum(name, shape):
            return ctx.enter_context(nc.psum_tensor(name, shape, F32))

        def sig(name, per_round, unit=1, start=True):
            return Signal(ctx.enter_context(nc.semaphore(name)), per_round, unit, start)

        X = psum("X", [128, 2, 512])
        SC = [psum("SC0", [128, 2, 512]), psum("SC1", [128, 2, 512])]
        PV = psum("PV", [128, 2, 512])
        turn_banks = [X[:, 0, :], X[:, 1, :], PV[:, 0, :]]
        wo_banks = [PV[:, 1, :], X[:, 0, :], X[:, 1, :]]
        xn_banks = [X[:, 1, 0:256], X[:, 1, 256:512], X[:, 0, 0:256]]
        proj = [SC[0], SC[1], SC[0]]
        up_banks = [SC[0][:, 0, :], SC[0][:, 1, :], SC[1][:, 0, :], SC[1][:, 1, :]]
        y_banks = [PV[:, 1, :], X[:, 0, :]]

        C = sb("C", [128, NCONST])

        def const(name, rows=128):
            lo, hi = COLS[name]
            return C[0:rows, lo:hi]

        ident = sb("ident", [128, 128], F16)
        identb = sb("identb", [128, 128], BF16)
        mask_main = sb("mask_main", [128, MAIN], BF16)
        mask_tail = sb("mask_tail", [128, S], BF16)
        mask_t_main = sb("mask_t_main", [128, S], BF16)
        mask_t_tail = sb("mask_t_tail", [128, TAIL], BF16)
        before = sb("before", [128, 128], F16)
        ones = sb("ones", [128, 128], F16)
        head_sel = sb("head_sel", [128, H, 128], F16)
        cls_b_sb = sb("cls_b_sb", [2, D])
        pos_sb = sb("pos_sb", [128, D])
        wq_h = sb("wq_h", [128, 2, 3 * D], F16)
        wq_l = sb("wq_l", [128, 2, 3 * D], F16)
        wo_h = sb("wo_h", [128, 2, D], F16)
        wo_l = sb("wo_l", [128, 2, D], F16)
        rw_raw = sb("rw_raw", [128, 2, E])
        rw_h = sb("rw_h", [128, 2, E], F16)
        rw_l = sb("rw_l", [128, 2, E], F16)
        rb_sb = sb("rb_sb", [128, E])

        patch_sb = sb("patch_sb", [128, KP, PR])
        h0 = sb("h0", [128, 3, D])
        h1 = sb("h1", [128, 3, D])
        stats = sb("stats", [128, 3, 6])
        mv = sb("mv", [128, 3, 2])
        rstd = sb("rstd", [128, 3])
        xn = sb("xn", [128, 3, D])
        xn_h = sb("xn_h", [128, 3, D], F16)
        xn_l = sb("xn_l", [128, 3, D], F16)
        xT = sb("xT", [128, 3, 2, 2, 128], F16)
        rope_a = sb("rope_a", [128, 2 * D])
        rope_b = sb("rope_b", [128, 2 * D])
        qk = sb("qk", [128, 2, 2 * D])
        pack = sb("pack", [128, 2, 2, H, 64], F16)
        QT = sb("QT", [128, 2, 8, S], F16)
        KT = sb("KT", [128, 2, 8, S], F16)
        V_h = sb("V_h", [128, 3, H, DH + 1], F16)
        V_l = sb("V_l", [128, 3, H, DH + 1], F16)
        smax = sb("smax", [128, 3, H])
        neg_m = sb("neg_m", [128, 3, 2, 64], F16)
        mT = sb("mT", [128, 2, S], F16)
        P32t = sb("P32t", [128, 2, 8, TAIL])
        Pt_h = sb("Pt_h", [128, H, TAIL], F16)
        Pt_l = sb("Pt_l", [128, H, TAIL], F16)
        rinv = sb("rinv", [128, 3, H])
        O = sb("O", [128, 3, D])
        O_h = sb("O_h", [128, 3, D], F16)
        O_l = sb("O_l", [128, 3, D], F16)
        oT = sb("oT", [128, 3, 2, 2, 128], F16)
        stats2 = sb("stats2", [128, 3, 6])
        mv2 = sb("mv2", [128, 3, 2])
        rstd2 = sb("rstd2", [128, 3])
        xn2 = sb("xn2", [128, 3, D])
        x2_hl = sb("x2_hl", [128, 3, 2, D], F16)
        x2T = sb("x2T", [128, 3, 2, 2, 128], F16)
        logit = sb("logit", [128, 3, E])
        lmax = sb("lmax", [128, 3])
        tie = sb("tie", [128, 3, E])
        pick = sb("pick", [128, 3, E])
        first = sb("first", [128, 3])
        onehot = sb("onehot", [128, 3, E])
        onehot16 = sb("onehot16", [128, 3, E], F16)
        place_e = sb("place_e", [128, 3, E])
        place_f = sb("place_f", [128, 3])
        place = sb("place", [128, 3], I32)
        ids_f = sb("ids_f", [128, 3])
        ids = sb("ids", [128, 3], I32)
        pad_ids = sb("pad_ids", [128, E * CAP // 128], I32)
        zero_row = sb("zero_row", [1, D])
        minus_half = sb("minus_half", [128, 3])
        base = sb("base", [128, E])
        count = sb("count", [128, E])
        above = sb("above", [128, E, MAXT - 1])
        tiles = sb("tiles", [128, E])
        cum_all = sb("cum_all", [128, E, E])
        cum = sb("cum", [128, E])
        table_f = sb("table_f", [128, 2 * E + 1])
        table = sb("table", [128, 2 * E + 1], I32)

        W1N, W2N = 2 * 2 * HID, 8 * D
        WN = W1N + W2N
        PIECE = WN // PIECES
        w_raw = [sb(f"w_raw{u}", [128, WN]) for u in range(2)]
        w1_raw = [w[:, 0:W1N].rearrange("p (k n) -> p k n", k=2) for w in w_raw]
        w2_raw = [w[:, W1N:WN].rearrange("p (k n) -> p k n", k=8) for w in w_raw]
        b1_all = sb("b1_all", [128, E, 16])
        w_hi, w_lo = ([sb(f"w_{name}{u}", [128, WN], F16) for u in range(2)] for name in ("hi", "lo"))
        w1_h, w1_l = ([w[:, 0:W1N].rearrange("p (k n) -> p k n", k=2) for w in ws] for ws in (w_hi, w_lo))
        w2_h, w2_l = ([w[:, W1N:WN].rearrange("p (k n) -> p k n", k=8) for w in ws] for ws in (w_hi, w_lo))
        b1_lin = [sb(f"b1_lin{u}", [128, 8]) for u in range(2)]
        b1_gate = [sb(f"b1_gate{u}", [128, 8]) for u in range(2)]
        b2_e = [sb(f"b2_e{u}", [HT, D]) for u in range(2)]
        idx_in = sb("idx_in", [HT, 2], I32)
        idx_out = sb("idx_out", [HT, 2], I32)
        Xg = sb("Xg", [HT, 2, 2 * D], F16)
        gT = sb("gT", [128, 2, 2, TT], F16)
        sigm = sb("sigm", [128, 2, TT])
        u32 = sb("u32", [128, U32, TT])

        spare = w_raw[1]
        wq_raw = spare[:, 0:6 * D].rearrange("p (k n) -> p k n", k=2)
        wo_raw = spare[:, 6 * D:8 * D].rearrange("p (k n) -> p k n", k=2)
        P32_flat = spare[:, 8 * D:8 * D + 12 * S].rearrange("p (x n) -> p x n", x=2)

        def P32(x, nj):
            return P32_flat[:, x, 0:2 * nj * S].rearrange("p (h q) -> p h q", q=S)

        def P32_par(x, nj):
            return P32(x, nj).rearrange("p (a j) q -> p a j q", a=2)

        w_emb_sb = w2_raw[1][:, 0:KP, :]
        P_h = w_hi[1][:, 0:2 * H * S].rearrange("p (u h q) -> p u h q", u=2, h=H)
        P_l = w_lo[1][:, 0:2 * H * S].rearrange("p (u h q) -> p u h q", u=2, h=H)
        pack_flat = pack[:, :, :, :, :].rearrange("p x m h s -> p (x m h s)")
        u_h = pack_flat[:, 0:8 * TT].rearrange("p (k n) -> p k n", k=8)
        u_l = pack_flat[:, 8 * TT:16 * TT].rearrange("p (k n) -> p k n", k=8)
        Hg, hb, yo = xn2[0:HT, 0:2, :], xn[0:HT, 0:2, :], O[0:HT, 0:2, :]

        passed = sig("passed", 1)
        const_in = sig("const_in", 1, 16)
        w_in = sig("w_in", 9, 16)
        const_ready = sig("const_ready", 12)
        split_h = sig("split_h", 3)
        w_ready = sig("w_ready", 3)
        filled = sig("filled", 9)
        fill_out = sig("fill_out", 1, 16)
        patches_in = sig("patches_in", 1, 16)
        txt_in = sig("txt_in", 4, 16)
        emb_ready = sig("emb_ready", 1)
        emb_added = sig("emb_added", 2)
        ln1 = sig("ln1", 9)
        rsqrt1 = sig("rsqrt1", 2)
        xn_hi = sig("xn_hi", 3)
        xn_lo = sig("xn_lo", 3)
        xn_turned = sig("xn_turned", 3)
        xT_ready = sig("xT_ready", 2)
        qkv_ready = sig("qkv_ready", 3)
        v_hi = sig("v_hi", 3)
        v_lo = sig("v_lo", 3)
        rope = sig("rope", 9)
        qk_ready = sig("qk_ready", 3)
        pack_hi = sig("pack_hi", 6)
        pack_lo = sig("pack_lo", 6)
        pack_turned = sig("pack_turned", 3)
        qT_ready = sig("qT_ready", 3)
        kT_ready = sig("kT_ready", 3)
        s_ready = sig("s_ready", 7)
        max_done = sig("max_done", 7)
        negm_hi = sig("negm_hi", 1)
        negm_ready = sig("negm_ready", 2)
        negm_turned = sig("negm_turned", 1)
        mT_ready = sig("mT_ready", 2)
        st_ready = sig("st_ready", 7)
        exp_done = sig("exp_done", 8)
        p_hi = sig("p_hi", 8)
        p_lo = sig("p_lo", 4)
        p_lo_odd = sig("p_lo_odd", 4)
        pv_ready = sig("pv_ready", 3)
        o_rinv = sig("o_rinv", 4)
        o_ready = sig("o_ready", 4)
        o_hi = sig("o_hi", 3)
        o_lo = sig("o_lo", 3)
        o_turned = sig("o_turned", 3)
        oT_ready = sig("oT_ready", 3)
        wo_ready = sig("wo_ready", 3)
        h1_ready = sig("h1_ready", 3)
        ln2 = sig("ln2", 9)
        rsqrt2 = sig("rsqrt2", 2)
        x2_hi = sig("x2_hi", 3)
        x2_lo = sig("x2_lo", 3)
        x2_turned = sig("x2_turned", 3)
        x2T_ready = sig("x2T_ready", 3)
        h_out = sig("h_out", 4, 16)
        rows_out = sig("rows_out", 4, 16)
        h_kept = sig("h_kept", 1)
        logits_ready = sig("logits_ready", 1)
        route = sig("route", 14)
        ranks_ready = sig("ranks_ready", 1)
        ids_out = sig("ids_out", 3, 16, start=False)
        tabled = sig("tabled", 10)
        ew_in = [sig(f"ew_in{u}", LOADS, 16) for u in range(2)]
        b2_in = [sig(f"b2_in{u}", 1, 16) for u in range(2)]
        ew_hi = sig("ew_hi", PIECES)
        ew_lo = sig("ew_lo", PIECES)
        bias_ready = sig("bias_ready", 2)
        idx_in_in = sig("idx_in_in", 1, 16)
        idx_out_in = sig("idx_out_in", 1, 16)
        x_in = sig("x_in", 2, 16, start=False)
        h_in = sig("h_in", 2, 16, start=False)
        g_turned = sig("g_turned", 1)
        gT_ready = sig("gT_ready", 1)
        up_ready = sig("up_ready", 8)
        sig_done = sig("sig_done", 8)
        glu_done = sig("glu_done", 8)
        u_hi = sig("u_hi", 8)
        u_lo = sig("u_lo", 8)
        y_ready = sig("y_ready", 2)
        hb_done = sig("hb_done", 1)
        yo_ready = sig("yo_ready", 2)
        out_done = sig("out_done", 2, 16)

        every = {
            "sync": [passed, const_in, w_in, fill_out, patches_in, txt_in, h_out, rows_out, *ew_in, *b2_in, idx_in_in,
                     idx_out_in],
            "gpsimd": [rsqrt1, rsqrt2, h_kept, pack_lo, xn_lo, p_lo, o_lo, x2_lo, u_lo],
            "scalar": [xn_hi, xT_ready, v_hi, pack_hi, qT_ready, mT_ready, exp_done, o_hi, oT_ready, x2_hi,
                       x2T_ready, ew_hi, gT_ready, sig_done, split_h],
            "vector": [const_ready, w_ready, emb_added, ln1, v_lo, rope, qk_ready, kT_ready, p_lo_odd, max_done,
                       negm_hi, negm_ready, p_hi, o_rinv, o_ready, ew_lo, h1_ready, ln2, route, tabled,
                       bias_ready, filled, glu_done, u_hi, hb_done, yo_ready],
            "tensor": [emb_ready, xn_turned, qkv_ready, pack_turned, s_ready, negm_turned, st_ready, pv_ready,
                       o_turned, wo_ready, x2_turned, logits_ready, ranks_ready, g_turned, up_ready, y_ready],
        }

        def start_signals(eng, name):
            for s in every[name]:
                eng.sem_inc(s.sem, s.per_round * s.unit)

        def score_heads(q):
            return 6 * q, min(3, (H - 6 * q) // 2)

        def token_rows(dram, img, lo, n):
            return dram[bass.ds(img * S + lo, n), :]

        def weights_part(e, u, n):
            if n < 8:
                k, cols = n // 4, slice(512 * (n % 4), 512 * (n % 4) + 512)
                return (w1_raw[u][:, k, cols],
                        w1[bass.ds(e, 1), 128 * k:128 * k + 128, cols].rearrange("a p n -> (a p) n"))
            ks = slice(2 * (n - 8), 2 * (n - 8) + 2)
            return (w2_raw[u][:, ks, :], w2[bass.ds(e, 1), 128 * ks.start:128 * ks.stop, :].rearrange(
                "a (k p) n -> p (a k) n", p=128))

        block = ctx.enter_context(nc.Block())

        @block.sync
        def _(sp):
            start_signals(sp, "sync")
            sp.dma_start(C[:, :], consts).then_inc(const_in.sem, 16)
            for dst, src in ((w_emb_sb[:, :, :], w_emb), (cls_b_sb[:, :], cls_b), (pos_sb[0:EMB, :], pos),
                             (pos_sb[TAILS:TAILS + EMB, :], pos), (wq_raw[:, :, :], w_qkv),
                             (wo_raw[:, :, :], w_o), (rw_raw[:, :, :], router_w),
                             (rb_sb[:, :], router_b.broadcast_to((128, E))), (b1_all[:, :, :], b1)):
                sp.dma_start(dst, src).then_inc(w_in.sem, 16)
            sp.wait_ge(filled.sem, filled.at(0, 9))
            sp.dma_start(id_list[0:E * CAP, :].rearrange("(p n) a -> p (n a)", p=128), pad_ids[:, :]).then_inc(fill_out.sem, 16)
            def load_weights(e, u):
                for n in range(LOADS):
                    dst, src = weights_part(e, u, n)
                    sp.dma_start(dst, src).then_inc(ew_in[u].sem, 16)

            def load_pair(i):
                sp.wait_ge(emb_ready.sem, emb_ready.before(i))
                sp.dma_start(patch_sb[:, :, :], patches[bass.ds(i, 1)].rearrange("a p k n -> p (a k) n")
                             ).then_inc(patches_in.sem, 16)
                sp.wait_ge(h_kept.sem, h_kept.before(i))
                for u in range(2):
                    img = txt[bass.ds(2 * i + u, 1)].rearrange("a t d -> (a t) d")
                    sp.dma_start(h0[EMB:128, u, :], img[0:MAIN - EMB, :]).then_inc(txt_in.sem, 16)
                    sp.dma_start(h0[TAILS * u:TAILS * u + TAIL, 2, :], img[MAIN - EMB:TXT, :]).then_inc(txt_in.sem, 16)

            def store_pair(i):
                sp.wait_ge(h1_ready.sem, h1_ready.at(i, 3))
                for u in range(2):
                    sp.dma_start(token_rows(rows_h, 2 * i + u, 0, MAIN), h1[:, u, :]).then_inc(h_out.sem, 16)
                    sp.dma_start(token_rows(rows_h, 2 * i + u, MAIN, TAIL), h1[TAILS * u:TAILS * u + TAIL, 2, :]
                                 ).then_inc(h_out.sem, 16)
                sp.wait_ge(x2_hi.sem, x2_hi.at(i, 3))
                sp.wait_ge(x2_lo.sem, x2_lo.at(i, 3))
                for u in range(2):
                    sp.dma_start(token_rows(rows_x, 2 * i + u, 0, MAIN),
                                 x2_hl[:, u, :, :].rearrange("p a b -> p (a b)")).then_inc(rows_out.sem, 16)
                    sp.dma_start(token_rows(rows_x, 2 * i + u, MAIN, TAIL),
                                 x2_hl[TAILS * u:TAILS * u + TAIL, 2, :, :].rearrange("p a b -> p (a b)")
                                 ).then_inc(rows_out.sem, 16)

            load_pair(0)
            sp.dma_start(b2_e[0][:, :], b2[0:1, :].broadcast_to((HT, D))).then_inc(b2_in[0].sem, 16)
            load_weights(0, 0)
            with sp.Fori(0, PAIRS - 1) as i:
                load_pair(i + 1)
                store_pair(i)
            sp.wait_ge(emb_ready.sem, emb_ready.at(PAIRS - 1, 1))
            sp.wait_ge(p_hi.sem, p_hi.at(PAIRS - 1, 8))
            sp.wait_ge(p_lo.sem, p_lo.at(PAIRS - 1, 4))
            sp.wait_ge(p_lo_odd.sem, p_lo_odd.at(PAIRS - 1, 4))
            load_weights(1, 1)
            store_pair(PAIRS - 1)

            def tile_ids(e):
                lo = sp.value_load(table[0:1, bass.ds(e, 1)], min_val=0, max_val=E + MAXT)
                hi = sp.value_load(table[0:1, bass.ds(e + 1, 1)], min_val=1, max_val=E + MAXT)
                off = sp.value_load(table[0:1, bass.ds(e + E + 1, 1)], min_val=0, max_val=E * CAP)
                with sp.Fori(lo, hi) as g:
                    places = id_list[bass.ds(g * TT + off, TT), :].rearrange("(s p) a -> p (s a)", s=2)
                    with nc.allow_non_contiguous_dma(reason="ids, one to a partition"):
                        sp.wait_ge(g_turned.sem, g_turned.before(g))
                        sp.wait_ge(hb_done.sem, hb_done.before(g))
                        sp.dma_start(idx_in[:, :], places).then_inc(idx_in_in.sem, 16)

            sp.wait_ge(tabled.sem, tabled.at(0, 10))
            sp.wait_ge(ids_out.sem, ids_out.at(PAIRS - 1, 3))
            with sp.Fori(0, E) as e:
                tile_ids(e)
            last = sp.value_load(table[0:1, E:E + 1], min_val=E, max_val=E + MAXT)
            sp.wait_ge(g_turned.sem, g_turned.before(last))
            sp.wait_ge(hb_done.sem, hb_done.before(last))
            with nc.allow_non_contiguous_dma(reason="ids, one to a partition"):
                sp.dma_start(idx_in[:, :], id_list[0:TT, :].rearrange("(s p) a -> p (s a)", s=2)
                             ).then_inc(idx_in_in.sem, 16)
            sp.wait_ge(out_done.sem, out_done.before(last))
            sp.sem_inc(passed.sem, 1)

        @block.gpsimd
        def _(pool):
            start_signals(pool, "gpsimd")
            def inverse_deviation(i, mvt, rs, moments, rsqrt):
                pool.wait_ge(moments.sem, moments.at(i, 6))
                pool.sem_inc(passed.sem, 1)
                pool.tensor_scalar(rs[:, :], mvt[:, :, 1], EPS, None, ALU.add).then_inc(rsqrt.sem, 1)
                pool.wait_ge(rsqrt.sem, rsqrt.at(i, 1))
                pool.tensor_tensor(rs[:, :], rs[:, :], minus_half[:, :], ALU.pow).then_inc(rsqrt.sem, 1)

            pool.wait_ge(filled.sem, filled.at(0, 9))
            pool.dma_start(rows_x[NTOK:NTOK + 1, :], zero_row[0:1, :].bitcast(F16)).then_inc(out_done.sem, 16)
            pool.dma_start(rows_h[NTOK:NTOK + 1, :], zero_row[0:1, :]).then_inc(out_done.sem, 16)
            pool.wait_ge(out_done.sem, out_done.before(0))
            pool.wait_ge(fill_out.sem, fill_out.at(0, 1))
            def low_xn(i):
                for t in range(3):
                    pool.wait_ge(xn_hi.sem, xn_hi.at(i, t + 1))
                    pool.tensor_tensor(xn_l[:, t, :], xn[:, t, :], xn_h[:, t, :], ALU.subtract).then_inc(xn_lo.sem, 1)

            def low_pack(i, t):
                for m in range(2):
                    pool.wait_ge(pack_hi.sem, pack_hi.at(i, 2 * t + m + 1))
                    src = qk[:, t % 2, D * m:D * m + D].rearrange("p (h d) -> p h d", h=H)
                    dst = pack[:, t % 2, m, :, :]
                    at = DH * (2 - m)
                    pool.tensor_tensor(dst[:, :, at:at + DH], src, dst[:, :, 0:DH], ALU.subtract
                                       ).then_inc(pack_lo.sem, 1)

            def keep_h(i):
                pool.wait_ge(emb_added.sem, emb_added.at(i, 2))
                pool.wait_ge(ln2.sem, ln2.before(i))
                pool.wait_ge(h_out.sem, h_out.before(i))
                pool.wait_ge(ln1.sem, ln1.at(i, 9))
                pool.sem_inc(passed.sem, 1)
                pool.tensor_copy(h1[:, :, :], h0[:, :, :]).then_inc(h_kept.sem, 1)

            def low_p(i, n):
                u, (h, nj) = n // 3, score_heads(n % 3)
                pool.wait_ge(p_hi.sem, p_hi.at(i, n + 1))
                pool.tensor_tensor(by_parity(P_l[:, u, h:h + 2 * nj, :]), P32_par(n % 2, nj),
                                   by_parity(P_h[:, u, h:h + 2 * nj, :]), ALU.subtract).then_inc(p_lo.sem, 1)

            def pair(i, following):
                if following:
                    inverse_deviation(i + 1, mv, rstd, ln1, rsqrt1)
                low_p(i, 0)
                low_p(i, 2)
                if following:
                    low_xn(i + 1)
                low_p(i, 4)
                rows = slice(0, TAIL)
                pool.wait_ge(p_hi.sem, p_hi.at(i, 7))
                pool.wait_ge(p_lo.sem, p_lo.at(i, 3))
                pool.tensor_tensor(by_parity(Pt_l[rows]), P32t[rows], by_parity(Pt_h[rows]), ALU.subtract
                                   ).then_inc(p_lo.sem, 1)
                pool.wait_ge(p_lo.sem, p_lo.at(i, 4))
                for t in range(3):
                    pool.wait_ge(o_hi.sem, o_hi.at(i, t + 1))
                    pool.tensor_tensor(O_l[:, t, :], O[:, t, :], O_h[:, t, :], ALU.subtract).then_inc(o_lo.sem, 1)
                if following:
                    low_pack(i + 1, 0)
                inverse_deviation(i, mv2, rstd2, ln2, rsqrt2)
                if following:
                    low_pack(i + 1, 1)
                for t in range(3):
                    pool.wait_ge(x2_hi.sem, x2_hi.at(i, t + 1))
                    pool.tensor_tensor(x2_hl[:, t, 1, :], xn2[:, t, :], x2_hl[:, t, 0, :], ALU.subtract
                                       ).then_inc(x2_lo.sem, 1)
                if following:
                    low_pack(i + 1, 2)
                    keep_h(i + 1)
                pool.wait_ge(route.sem, route.at(i, 14))
                pool.sem_inc(passed.sem, 1)
                for t in range(3):
                    pool.indirect_dma_start(
                        out=id_list[:, :], out_offset=bass.IndirectOffsetOnAxis(ap=place[:, t:t + 1], axis=0),
                        in_=ids[:, t:t + 1], in_offset=None, bounds_check=E * CAP - 1, oob_is_err=False,
                    ).then_inc(ids_out.sem, 16)
                pool.wait_ge(ids_out.sem, ids_out.at(i, 3))

            inverse_deviation(0, mv, rstd, ln1, rsqrt1)
            low_xn(0)
            keep_h(0)
            for t in range(3):
                low_pack(0, t)
            with pool.Fori(0, PAIRS - 1) as i:
                pair(i, True)
            pair(PAIRS - 1, False)

            pool.wait_ge(tabled.sem, tabled.at(0, 10))
            pool.wait_ge(h_out.sem, h_out.at(PAIRS - 1, 4))
            pool.wait_ge(rows_out.sem, rows_out.at(PAIRS - 1, 4))

            def gather_x(g, s):
                if s == 0:
                    pool.wait_ge(idx_in_in.sem, idx_in_in.at(g, 1))
                    pool.sem_inc(passed.sem, 1)
                    pool.wait_ge(g_turned.sem, g_turned.before(g))
                    pool.sem_inc(passed.sem, 1)
                pool.indirect_dma_start(
                    out=Xg[:, s, :], out_offset=None, in_=rows_x[:, :],
                    in_offset=bass.IndirectOffsetOnAxis(ap=idx_in[:, s:s + 1], axis=0),
                    bounds_check=NTOK, oob_is_err=False).then_inc(x_in.sem, 16)

            def gather_h(g):
                pool.wait_ge(hb_done.sem, hb_done.before(g))
                pool.sem_inc(passed.sem, 1)
                for s in range(2):
                    pool.indirect_dma_start(
                        out=Hg[:, s, :], out_offset=None, in_=rows_h[:, :],
                        in_offset=bass.IndirectOffsetOnAxis(ap=idx_in[:, s:s + 1], axis=0),
                        bounds_check=NTOK, oob_is_err=False).then_inc(h_in.sem, 16)

            gather_x(0, 0)
            gather_x(0, 1)
            gather_h(0)
            last = pool.value_load(table[0:1, E:E + 1], min_val=E, max_val=E + MAXT)
            with pool.Fori(0, last) as g:
                for k in range(8):
                    pool.wait_ge(u_hi.sem, u_hi.at(g, k + 1))
                    pool.tensor_tensor(u_l[:, k, :], u32[:, k % U32, :], u_h[:, k, :], ALU.subtract
                                       ).then_inc(u_lo.sem, 1)
                    if k in (2, 4):
                        gather_x(g + 1, k // 4)
                gather_h(g + 1)
                pool.wait_ge(idx_out_in.sem, idx_out_in.at(g, 1))
                for s in range(2):
                    pool.wait_ge(yo_ready.sem, yo_ready.at(g, s + 1))
                    pool.sem_inc(passed.sem, 1)
                    pool.indirect_dma_start(
                        out=out[:, :], out_offset=bass.IndirectOffsetOnAxis(ap=idx_out[:, s:s + 1], axis=0),
                        in_=yo[:, s, :], in_offset=None, bounds_check=NTOK - 1, oob_is_err=False,
                    ).then_inc(out_done.sem, 16)
            pool.wait_ge(x_in.sem, x_in.at(last, 2))
            pool.wait_ge(h_in.sem, h_in.at(last, 2))

        @block.scalar
        def _(act):
            start_signals(act, "scalar")
            act.wait_ge(w_in.sem, w_in.at(0, 9))
            for raw, hi_ in ((wq_raw, wq_h), (wo_raw, wo_h), (rw_raw, rw_h)):
                act.activation(hi_[:, :, :], raw[:, :, :], ACT.Copy, scale=WS).then_inc(split_h.sem, 1)
            act.wait_ge(const_ready.sem, const_ready.at(0, 12))

            def high_xn(i):
                for t in range(3):
                    act.wait_ge(ln1.sem, ln1.at(i, 7 + t))
                    act.wait_ge(xn_turned.sem, xn_turned.before(i))
                    act.activation(xn_h[:, t, :], xn[:, t, :], ACT.Copy).then_inc(xn_hi.sem, 1)

            def turned_xn(i):
                for tiles, bank, turned in ((slice(0, 2), X[:, 1, :], 2), (slice(2, 3), X[:, 0, 0:256], 3)):
                    act.wait_ge(xn_turned.sem, xn_turned.at(i, turned))
                    act.activation(xT[:, tiles].rearrange("p t a b c -> p (t a b c)"), bank.bitcast(F16), ACT.Copy
                                   ).then_inc(xT_ready.sem, 1)

            def high_v(i, t):
                act.wait_ge(qkv_ready.sem, qkv_ready.at(i, t + 1))
                act.activation(V_h[:, t, :, 0:DH], proj[t][:, 1, 0:D].rearrange("p (h d) -> p h d", h=H), ACT.Copy,
                               scale=1 / WS).then_inc(v_hi.sem, 1)

            def high_pack(i, t):
                act.wait_ge(qk_ready.sem, qk_ready.at(i, t + 1))
                if t >= 2:
                    act.wait_ge(pack_turned.sem, pack_turned.at(i, t - 1))
                else:
                    act.wait_ge(pack_turned.sem, pack_turned.before(i))
                for m in range(2):
                    src = qk[:, t % 2, D * m:D * m + D].rearrange("p (h a d) -> p h a d", h=H, a=1
                                                                  ).broadcast_to((128, H, 2, DH))
                    dst = pack[:, t % 2, m, :, :].rearrange("p h (s d) -> p h s d", d=DH)
                    dst = dst[:, :, 0:2, :] if m == 0 else dst[:, :, 0:3:2, :]
                    act.activation(dst, src, ACT.Copy).then_inc(pack_hi.sem, 1)

            def turned_q(i, t):
                act.wait_ge(pack_turned.sem, pack_turned.at(i, t + 1))
                src = halves(SC[1 - t % 2][:, 0, :])
                if t < 2:
                    act.activation(QT[:, t, :, 0:MAIN], src, ACT.Copy).then_inc(qT_ready.sem, 1)
                else:
                    act.activation(QT[:, :, :, MAIN:S], tail_cols(src), ACT.Copy).then_inc(qT_ready.sem, 1)

            def turned_tiles(i, turned, dst, ready):
                for t in range(3):
                    act.wait_ge(turned.sem, turned.at(i, t + 1))
                    act.activation(dst[:, t].rearrange("p a b c -> p (a b c)"), turn_banks[t].bitcast(F16)[:, 0:512], ACT.Copy
                                   ).then_inc(ready.sem, 1)

            def exponentials(i, items):
                for n in items:
                    act.wait_ge(st_ready.sem, st_ready.at(i, min(n, 6) + 1))
                    if n >= 6:
                        rows = slice(TAILS * (n - 6), TAILS * (n - 6) + TAIL)
                        act.activation(P32t[rows], SC[1][rows, :, 0:8 * TAIL].rearrange("p a (b q) -> p a b q", b=8),
                                       ACT.Exp, scale=DH ** -0.5).then_inc(exp_done.sem, 1)
                        continue
                    _, nj = score_heads(n % 3)
                    if n == 0:
                        act.wait_ge(p_lo.sem, p_lo.before(i))
                    elif n == 1:
                        act.wait_ge(p_lo_odd.sem, p_lo_odd.before(i))
                    elif n % 2 == 0:
                        act.wait_ge(p_lo.sem, p_lo.at(i, n // 2))
                    else:
                        act.wait_ge(p_lo_odd.sem, p_lo_odd.at(i, n // 2))
                    act.activation(P32_par(n % 2, nj),
                                   SC[(n + 7) % 2][:, :, 0:nj * S].rearrange("p a (b q) -> p a b q", b=nj),
                                   ACT.Exp, scale=DH ** -0.5).then_inc(exp_done.sem, 1)

            def pair(i, following):
                act.wait_ge(negm_turned.sem, negm_turned.at(i, 1))
                mt = X[:, 1, :].bitcast(F16)[:, 0:384].rearrange("p (t n) -> p t n", t=3)
                act.activation(mT[:, :, 0:MAIN], mt[:, 0:2, :], ACT.Copy).then_inc(mT_ready.sem, 1)
                act.activation(mT[:, :, MAIN:S], mt[:, 2, :].rearrange("p (u n) -> p u n", u=2)[:, :, 0:TAIL], ACT.Copy
                               ).then_inc(mT_ready.sem, 1)
                exponentials(i, range(0, 3))
                if following:
                    high_xn(i + 1)
                exponentials(i, range(3, 8))
                if following:
                    turned_xn(i + 1)
                for c in range(2):
                    if c == 0:
                        act.wait_ge(ew_in[0].sem, ew_in[0].at(0, LOADS))
                    piece = bass.ds((2 * i + c) * PIECE, PIECE)
                    act.activation(w_hi[0][:, piece], w_raw[0][:, piece], ACT.Copy, scale=WS).then_inc(ew_hi.sem, 1)
                for t in range(3):
                    act.wait_ge(o_ready.sem, o_ready.at(i, t + 1 if t < 2 else 4))
                    act.activation(O_h[:, t, :], O[:, t, :], ACT.Copy).then_inc(o_hi.sem, 1)
                if following:
                    high_v(i + 1, 0)
                turned_tiles(i, o_turned, oT, oT_ready)
                if following:
                    for t in range(2):
                        if t:
                            high_v(i + 1, t)
                        high_pack(i + 1, t)
                for t in range(3):
                    act.wait_ge(ln2.sem, ln2.at(i, 7 + t))
                    act.wait_ge(x2_turned.sem, x2_turned.before(i))
                    act.wait_ge(rows_out.sem, rows_out.before(i))
                    act.activation(x2_hl[:, t, 0, :], xn2[:, t, :], ACT.Copy).then_inc(x2_hi.sem, 1)
                if following:
                    high_v(i + 1, 2)
                turned_tiles(i, x2_turned, x2T, x2T_ready)
                if following:
                    turned_q(i + 1, 0)
                    high_pack(i + 1, 2)
                    turned_q(i + 1, 1)
                    turned_q(i + 1, 2)

            high_xn(0)
            turned_xn(0)
            for t in range(3):
                high_v(0, t)
                if t == 2:
                    turned_q(0, 0)
                high_pack(0, t)
            turned_q(0, 1)
            turned_q(0, 2)
            with act.Fori(0, PAIRS - 1) as i:
                pair(i, True)
            pair(PAIRS - 1, False)

            def turned_x(g):
                act.wait_ge(g_turned.sem, g_turned.at(g, 1))
                act.activation(gT[:, :, :, :].rearrange("p a b c -> p (a b c)"),
                               PV[:, 0, :].bitcast(F16)[:, 0:4 * TT], ACT.Copy).then_inc(gT_ready.sem, 1)

            def tile(g, off, u, load_part, split_piece):
                for k in range(8):
                    if k == 5:
                        act.wait_ge(out_done.sem, out_done.before(g))
                        with nc.allow_non_contiguous_dma(reason="ids, one to a partition"):
                            act.dma_start(idx_out[:, :], id_list[bass.ds(g * TT + off, TT), :].rearrange(
                                "(s p) a -> p (s a)", s=2)).then_inc(idx_out_in.sem, 16)
                    load_part(k)
                    act.wait_ge(up_ready.sem, up_ready.at(g, k + 1))
                    if k >= 2:
                        act.wait_ge(glu_done.sem, glu_done.at(g, k - 1))
                    else:
                        act.wait_ge(glu_done.sem, glu_done.before(g))
                    act.activation(sigm[:, k % 2, :], up_banks[k % 4][:, TT:2 * TT], ACT.Sigmoid,
                                   scale=1 / WS, bias=b1_gate[u][:, k:k + 1]).then_inc(sig_done.sem, 1)
                    if k % 2:
                        split_piece(k // 2)
                for n in range(4, PIECES):
                    load_part(4 + n)
                    split_piece(n)
                turned_x(g + 1)

            def expert(j, u, load, split):
                e = 2 * j + u
                lo = act.value_load(table[0:1, bass.ds(e, 1)], min_val=0, max_val=E + MAXT)
                hi = act.value_load(table[0:1, bass.ds(e + 1, 1)], min_val=1, max_val=E + MAXT)
                off = act.value_load(table[0:1, bass.ds(e + E + 1, 1)], min_val=0, max_val=E * CAP)

                def split_piece(n):
                    if n == 0:
                        act.wait_ge(ew_in[1 - u].sem, ew_in[1 - u].at(j + u, LOADS))
                        act.wait_ge(y_ready.sem, y_ready.before(lo))
                    piece = slice(n * PIECE, (n + 1) * PIECE)
                    act.activation(w_hi[1 - u][:, piece], w_raw[1 - u][:, piece], ACT.Copy, scale=WS
                                   ).then_inc(ew_hi.sem, 1)

                if split:
                    act.wait_ge(hb_done.sem, hb_done.before(lo))
                    act.dma_start(b2_e[1 - u][:, :], b2[bass.ds(e + 1, 1), :].broadcast_to((HT, D))
                                  ).then_inc(b2_in[1 - u].sem, 16)
                def load_part(n):
                    if n == 0:
                        act.wait_ge(ew_lo.sem, ew_lo.at(e, PIECES))
                    dst, src = weights_part(e + 2, u, n)
                    act.dma_start(dst, src).then_inc(ew_in[u].sem, 16)

                act.wait_ge(bias_ready.sem, bias_ready.at(e, 2))
                tile(lo, off, u, load_part if load else lambda n: None, split_piece if split else lambda n: None)
                with act.If(lo + 1 < hi):
                    with act.Fori(lo + 1, hi) as g:
                        tile(g, off, u, lambda n: None, lambda n: None)

            act.activation(sigm[0:1, 0, 0:1], zero_row[0:1, 0:1], ACT.Sigmoid)
            act.wait_ge(tabled.sem, tabled.at(0, 10))
            turned_x(0)
            with act.Fori(0, E // 2 - 1) as j:
                for u in range(2):
                    expert(j, u, True, True)
            for u in range(2):
                expert(E // 2 - 1, u, False, u == 0)

        @block.vector
        def _(dve):
            start_signals(dve, "vector")
            for dst, value in ((h0[:, :, :], 0.0), (pack[:, :, :, :, :], 0.0), (neg_m[:, :, :, :], 0.0),
                               (O[:, :, :], 0.0), (V_l[:, :, :, :], 0.0), (V_h[:, :, :, :], 1.0),
                               (pad_ids[:, :], NTOK), (zero_row[:, :], 0.0), (minus_half[:, :], -0.5)):
                dve.memset(dst, value).then_inc(filled.sem, 1)
            dve.wait_ge(const_in.sem, const_in.at(0, 1))
            dve.memset(ones[:, :], 1.0).then_inc(const_ready.sem, 1)
            for dst, name in ((ident, "ident"), (identb, "ident"), (mask_main, "mask_main"), (mask_tail, "mask_tail"),
                              (mask_t_main, "mask_t_main"), (mask_t_tail, "mask_t_tail"),
                              (before, "before"), (base, "list_base"), (ids_f, "id0")):
                dve.tensor_copy(dst[:, :], const(name)).then_inc(const_ready.sem, 1)
            dve.tensor_copy(head_sel[:, :, :], const("head_rows").rearrange("p (h a) -> p h a", a=1
                                                                            ).broadcast_to((128, H, 128))
                            ).then_inc(const_ready.sem, 1)
            dve.tensor_copy(rstd[:, :], const("valid")).then_inc(const_ready.sem, 1)
            dve.wait_ge(w_in.sem, w_in.at(0, 9))
            for n, (raw, hi_, lo_) in enumerate(((wq_raw, wq_h, wq_l), (wo_raw, wo_h, wo_l), (rw_raw, rw_h, rw_l))):
                dve.wait_ge(split_h.sem, split_h.at(0, n + 1))
                dve.scalar_tensor_tensor(out=lo_[:, :, :], in0=raw[:, :, :], scalar=WS, in1=hi_[:, :, :],
                                         op0=ALU.mult, op1=ALU.subtract).then_inc(w_ready.sem, 1)

            def moments(i, src, st, mvt, signal):
                for t in range(3):
                    dve.bn_stats(st[:, t, :], src[:, t, :]).then_inc(signal.sem, 1)
                for t in range(3):
                    dve.wait_ge(signal.sem, signal.at(i, t + 1))
                    dve.sem_inc(passed.sem, 1)
                    dve.bn_aggr(mvt[:, t, :], st[:, t, :]).then_inc(signal.sem, 1)

            def normed(i, src, dst, mvt, rs, signal, rsqrt):
                dve.wait_ge(rsqrt.sem, rsqrt.at(i, 2))
                for t in range(3):
                    dve.tensor_scalar(dst[:, t, :], src[:, t, :], mvt[:, t, 0:1], rs[:, t:t + 1],
                                      ALU.subtract, ALU.mult).then_inc(signal.sem, 1)

            def embedding(i):
                dve.wait_ge(emb_ready.sem, emb_ready.at(i, 1))
                dve.wait_ge(txt_in.sem, txt_in.at(i, 4))
                for u in range(2):
                    rows = slice(TAILS * u, TAILS * u + EMB)
                    dve.tensor_tensor(h0[0:EMB, u, :], X[rows, 0, 0:D], pos_sb[rows, :], ALU.add
                                      ).then_inc(emb_added.sem, 1)
                dve.wait_ge(emb_added.sem, emb_added.at(i, 2))
                moments(i, h0, stats, mv, ln1)

            def first_norm(i):
                dve.wait_ge(xn_lo.sem, xn_lo.before(i))
                normed(i, h0, xn, mv, rstd, ln1, rsqrt1)

            def rotary(i, t):
                dve.wait_ge(qkv_ready.sem, qkv_ready.at(i, t + 1))
                ty = t // 2
                pair_of = proj[t][:, 0, :].rearrange("p (n a d) -> p n a d", a=2, d=8)
                a_of = rope_a[:, :].rearrange("p (n a d) -> p n a d", a=2, d=8)
                b_of = rope_b[:, :].rearrange("p (n a d) -> p n a d", a=2, d=8)
                cos = const("cos").rearrange("p (t n a d) -> p t n a d", t=2, n=1, a=2)[:, ty]
                sin = const("sin").rearrange("p (t n a d) -> p t n a d", t=2, n=1, a=2)[:, ty]
                if t:
                    dve.wait_ge(qk_ready.sem, qk_ready.at(i, t))
                else:
                    dve.wait_ge(qk_ready.sem, qk_ready.before(i))
                dve.tensor_tensor(a_of, pair_of, cos.broadcast_to((128, 2 * H, 2, 8)), ALU.mult
                                  ).then_inc(rope.sem, 1)
                for half in range(2):
                    dve.tensor_tensor(b_of[:, :, half, :], pair_of[:, :, 1 - half, :],
                                      sin[:, :, half, :].broadcast_to((128, 2 * H, 8)), ALU.mult
                                      ).then_inc(rope.sem, 1)
                dve.wait_ge(v_hi.sem, v_hi.at(i, t + 1))
                dve.scalar_tensor_tensor(out=V_l[:, t, :, 0:DH],
                                         in0=proj[t][:, 1, 0:D].rearrange("p (h d) -> p h d", h=H),
                                         scalar=1 / WS, in1=V_h[:, t, :, 0:DH], op0=ALU.mult, op1=ALU.subtract
                                         ).then_inc(v_lo.sem, 1)
                if t >= 2:
                    dve.wait_ge(pack_hi.sem, pack_hi.at(i, 2))
                    dve.wait_ge(pack_lo.sem, pack_lo.at(i, 2))
                elif t == 0:
                    dve.wait_ge(pack_hi.sem, pack_hi.before(i))
                    dve.wait_ge(pack_lo.sem, pack_lo.before(i))
                dve.wait_ge(rope.sem, rope.at(i, 3 * t + 3))
                dve.tensor_tensor(qk[:, t % 2, :], rope_a[:, :], rope_b[:, :], ALU.add).then_inc(qk_ready.sem, 1)

            def turned_k(i, t):
                dve.wait_ge(pack_turned.sem, pack_turned.at(i, t + 1))
                src = halves(SC[1 - t % 2][:, 1, :])
                if t < 2:
                    dve.tensor_copy(KT[:, t, :, 0:MAIN], src).then_inc(kT_ready.sem, 1)
                else:
                    dve.tensor_copy(KT[:, :, :, MAIN:S], tail_cols(src)).then_inc(kT_ready.sem, 1)

            def split_p(i, items):
                for n in items:
                    dve.wait_ge(exp_done.sem, exp_done.at(i, n + 1))
                    if n < 6:
                        u, (h, nj) = n // 3, score_heads(n % 3)
                        hi_, lo_, raw = (by_parity(P_h[:, u, h:h + 2 * nj, :]), by_parity(P_l[:, u, h:h + 2 * nj, :]),
                                         P32_par(n % 2, nj))
                    else:
                        rows = slice(TAILS * (n - 6), TAILS * (n - 6) + TAIL)
                        hi_, lo_, raw = by_parity(Pt_h[rows]), by_parity(Pt_l[rows]), P32t[rows]
                    dve.tensor_copy(hi_, raw).then_inc(p_hi.sem, 1)
                    if n % 2:
                        dve.wait_ge(p_hi.sem, p_hi.at(i, n + 1))
                        dve.tensor_tensor(lo_, raw, hi_, ALU.subtract).then_inc(p_lo_odd.sem, 1)

            def by_tile(ap):
                return ap.rearrange("p (t e) -> p t e", t=1).broadcast_to((128, 3, E))

            def by_expert(ap):
                return ap.rearrange("p (t e) -> p t e", e=1).broadcast_to((128, 3, E))

            def pair(i, following):
                for n in range(7):
                    dve.wait_ge(s_ready.sem, s_ready.at(i, n + 1))
                    if n < 4:
                        tile, h, nj, width = n // 2, 8 * (n % 2), 4, MAIN
                    else:
                        (h, nj), tile, width = score_heads(n - 4), 2, S
                    dve.tensor_reduce(smax[:, tile, h:h + 2 * nj].rearrange("p (j a) -> p a j", a=2),
                                      SC[n % 2][:, :, 0:nj * width].rearrange("p a (j k) -> p a j k", j=nj),
                                      AX, ALU.max).then_inc(max_done.sem, 1)
                dve.wait_ge(max_done.sem, max_done.at(i, 7))
                nm = neg_m[:, :, :, 0:H]
                dve.tensor_scalar(nm, smax[:, :, :].rearrange("p t (a h) -> p t a h", a=1
                                                              ).broadcast_to((128, 3, 2, H)), -1.0, None, ALU.mult
                                  ).then_inc(negm_hi.sem, 1)
                dve.wait_ge(negm_hi.sem, negm_hi.at(i, 1))
                for d in range(2):
                    ins = dve.scalar_tensor_tensor(out=neg_m[:, :, d, H:2 * H], in0=smax[:, :, :], scalar=-1.0,
                                                   in1=neg_m[:, :, d, 0:H], op0=ALU.mult, op1=ALU.subtract)
                    ins.then_inc(negm_ready.sem, 1)


                if following:
                    embedding(i + 1)
                split_p(i, range(0, 2))
                if following:
                    first_norm(i + 1)
                split_p(i, range(2, 8))

                for c in range(2):
                    dve.wait_ge(ew_hi.sem, ew_hi.at(0, 2 * i + c + 1))
                    piece = bass.ds((2 * i + c) * PIECE, PIECE)
                    dve.scalar_tensor_tensor(out=w_lo[0][:, piece], in0=w_raw[0][:, piece], scalar=WS,
                                             in1=w_hi[0][:, piece], op0=ALU.mult, op1=ALU.subtract
                                             ).then_inc(ew_lo.sem, 1)

                dve.wait_ge(o_lo.sem, o_lo.before(i))
                for n in range(4):
                    dve.wait_ge(pv_ready.sem, pv_ready.at(i, min(n, 2) + 1))
                    t = min(n, 2)
                    rows = slice(0, 128) if n < 2 else slice(TAILS * (n - 2), TAILS * (n - 2) + TAIL)
                    src = (PV[:, t, :] if n < 2 else X[:, 0, :])[rows, 0:H * (DH + 1)].rearrange("p (h d) -> p h d", h=H)
                    dve.reciprocal(rinv[rows, t, :], src[:, :, DH]).then_inc(o_rinv.sem, 1)
                    dve.wait_ge(o_rinv.sem, o_rinv.at(i, n + 1))
                    n_rows = rows.stop - rows.start
                    dve.tensor_tensor(O[rows, t, :].rearrange("p (h d) -> p h d", h=H), src[:, :, 0:DH],
                                      rinv[rows, t, :].rearrange("p (h a) -> p h a", a=1
                                                                 ).broadcast_to((n_rows, H, DH)), ALU.mult
                                      ).then_inc(o_ready.sem, 1)

                if following:
                    rotary(i + 1, 0)
                dve.wait_ge(h_kept.sem, h_kept.at(i, 1))
                for t in range(3):
                    dve.wait_ge(wo_ready.sem, wo_ready.at(i, t + 1))
                    dve.scalar_tensor_tensor(out=h1[:, t, :], in0=wo_banks[t][:, 0:D], scalar=1 / WS, in1=h1[:, t, :],
                                             op0=ALU.mult, op1=ALU.add).then_inc(h1_ready.sem, 1)
                dve.wait_ge(h1_ready.sem, h1_ready.at(i, 3))
                moments(i, h1, stats2, mv2, ln2)
                if following:
                    rotary(i + 1, 1)
                dve.wait_ge(x2_lo.sem, x2_lo.before(i))
                normed(i, h1, xn2, mv2, rstd2, ln2, rsqrt2)
                if following:
                    rotary(i + 1, 2)
                    turned_k(i + 1, 0)

                dve.wait_ge(logits_ready.sem, logits_ready.at(i, 1))
                dve.scalar_tensor_tensor(out=logit[:, :, :], in0=PV[:, 1, 0:3 * E].rearrange("p (t e) -> p t e", t=3),
                                         scalar=1 / WS, in1=by_tile(rb_sb[:, :]), op0=ALU.mult, op1=ALU.add
                                         ).then_inc(route.sem, 1)
                dve.wait_ge(route.sem, route.at(i, 1))
                dve.tensor_reduce(lmax[:, :], logit[:, :, :], AX, ALU.max).then_inc(route.sem, 1)
                dve.wait_ge(route.sem, route.at(i, 2))
                dve.tensor_tensor(tie[:, :, :], logit[:, :, :], by_expert(lmax[:, :]), ALU.is_equal).then_inc(route.sem, 1)
                dve.wait_ge(route.sem, route.at(i, 3))
                dve.tensor_tensor(pick[:, :, :], tie[:, :, :], by_tile(const("expert_m8")), ALU.mult).then_inc(route.sem, 1)
                dve.wait_ge(route.sem, route.at(i, 4))
                dve.tensor_reduce(first[:, :], pick[:, :, :], AX, ALU.min).then_inc(route.sem, 1)
                dve.wait_ge(route.sem, route.at(i, 5))
                dve.tensor_tensor(onehot[:, :, :], by_tile(const("expert_m8")), by_expert(first[:, :]), ALU.is_equal
                                  ).then_inc(route.sem, 1)
                dve.wait_ge(route.sem, route.at(i, 6))
                dve.tensor_tensor(onehot16[:, :, :], onehot[:, :, :], by_expert(const("valid")), ALU.mult
                                  ).then_inc(route.sem, 1)
                if following:
                    turned_k(i + 1, 1)
                dve.wait_ge(ranks_ready.sem, ranks_ready.at(i, 1))
                dve.wait_ge(route.sem, route.at(i, 7))
                dve.tensor_tensor(place_e[:, :, :], X[:, 0, 0:3 * E].rearrange("p (t e) -> p t e", t=3),
                                  by_tile(base[:, :]), ALU.add).then_inc(route.sem, 1)
                dve.wait_ge(route.sem, route.at(i, 8))
                dve.tensor_tensor(place_e[:, :, :], place_e[:, :, :], onehot16[:, :, :], ALU.mult).then_inc(route.sem, 1)
                dve.wait_ge(route.sem, route.at(i, 9))
                dve.tensor_reduce(place_f[:, :], place_e[:, :, :], AX, ALU.add).then_inc(route.sem, 1)
                dve.wait_ge(route.sem, route.at(i, 10))
                dve.tensor_tensor(place[:, :], place_f[:, :], const("pad_place"), ALU.add).then_inc(route.sem, 1)
                dve.tensor_tensor(base[:, :], base[:, :], X[:, 0, 3 * E:4 * E], ALU.add).then_inc(route.sem, 1)
                dve.tensor_copy(ids[:, :], ids_f[:, :]).then_inc(route.sem, 1)
                dve.tensor_scalar(ids_f[:, :], ids_f[:, :], float(2 * S), None, ALU.add).then_inc(route.sem, 1)
                if following:
                    turned_k(i + 1, 2)

            embedding(0)
            first_norm(0)
            for t in range(3):
                rotary(0, t)
            for t in range(3):
                turned_k(0, t)
            with dve.Fori(0, PAIRS - 1) as i:
                pair(i, True)
            pair(PAIRS - 1, False)

            steps = [0]

            def step(ins):
                steps[0] += 1
                ins.then_inc(tabled.sem, 1)
                dve.wait_ge(tabled.sem, tabled.at(0, steps[0]))

            dve.wait_ge(route.sem, route.at(PAIRS - 1, 14))
            step(dve.tensor_tensor(count[:, :], base[:, :], const("list_base"), ALU.subtract))
            step(dve.tensor_tensor(above[:, :, :], count[:, :].rearrange("p (e a) -> p e a", a=1
                                                                         ).broadcast_to((128, E, MAXT - 1)),
                                   const("tile_edges").rearrange("p (a n) -> p a n", a=1
                                                                 ).broadcast_to((128, E, MAXT - 1)), ALU.is_gt))
            step(dve.tensor_reduce(tiles[:, :], above[:, :, :], AX, ALU.add))
            step(dve.tensor_scalar(tiles[:, :], tiles[:, :], 1.0, None, ALU.add))
            step(dve.tensor_tensor(cum_all[:, :, :], const("lower").rearrange("p (e n) -> p e n", e=E),
                                   tiles[:, :].rearrange("p (a n) -> p a n", a=1).broadcast_to((128, E, E)), ALU.mult))
            step(dve.tensor_reduce(cum[:, :], cum_all[:, :, :], AX, ALU.add))
            step(dve.tensor_copy(table_f[:, 0:E], cum[:, :]))
            step(dve.tensor_tensor(table_f[:, E:E + 1], cum[:, E - 1:E], tiles[:, E - 1:E], ALU.add))
            step(dve.scalar_tensor_tensor(out=table_f[:, E + 1:2 * E + 1], in0=cum[:, :], scalar=-float(TT),
                                          in1=const("list_base"), op0=ALU.mult, op1=ALU.add))
            step(dve.tensor_copy(table[:, :], table_f[:, :]))

            def tile(g, u, split_piece):
                dve.wait_ge(h_in.sem, h_in.at(g, 2))
                dve.wait_ge(yo_ready.sem, yo_ready.before(g))
                dve.tensor_tensor(hb[:, :, :], Hg[:, :, :], b2_e[u][:, :].rearrange("p (a d) -> p a d", a=1
                                                                               ).broadcast_to((HT, 2, D)),
                                  ALU.add).then_inc(hb_done.sem, 1)
                for k in range(8):
                    dve.wait_ge(sig_done.sem, sig_done.at(g, k + 1))
                    if k >= U32:
                        dve.wait_ge(u_lo.sem, u_lo.at(g, k - U32 + 1))
                    elif k == 0:
                        dve.wait_ge(u_lo.sem, u_lo.before(g))
                    dve.scalar_tensor_tensor(out=u32[:, k % U32, :], in0=up_banks[k % 4][:, 0:TT],
                                             scalar=b1_lin[u][:, k:k + 1], in1=sigm[:, k % 2, :],
                                             op0=ALU.add, op1=ALU.mult).then_inc(glu_done.sem, 1)
                    dve.wait_ge(glu_done.sem, glu_done.at(g, k + 1))
                    dve.tensor_copy(u_h[:, k, :], u32[:, k % U32, :]).then_inc(u_hi.sem, 1)
                    if k % 2:
                        split_piece(k // 2)
                for n in range(4, PIECES):
                    split_piece(n)
                dve.wait_ge(hb_done.sem, hb_done.at(g, 1))
                dve.wait_ge(out_done.sem, out_done.before(g))
                for s in range(2):
                    dve.wait_ge(y_ready.sem, y_ready.at(g, s + 1))
                    dve.scalar_tensor_tensor(out=yo[:, s, :], in0=y_banks[s][0:HT, 0:D], scalar=1 / (WS * WS),
                                             in1=hb[:, s, :], op0=ALU.mult, op1=ALU.add
                                             ).then_inc(yo_ready.sem, 1)

            def expert(j, u, split):
                e = 2 * j + u
                lo = dve.value_load(table[0:1, bass.ds(e, 1)], min_val=0, max_val=E + MAXT)
                hi = dve.value_load(table[0:1, bass.ds(e + 1, 1)], min_val=1, max_val=E + MAXT)

                def split_piece(n):
                    dve.wait_ge(ew_hi.sem, ew_hi.at(e + 1, n + 1))
                    piece = slice(n * PIECE, (n + 1) * PIECE)
                    dve.scalar_tensor_tensor(out=w_lo[1 - u][:, piece], in0=w_raw[1 - u][:, piece], scalar=WS,
                                             in1=w_hi[1 - u][:, piece], op0=ALU.mult, op1=ALU.subtract
                                             ).then_inc(ew_lo.sem, 1)

                b1_of = b1_all[:, bass.ds(e, 1), :].rearrange("p a c -> p (a c)")
                dve.tensor_scalar(b1_lin[u][:, :], b1_of[:, 0:8], WS, None, ALU.mult).then_inc(bias_ready.sem, 1)
                dve.tensor_copy(b1_gate[u][:, :], b1_of[:, 8:16]).then_inc(bias_ready.sem, 1)
                dve.wait_ge(bias_ready.sem, bias_ready.at(e, 2))
                dve.sem_inc(passed.sem, 1)
                dve.wait_ge(b2_in[u].sem, b2_in[u].at(j, 1))
                dve.sem_inc(passed.sem, 1)
                tile(lo, u, split_piece if split else lambda n: None)
                with dve.If(lo + 1 < hi):
                    with dve.Fori(lo + 1, hi) as g:
                        tile(g, u, lambda n: None)

            with dve.Fori(0, E // 2 - 1) as j:
                for u in range(2):
                    expert(j, u, True)
            for u in range(2):
                expert(E // 2 - 1, u, u == 0)

        @block.tensor
        def _(pe):
            start_signals(pe, "tensor")
            pe.wait_ge(const_ready.sem, const_ready.at(0, 12))
            pe.wait_ge(w_ready.sem, w_ready.at(0, 3))
            pe.wait_ge(filled.sem, filled.at(0, 9))

            def split_product(dst, pairs_h, pairs_l):
                terms = []
                for (ah, al), (bh, bl) in zip(pairs_h, pairs_l):
                    terms += [(ah, bh), (ah, bl), (al, bh)]
                for n, (a, b) in enumerate(terms):
                    ins = pe.matmul(dst, a, b, start=(n == 0), stop=(n == len(terms) - 1))
                return ins

            def turn(t, hl_of, src_ready, rnd, signal):
                dst = turn_banks[t].bitcast(F16)
                for hl in range(2):
                    pe.wait_ge(src_ready[hl].sem, src_ready[hl].at(rnd, t + 1))
                    for c in range(2):
                        n = 2 * hl + c
                        ins = pe.transpose(dst[:, 128 * n:128 * n + 128], hl_of(hl)[:, 128 * c:128 * c + 128], ident[:, :])
                ins.then_inc(signal.sem, 1)

            def tokens(buf, t):
                return [(buf[:, t, 0, c, :], buf[:, t, 1, c, :]) for c in range(2)]

            def embed(i, chunks):
                if 0 in chunks:
                    pe.wait_ge(patches_in.sem, patches_in.at(i, 1))
                for c in chunks:
                    pe.matmul(X[0:PR, 0, 0:D], patch_sb[:, c, :], w_emb_sb[:, c, :], start=(c == 0), stop=False,
                              skip_group_check=True)
                if KP - 1 in chunks:
                    pe.matmul(X[0:PR, 0, 0:D], const("emb_rows", 2), cls_b_sb[:, :], start=False, stop=True,
                              skip_group_check=True).then_inc(emb_ready.sem, 1)

            def turn_xn(i):
                pe.wait_ge(emb_added.sem, emb_added.at(i, 2))
                for t in range(3):
                    for hl, (src, ready) in enumerate(((xn_h, xn_hi), (xn_l, xn_lo))):
                        pe.wait_ge(ready.sem, ready.at(i, t + 1))
                        for c in range(2):
                            n = 2 * hl + c
                            ins = pe.transpose(xn_banks[t].bitcast(F16)[:, 128 * n:128 * n + 128],
                                               src[:, t, 128 * c:128 * c + 128], ident[:, :])
                    ins.then_inc(xn_turned.sem, 1)

            def project(i, t):
                pe.wait_ge(xT_ready.sem, xT_ready.at(i, 1 if t < 2 else 2))
                if t == 2:
                    pe.wait_ge(v_lo.sem, v_lo.at(i, 1))
                    pe.wait_ge(rope.sem, rope.at(i, 3))
                split_product(proj[t][:, 0, :], tokens(xT, t),
                              [(wq_h[:, c, 0:2 * D], wq_l[:, c, 0:2 * D]) for c in range(2)])
                split_product(proj[t][:, 1, 0:D], tokens(xT, t),
                              [(wq_h[:, c, 2 * D:3 * D], wq_l[:, c, 2 * D:3 * D]) for c in range(2)]
                              ).then_inc(qkv_ready.sem, 1)

            def turn_pack(i, t):
                pe.wait_ge(pack_hi.sem, pack_hi.at(i, 2 * t + 2))
                pe.wait_ge(pack_lo.sem, pack_lo.at(i, 2 * t + 2))
                if t < 2:
                    pe.wait_ge(v_lo.sem, v_lo.at(i, t + 2))
                    pe.wait_ge(rope.sem, rope.at(i, 3 * t + 6))
                else:
                    pe.wait_ge(qT_ready.sem, qT_ready.at(i, 1))
                    pe.wait_ge(kT_ready.sem, kT_ready.at(i, 1))
                for m in range(2):
                    src = pack[:, t % 2, m, :, :].rearrange("p h s -> p (h s)")
                    dst = halves(SC[1 - t % 2][:, m, :])
                    for b in range(8):
                        ins = pe.transpose(dst[:, b, :], src[:, 128 * b:128 * b + 128], ident[:, :])
                ins.then_inc(pack_turned.sem, 1)

            def pair(i, following):
                pe.wait_ge(qT_ready.sem, qT_ready.at(i, 3))
                pe.wait_ge(kT_ready.sem, kT_ready.at(i, 3))

                for n in range(7):
                    if n >= 2:
                        pe.wait_ge(max_done.sem, max_done.at(i, n - 1))
                    dst = SC[n % 2]
                    for par in range(2):
                        rows = slice(64 * par, 64 * par + 64)
                        if n < 4:
                            u, q = n // 2, n % 2
                            pe.matmul(dst[:, par, :], identb[:, :], mask_main[:, :].rearrange("p (a k) -> p a k", a=1
                                                                        ).broadcast_to((128, 4, MAIN)),
                                      start=True, stop=False, skip_group_check=True)
                            for j in range(4):
                                ins = pe.matmul(dst[:, par, MAIN * j:MAIN * j + MAIN], QT[rows, u, 4 * q + j, 0:MAIN],
                                                KT[rows, u, 4 * q + j, 0:MAIN], start=False, stop=True,
                                                skip_group_check=True)
                        else:
                            h, nj = score_heads(n - 4)
                            pe.matmul(dst[:, par, 0:nj * S], identb[:, :], mask_tail[:, :].rearrange("p (a k) -> p a k", a=1
                                                                        ).broadcast_to((128, nj, S)),
                                      start=True, stop=False, skip_group_check=True)
                            for u in range(2):
                                for j in range(nj):
                                    ins = pe.matmul(dst[TAILS * u:TAILS * u + TAIL, par, S * j:S * j + S],
                                                    QT[rows, u, h // 2 + j, MAIN:S], KT[rows, u, h // 2 + j, :],
                                                    start=False, stop=True, skip_group_check=True)
                    ins.then_inc(s_ready.sem, 1)
                if following:
                    pe.wait_ge(route.sem, route.before(i))
                    embed(i + 1, range(0, KP // 2))
                pe.wait_ge(negm_ready.sem, negm_ready.at(i, 2))
                for t in range(3):
                    ins = pe.transpose(X[:, 1, :].bitcast(F16)[:, 128 * t:128 * t + 128],
                                       neg_m[:, t, :, :].rearrange("p a b -> p (a b)"), ident[:, :])
                ins.then_inc(negm_turned.sem, 1)
                if following:
                    embed(i + 1, range(KP // 2, KP))
                pe.wait_ge(mT_ready.sem, mT_ready.at(i, 2))

                for n in range(7):
                    if n < 2:
                        pe.wait_ge(max_done.sem, max_done.at(i, 6 + n))
                    else:
                        pe.wait_ge(exp_done.sem, exp_done.at(i, n - 1))
                    pe.sem_inc(passed.sem, 1)
                    dst = SC[(n + 7) % 2]
                    if n < 6:
                        (h, nj), us, keys, queries, width = score_heads(n % 3), [n // 3], slice(0, MAIN), slice(0, S), S
                    else:
                        h, nj, us, keys, queries, width = 0, 8, [0, 1], slice(MAIN, S), slice(MAIN, S), TAIL
                    nk = keys.stop - keys.start
                    for par in range(2):
                        if n < 6:
                            pe.matmul(dst[:, par, 0:nj * S], identb[:, :], mask_t_main[:, :].rearrange(
                                "p (a k) -> p a k", a=1).broadcast_to((128, nj, S)),
                                start=True, stop=False, skip_group_check=True)
                        else:
                            pe.matmul(dst[0:PR, par, 0:nj * TAIL], identb[:, 0:PR], mask_t_tail[:, :].rearrange(
                                "p (a k) -> p a k", a=1).broadcast_to((128, nj, TAIL)),
                                start=True, stop=False, skip_group_check=True)
                    for u in us:
                        at = 0 if n < 6 else TAILS * u
                        for par in range(2):
                            rows = slice(64 * par, 64 * par + 64)
                            for j in range(nj):
                                to = dst[at:at + nk, par, width * j:width * j + width]
                                pe.matmul(to, head_sel[rows, h + 2 * j + par, 0:nk], mT[rows, u, queries],
                                          start=False, stop=False, skip_group_check=True)
                                ins = pe.matmul(to, KT[rows, u, h // 2 + j, keys], QT[rows, u, h // 2 + j, queries],
                                                start=False, stop=True, skip_group_check=True)
                    ins.then_inc(st_ready.sem, 1)

                if following:
                    turn_xn(i + 1)

                for u in range(2):
                    pe.wait_ge(p_lo.sem, p_lo.at(i, 2 + u))
                    pe.wait_ge(p_lo_odd.sem, p_lo_odd.at(i, 1 + 2 * u))
                    for h in range(H):
                        ins = split_product(PV[:, u, (DH + 1) * h:(DH + 1) * (h + 1)],
                                            [(P_h[:, u, h, 0:MAIN], P_l[:, u, h, 0:MAIN])],
                                            [(V_h[:, u, h, :], V_l[:, u, h, :])])
                    ins.then_inc(pv_ready.sem, 1)
                if following:
                    pe.wait_ge(xT_ready.sem, xT_ready.at(i + 1, 2))
                for u in range(2):
                    if u == 0:
                        pe.wait_ge(p_lo.sem, p_lo.at(i, 4))
                    else:
                        pe.wait_ge(p_lo_odd.sem, p_lo_odd.at(i, 4))
                    rows = slice(TAILS * u, TAILS * u + TAIL)
                    for h in range(H):
                        ins = split_product(X[rows, 0, (DH + 1) * h:(DH + 1) * (h + 1)],
                                            [(P_h[:, u, h, MAIN:S], P_l[:, u, h, MAIN:S]), (Pt_h[rows, h, :], Pt_l[rows, h, :])],
                                            [(V_h[:, u, h, :], V_l[:, u, h, :]), (V_h[rows, 2, h, :], V_l[rows, 2, h, :])])
                ins.then_inc(pv_ready.sem, 1)

                if following:
                    pe.wait_ge(exp_done.sem, exp_done.at(i, 6))
                    project(i + 1, 0)
                pe.wait_ge(o_ready.sem, o_ready.at(i, 4))
                for t in range(3):
                    turn(t, lambda hl: (O_h, O_l)[hl][:, t, :], (o_hi, o_lo), i, o_turned)
                if following:
                    pe.wait_ge(exp_done.sem, exp_done.at(i, 8))
                    project(i + 1, 1)
                for t in range(3):
                    pe.wait_ge(oT_ready.sem, oT_ready.at(i, t + 1))
                    split_product(wo_banks[t][:, 0:D], tokens(oT, t),
                                  [(wo_h[:, c, :], wo_l[:, c, :]) for c in range(2)]).then_inc(wo_ready.sem, 1)
                if following:
                    project(i + 1, 2)
                for t in range(3):
                    if t == 0:
                        pe.wait_ge(h1_ready.sem, h1_ready.at(i, 3))
                    turn(t, lambda hl: x2_hl[:, t, hl, :], (x2_hi, x2_lo), i, x2_turned)
                if following:
                    turn_pack(i + 1, 0)
                for t in range(3):
                    pe.wait_ge(x2T_ready.sem, x2T_ready.at(i, t + 1))
                    ins = split_product(PV[:, 1, E * t:E * t + E], tokens(x2T, t),
                                        [(rw_h[:, c, :], rw_l[:, c, :]) for c in range(2)])
                ins.then_inc(logits_ready.sem, 1)
                if following:
                    turn_pack(i + 1, 1)
                pe.wait_ge(route.sem, route.at(i, 7))
                for t in range(4):
                    terms = [(ones, s) for s in range(min(t, 3))] + ([(before, t)] if t < 3 else [])
                    for n, (a, s) in enumerate(terms):
                        ins = pe.matmul(X[:, 0, E * t:E * t + E], a[:, :], onehot16[:, s, :], start=(n == 0),
                                        stop=(n == len(terms) - 1))
                ins.then_inc(ranks_ready.sem, 1)
                if following:
                    turn_pack(i + 1, 2)

            embed(0, range(KP))
            turn_xn(0)
            for t in range(3):
                project(0, t)
            for t in range(3):
                turn_pack(0, t)
            with pe.Fori(0, PAIRS - 1) as i:
                pair(i, True)
            pair(PAIRS - 1, False)

            def turn_x(g):
                pe.wait_ge(x_in.sem, x_in.at(g, 2))
                for n in range(8):
                    hl, c, s = n // 4, n // 2 % 2, n % 2
                    ins = pe.transpose(PV[:, 0, :].bitcast(F16)[:, HT * n:HT * n + HT],
                                       Xg[:, s, D * hl + 128 * c:D * hl + 128 * c + 128], ident[0:HT, 0:HT])
                ins.then_inc(g_turned.sem, 1)

            pe.wait_ge(tabled.sem, tabled.at(0, 10))
            turn_x(0)
            with pe.Fori(0, E // 2) as j:
                for u in range(2):
                    e = 2 * j + u
                    lo = pe.value_load(table[0:1, bass.ds(e, 1)], min_val=0, max_val=E + MAXT)
                    hi = pe.value_load(table[0:1, bass.ds(e + 1, 1)], min_val=1, max_val=E + MAXT)
                    pe.wait_ge(ew_lo.sem, ew_lo.at(e, PIECES))
                    pe.sem_inc(passed.sem, 1)
                    with pe.Fori(lo, hi) as g:
                        pe.wait_ge(gT_ready.sem, gT_ready.at(g, 1))
                        for k in range(8):
                            if k >= 4:
                                pe.wait_ge(glu_done.sem, glu_done.at(g, k - 3))
                            else:
                                pe.wait_ge(glu_done.sem, glu_done.at(g - 1, k + 5))
                            for part in range(2):
                                at = HID * part + 128 * k
                                ins = split_product(up_banks[k % 4][:, TT * part:TT * part + TT],
                                                    [(w1_h[u][:, c, at:at + 128], w1_l[u][:, c, at:at + 128]) for c in range(2)],
                                                    [(gT[:, 0, c, :], gT[:, 1, c, :]) for c in range(2)])
                            ins.then_inc(up_ready.sem, 1)
                        pe.wait_ge(yo_ready.sem, yo_ready.before(g))
                        for k in range(8):
                            pe.wait_ge(u_lo.sem, u_lo.at(g, k + 1))
                            for s in range(2):
                                uh, ul = (x[:, k, HT * s:HT * s + HT] for x in (u_h, u_l))
                                wh, wl = w2_h[u][:, k, :], w2_l[u][:, k, :]
                                for n, (a, b) in enumerate(((uh, wh), (uh, wl), (ul, wh))):
                                    ins = pe.matmul(y_banks[s][0:HT, 0:D], a, b, start=(k == 0 and n == 0),
                                                    stop=(k == 7 and n == 2))
                                if k == 7:
                                    ins.then_inc(y_ready.sem, 1)
                            if k == 4:
                                turn_x(g + 1)


def by_parity(ap):
    return ap.rearrange("p (j a) n -> p a j n", a=2)


def halves(bank):
    return bank.bitcast(F16).rearrange("p (b n) -> p b n", b=8)


def tail_cols(blocks):
    return blocks.rearrange("p b (u n) -> p u b n", u=2)[:, :, :, 0:TAIL]


def kernel(**inputs):
    import concourse.bacc as bacc
    from concourse.bass_utils import run_bass_kernel_spmd

    def get(name):
        return np.ascontiguousarray(inputs[name])

    x = get("x").reshape(PAIRS, 2, 3, 6, 16, 6, 16).transpose(0, 2, 4, 6, 1, 3, 5).reshape(PAIRS, KP, 128, 2, NPATCH)
    patches = np.zeros((PAIRS, 128, KP, PR), x.dtype)
    for u in range(2):
        patches[:, :, :, TAILS * u + 1:TAILS * u + EMB] = x[:, :, :, u].transpose(0, 2, 1, 3)
    qkv = get("L0_attn_W_qkv")
    turned = qkv[:2 * D].reshape(2 * H, DH // 2, 2, D).transpose(0, 2, 1, 3).reshape(2 * D, D)
    qkv = np.concatenate([turned, qkv[2 * D:]], 0)

    def chunks(w):
        return np.ascontiguousarray(w.reshape(-1, 128, w.shape[1]).transpose(1, 0, 2))

    arrays = {
        "patches": patches,
        "txt": get("txt"),
        "w_emb": chunks(get("L0_tok_w").T),
        "cls_b": np.stack([get("L0_tok_cls_token"), get("L0_tok_b")]),
        "pos": get("L0_tok_pos"),
        "w_qkv": chunks(qkv.T),
        "w_o": chunks(get("L0_attn_W_o").T),
        "router_w": chunks(get("L0_ffn_router_w")),
        "router_b": get("L0_ffn_router_b").reshape(1, E),
        "w1": get("L0_ffn_w1"),
        "b1": np.ascontiguousarray(get("L0_ffn_b1").reshape(E, 16, 128).transpose(2, 0, 1)),
        "w2": get("L0_ffn_w2"),
        "b2": get("L0_ffn_b2"),
        "consts": constants(),
    }
    nc = bacc.Bacc("TRN2", target_bir_lowering=False, num_devices=1)
    args = [nc.dram_tensor(f"in_{n}", a.shape, mybir.dt.from_np(a.dtype), kind="ExternalInput").ap()
            for n, a in arrays.items()]
    out = nc.dram_tensor("out", (NTOK, D), F32, kind="ExternalOutput").ap()
    build(nc, *args, out)
    r = run_bass_kernel_spmd(nc, [{f"in_{n}": a for n, a in arrays.items()}], core_ids=[0])
    return r.results[0]["out"].reshape(B, S, D)
```

```python
from contextlib import ExitStack

import numpy as np

import concourse.bass as bass
from concourse import mybir

F32 = mybir.dt.float32
F16 = mybir.dt.float16
BF16 = mybir.dt.bfloat16
I32 = mybir.dt.int32
ALU = mybir.AluOpType
ACT = mybir.ActivationFunctionType
AX = mybir.AxisListType.X

B, D, H, DH = 8, 256, 16, 16
NPATCH, EMB, TXT = 36, 37, 128
S = EMB + TXT
MAIN, TAIL = 128, S - 128
PAIRS = B // 2
TAILS = 64
PR = TAILS + TAIL
KP = 6
E, HID = 8, 1024
NTOK = B * S
TT = 208
HT = TT // 2
MAXT = -(-NTOK // TT)
U32 = 3
LOADS = 12
PIECES = 8
CAP = MAXT * TT
WS = 16.0
EPS = 1e-5
NEG = -1e30

COLS = {}
_at = 0
for _name, _n in (("ident", 128), ("mask_main", MAIN), ("mask_tail", S), ("mask_t_main", S), ("mask_t_tail", TAIL), ("cos", 4 * 8), ("sin", 4 * 8),
                  ("before", 128), ("head_rows", H), ("expert_m8", E), ("valid", 3), ("pad_place", 3),
                  ("id0", 3), ("list_base", E), ("tile_edges", MAXT - 1), ("lower", E * E), ("emb_rows", PR)):
    COLS[_name] = (_at, _at + _n)
    _at += _n
NCONST = _at


def constants():
    t = np.zeros((128, NCONST), np.float32)

    def put(name, a):
        lo, hi = COLS[name]
        t[:, lo:hi] = np.asarray(a, np.float32).reshape(-1, hi - lo)

    p = np.arange(128)
    put("ident", np.eye(128))
    put("mask_main", np.where(p[None, :] <= p[:, None], 0.0, NEG))
    row = p % TAILS
    real = row < TAIL
    k = np.arange(S)
    put("mask_tail", np.where((k[None, :] <= MAIN + row[:, None]) | ~real[:, None], 0.0, NEG))
    put("mask_t_main", np.where(k[None, :] >= p[:, None], 0.0, NEG))
    put("mask_t_tail", np.where((np.arange(TAIL)[None, :] >= row[:, None]) | ~real[:, None], 0.0, NEG))
    freq = (np.float32(10000.0) ** (np.arange(0, DH, 2, dtype=np.float32) / np.float32(DH))).astype(np.float32)
    pos = np.stack([p, MAIN + row]).astype(np.float32)
    ang = (pos[:, :, None] / freq[None, None, :]).astype(np.float32).transpose(1, 0, 2)
    cos, sin = np.cos(ang), np.sin(ang)
    put("cos", np.stack([cos, cos], 2).reshape(128, -1) / WS)
    put("sin", np.stack([-sin, sin], 2).reshape(128, -1) / WS)
    put("before", p[:, None] < p[None, :])
    put("head_rows", (p[:, None] == np.arange(H)) | (p[:, None] == H + np.arange(H)))
    put("expert_m8", np.tile(np.arange(E) - E, (128, 1)))
    put("valid", np.stack([p >= 0, p >= 0, real], 1))
    put("pad_place", np.stack([0 * p, 0 * p, np.where(real, 0, 4 * E * CAP)], 1))
    put("id0", np.stack([p, S + p, MAIN + row + S * (p >= TAILS)], 1))
    put("list_base", np.tile(np.arange(E) * CAP, (128, 1)))
    put("tile_edges", np.tile(np.arange(1, MAXT) * TT, (128, 1)))
    put("lower", np.tile((np.arange(E)[None, :] < np.arange(E)[:, None]).reshape(1, -1), (128, 1)))
    cls = np.zeros((128, PR))
    cls[0, [0, TAILS]] = WS
    cls[1, 1:EMB] = WS
    cls[1, TAILS + 1:TAILS + EMB] = WS
    put("emb_rows", cls)
    return t


class Signal:

    def __init__(self, sem, per_round, unit=1, start=True):
        self.sem, self.per_round, self.unit, self.start = sem, per_round, unit, per_round if start else 0

    def at(self, rnd, k):
        return (rnd * self.per_round + self.start + k) * self.unit

    def before(self, rnd):
        return self.at(rnd, 0)



def build(nc, patches, txt, w_emb, cls_b, pos, w_qkv, w_o, router_w, router_b, w1, b1, w2, b2, consts, out):
    rows_x = nc.dram_tensor("rows_x", (NTOK + 1, 2 * D), F16).ap()
    rows_h = nc.dram_tensor("rows_h", (NTOK + 1, D), F32).ap()
    id_list = nc.dram_tensor("id_list", (E * CAP + (E + MAXT + 1) * TT, 1), I32).ap()

    ctx = ExitStack()
    with ctx:
        def sb(name, shape, dt=F32):
            return ctx.enter_context(nc.sbuf_tensor(name, shape, dt))

        def psum(name, shape):
            return ctx.enter_context(nc.psum_tensor(name, shape, F32))

        def sig(name, per_round, unit=1, start=True):
            return Signal(ctx.enter_context(nc.semaphore(name)), per_round, unit, start)

        X = psum("X", [128, 2, 512])
        SC = [psum("SC0", [128, 2, 512]), psum("SC1", [128, 2, 512])]
        PV = psum("PV", [128, 2, 512])
        turn_banks = [X[:, 0, :], X[:, 1, :], PV[:, 0, :]]
        wo_banks = [PV[:, 1, :], X[:, 0, :], X[:, 1, :]]
        xn_banks = [X[:, 1, 0:256], X[:, 1, 256:512], X[:, 0, 0:256]]
        proj = [SC[0], SC[1], SC[0]]
        up_banks = [SC[0][:, 0, :], SC[0][:, 1, :], SC[1][:, 0, :], SC[1][:, 1, :]]
        y_banks = [PV[:, 1, :], X[:, 0, :]]

        C = sb("C", [128, NCONST])

        def const(name, rows=128):
            lo, hi = COLS[name]
            return C[0:rows, lo:hi]

        ident = sb("ident", [128, 128], F16)
        identb = sb("identb", [128, 128], BF16)
        mask_main = sb("mask_main", [128, MAIN], BF16)
        mask_tail = sb("mask_tail", [128, S], BF16)
        mask_t_main = sb("mask_t_main", [128, S], BF16)
        mask_t_tail = sb("mask_t_tail", [128, TAIL], BF16)
        before = sb("before", [128, 128], F16)
        ones = sb("ones", [128, 128], F16)
        head_sel = sb("head_sel", [128, H, 128], F16)
        cls_b_sb = sb("cls_b_sb", [2, D])
        pos_sb = sb("pos_sb", [128, D])
        wq_h = sb("wq_h", [128, 2, 3 * D], F16)
        wq_l = sb("wq_l", [128, 2, 3 * D], F16)
        w_emb_hl = sb("w_emb_hl", [128, 2 * KP * D], F16)
        w_emb_h, w_emb_l = (w_emb_hl[:, KP * D * n:KP * D * (n + 1)].rearrange("p (k d) -> p k d", k=KP) for n in range(2))
        wo_h = sb("wo_h", [128, 2, D], F16)
        wo_l = sb("wo_l", [128, 2, D], F16)
        rw_raw = sb("rw_raw", [128, 2, E])
        rw_h = sb("rw_h", [128, 2, E], F16)
        rw_l = sb("rw_l", [128, 2, E], F16)
        rb_sb = sb("rb_sb", [128, E])

        patch_sb = sb("patch_sb", [128, KP, PR])
        patch_h = sb("patch_h", [128, KP, PR], F16)
        patch_l = sb("patch_l", [128, KP, PR], F16)
        h0 = sb("h0", [128, 3, D])
        h1 = sb("h1", [128, 3, D])
        stats = sb("stats", [128, 3, 6])
        mv = sb("mv", [128, 3, 2])
        rstd = sb("rstd", [128, 3])
        xn = sb("xn", [128, 3, D])
        xn_h = sb("xn_h", [128, 3, D], F16)
        xn_l = sb("xn_l", [128, 3, D], F16)
        xT = sb("xT", [128, 3, 2, 2, 128], F16)
        rope_a = sb("rope_a", [128, 2 * D])
        rope_b = sb("rope_b", [128, 2 * D])
        qk = sb("qk", [128, 2, 2 * D])
        pack = sb("pack", [128, 2, 2, H, 64], F16)
        QT_flat = sb("QT", [128, 2 * 8 * S + TAILS], F16)
        QT = QT_flat[:, 0:2 * 8 * S].rearrange("p (u b s) -> p u b s", u=2, b=8)
        KT = sb("KT", [128, 2, 8, S], F16)
        V_h = sb("V_h", [128, 3, H, DH + 1], F16)
        V_l = sb("V_l", [128, 3, H, DH + 1], F16)
        smax = sb("smax", [128, 3, H])
        neg_m = sb("neg_m", [128, 3, 2, 64], F16)
        mT = sb("mT", [128, 2, S], F16)
        P32t = sb("P32t", [128, 2, 8, TAIL])
        Pt_h_wide = sb("Pt_h", [128, H, TAILS], F16)
        Pt_l_wide = sb("Pt_l", [128, H, TAILS], F16)
        Pt_h, Pt_l = Pt_h_wide[:, :, 0:TAIL], Pt_l_wide[:, :, 0:TAIL]
        rinv = sb("rinv", [128, 4, H])
        O = sb("O", [128, 3, D])
        O_h = sb("O_h", [128, 3, D], F16)
        O_l = sb("O_l", [128, 3, D], F16)
        oT = sb("oT", [128, 3, 2, 2, 128], F16)
        stats2 = sb("stats2", [128, 3, 6])
        mv2 = sb("mv2", [128, 3, 2])
        rstd2 = sb("rstd2", [128, 3])
        xn2 = sb("xn2", [128, 3, D])
        x2_hl = sb("x2_hl", [128, 3, 2, D], F16)
        x2T = sb("x2T", [128, 3, 2, 2, 128], F16)
        logit = sb("logit", [128, 3, E])
        lmax = sb("lmax", [128, 3])
        tie = sb("tie", [128, 3, E])
        pick = sb("pick", [128, 3, E])
        first = sb("first", [128, 3])
        onehot = sb("onehot", [128, 3, E])
        onehot16 = sb("onehot16", [128, 3, E], F16)
        place_e = sb("place_e", [128, 3, E])
        place_f = sb("place_f", [128, 3])
        place = sb("place", [128, 3], I32)
        ids_f = sb("ids_f", [128, 3])
        ids = sb("ids", [128, 3], I32)
        pad_ids = sb("pad_ids", [128, E * CAP // 128], I32)
        zero_row = sb("zero_row", [1, D])
        minus_half = sb("minus_half", [128, 3])
        base = sb("base", [128, E])
        count = sb("count", [128, E])
        above = sb("above", [128, E, MAXT - 1])
        tiles = sb("tiles", [128, E])
        cum_all = sb("cum_all", [128, E, E])
        cum = sb("cum", [128, E])
        table_f = sb("table_f", [128, 2 * E + 1])
        table = sb("table", [128, 2 * E + 1], I32)

        W1N, W2N = 2 * 2 * HID, 8 * D
        WN = W1N + W2N
        PIECE = WN // PIECES
        w_raw = [sb(f"w_raw{u}", [128, WN]) for u in range(2)]
        w1_raw = [w[:, 0:W1N].rearrange("p (k n) -> p k n", k=2) for w in w_raw]
        w2_raw = [w[:, W1N:WN].rearrange("p (k n) -> p k n", k=8) for w in w_raw]
        b1_all = sb("b1_all", [128, E, 16])
        w_hi, w_lo = ([sb(f"w_{name}{u}", [128, WN], F16) for u in range(2)] for name in ("hi", "lo"))
        w1_h, w1_l = ([w[:, 0:W1N].rearrange("p (k n) -> p k n", k=2) for w in ws] for ws in (w_hi, w_lo))
        w2_h, w2_l = ([w[:, W1N:WN].rearrange("p (k n) -> p k n", k=8) for w in ws] for ws in (w_hi, w_lo))
        b1_lin = [sb(f"b1_lin{u}", [128, 8]) for u in range(2)]
        b1_gate = [sb(f"b1_gate{u}", [128, 8]) for u in range(2)]
        b2_e = [sb(f"b2_e{u}", [HT, D]) for u in range(2)]
        idx_in = sb("idx_in", [HT, 2], I32)
        idx_h = sb("idx_h", [HT, 2], I32)
        idx_out = sb("idx_out", [HT, 2], I32)
        u32 = sb("u32", [128, U32, TT])

        spare = w_raw[1]
        wq_raw = spare[:, 0:6 * D].rearrange("p (k n) -> p k n", k=2)
        wo_raw = spare[:, 6 * D:8 * D].rearrange("p (k n) -> p k n", k=2)
        P32_flat = spare[:, 8 * D:8 * D + 12 * S].rearrange("p (x n) -> p x n", x=2)

        def P32(x, nj):
            return P32_flat[:, x, 0:2 * nj * S].rearrange("p (h q) -> p h q", q=S)

        def P32_par(x, nj):
            return P32(x, nj).rearrange("p (a j) q -> p a j q", a=2)

        w_emb_sb = w2_raw[1][:, 0:KP, :]
        n_main = 2 * H * MAIN
        P_h, P_l = (w[1][:, 0:n_main].rearrange("p (u h q) -> p u h q", u=2, h=H) for w in (w_hi, w_lo))
        Pq_h, Pq_l = (w[1][:, n_main:n_main + 2 * H * TAILS].rearrange("p (u h q) -> p u h q", u=2, h=H)
                      for w in (w_hi, w_lo))
        n_x, n_t = 4 * D, 4 * TT
        Xg = w_emb_hl[0:HT, 0:n_x].rearrange("p (s d) -> p s d", s=2)
        gT = w_emb_hl[:, n_x:n_x + n_t].rearrange("p (a c n) -> p a c n", a=2, c=2)
        sigm = w_emb_hl[:, n_x + n_t:n_x + 2 * n_t].bitcast(F32).rearrange("p (x n) -> p x n", x=2)
        pack_flat = pack[:, :, :, :, :].rearrange("p x m h s -> p (x m h s)")
        u_h = pack_flat[:, 0:8 * TT].rearrange("p (k n) -> p k n", k=8)
        u_l = pack_flat[:, 8 * TT:16 * TT].rearrange("p (k n) -> p k n", k=8)
        Hg, hb, yo = xn2[0:HT, 0:2, :], xn[0:HT, 0:2, :], O[0:HT, 0:2, :]

        passed = sig("passed", 1)
        const_in = sig("const_in", 1, 16)
        emb_w_in = sig("emb_w_in", 2, 16)
        pos_in = sig("pos_in", 2, 16)
        w_in = sig("w_in", 5, 16)
        const_ready = sig("const_ready", 11)
        split_h = sig("split_h", 3)
        w_emb_hi = sig("w_emb_hi", 1)
        w_emb_ready = sig("w_emb_ready", 1)
        patch_hi = sig("patch_hi", 1)
        patch_lo = sig("patch_lo", 1)
        w_ready = sig("w_ready", 3)
        filled = sig("filled", 5)
        filled_too = sig("filled_too", 9)
        patches_in = sig("patches_in", 1, 16)
        txt_in = sig("txt_in", 4, 16)
        emb_ready = sig("emb_ready", 1)
        emb_added = sig("emb_added", 2)
        ln1 = sig("ln1", 9)
        rsqrt1 = sig("rsqrt1", 2)
        xn_hi = sig("xn_hi", 3)
        xn_lo = sig("xn_lo", 3)
        xn_turned = sig("xn_turned", 3)
        xT_ready = sig("xT_ready", 2)
        qkv_ready = sig("qkv_ready", 3)
        v_hi = sig("v_hi", 3)
        v_lo = sig("v_lo", 3)
        rope = sig("rope", 9)
        qk_ready = sig("qk_ready", 3)
        pack_hi = sig("pack_hi", 6)
        pack_lo = sig("pack_lo", 6)
        pack_turned = sig("pack_turned", 3)
        qT_ready = sig("qT_ready", 3)
        kT_ready = sig("kT_ready", 3)
        s_ready = sig("s_ready", 7)
        max_done = sig("max_done", 7)
        negm_hi = sig("negm_hi", 1)
        negm_ready = sig("negm_ready", 2)
        negm_turned = sig("negm_turned", 1)
        mT_ready = sig("mT_ready", 2)
        st_ready = sig("st_ready", 7)
        exp_done = sig("exp_done", 8)
        p_hi = sig("p_hi", 8)
        p_lo = sig("p_lo", 4)
        p_lo_odd = sig("p_lo_odd", 4)
        pv_ready = sig("pv_ready", 4)
        o_rinv = sig("o_rinv", 6)
        o_ready = sig("o_ready", 6)
        o_hi = sig("o_hi", 3)
        o_lo = sig("o_lo", 3)
        o_turned = sig("o_turned", 3)
        oT_ready = sig("oT_ready", 3)
        wo_ready = sig("wo_ready", 3)
        h1_ready = sig("h1_ready", 3)
        ln2 = sig("ln2", 9)
        rsqrt2 = sig("rsqrt2", 2)
        x2_hi = sig("x2_hi", 3)
        x2_lo = sig("x2_lo", 3)
        x2_turned = sig("x2_turned", 3)
        x2T_ready = sig("x2T_ready", 3)
        h_out = sig("h_out", 4, 16)
        rows_out = sig("rows_out", 4, 16)
        h_kept = sig("h_kept", 1)
        logits_ready = sig("logits_ready", 1)
        route = sig("route", 14)
        ranks_ready = sig("ranks_ready", 1)
        ids_out = sig("ids_out", 3, 16)
        tabled = sig("tabled", 10)
        ew_in = [sig(f"ew_in{u}", LOADS, 16) for u in range(2)]
        b2_in = [sig(f"b2_in{u}", 1, 16) for u in range(2)]
        ew_hi = sig("ew_hi", PIECES)
        ew_lo = sig("ew_lo", PIECES)
        bias_ready = sig("bias_ready", 2)
        idx_in_in = sig("idx_in_in", 1, 16)
        idx_h_in = sig("idx_h_in", 1, 16)
        idx_out_in = sig("idx_out_in", 1, 16)
        x_in = sig("x_in", 2, 16, start=False)
        h_in = sig("h_in", 2, 16, start=False)
        g_turned = sig("g_turned", 1)
        gT_ready = sig("gT_ready", 1)
        up_ready = sig("up_ready", 8)
        sig_done = sig("sig_done", 8)
        glu_done = sig("glu_done", 8)
        u_hi = sig("u_hi", 8)
        u_lo = sig("u_lo", 8)
        y_ready = sig("y_ready", 2)
        hb_done = sig("hb_done", 1)
        yo_ready = sig("yo_ready", 2)
        out_done = sig("out_done", 2, 16)

        every = {
            "sync": [passed, const_in, emb_w_in, pos_in, w_in, patches_in, txt_in, h_out, rows_out, *ew_in, *b2_in, idx_in_in,
                     idx_h_in, idx_out_in],
            "gpsimd": [patch_lo, filled_too, rsqrt1, rsqrt2, h_kept, pack_lo, xn_lo, p_lo, o_lo, x2_lo, u_lo],
            "scalar": [w_emb_hi, patch_hi, xn_hi, xT_ready, v_hi, pack_hi, qT_ready, mT_ready, exp_done, o_hi, oT_ready, x2_hi,
                       x2T_ready, ew_hi, gT_ready, sig_done, split_h],
            "vector": [w_emb_ready, const_ready, w_ready, emb_added, ln1, v_lo, rope, qk_ready, kT_ready, p_lo_odd, max_done,
                       negm_hi, negm_ready, p_hi, o_rinv, o_ready, ew_lo, h1_ready, ln2, route, tabled,
                       bias_ready, filled, glu_done, u_hi, hb_done, yo_ready],
            "tensor": [emb_ready, xn_turned, qkv_ready, pack_turned, s_ready, negm_turned, st_ready, pv_ready,
                       o_turned, wo_ready, x2_turned, logits_ready, ranks_ready, g_turned, up_ready, y_ready],
        }

        def start_signals(eng, name):
            for s in every[name]:
                eng.sem_inc(s.sem, s.per_round * s.unit)

        def score_heads(q):
            return 6 * q, min(3, (H - 6 * q) // 2)

        def token_rows(dram, img, lo, n):
            return dram[bass.ds(img * S + lo, n), :]

        def weights_part(e, u, n):
            if n < 8:
                k, cols = n // 4, slice(512 * (n % 4), 512 * (n % 4) + 512)
                return (w1_raw[u][:, k, cols],
                        w1[bass.ds(e, 1), 128 * k:128 * k + 128, cols].rearrange("a p n -> (a p) n"))
            ks = slice(2 * (n - 8), 2 * (n - 8) + 2)
            return (w2_raw[u][:, ks, :], w2[bass.ds(e, 1), 128 * ks.start:128 * ks.stop, :].rearrange(
                "a (k p) n -> p (a k) n", p=128))

        block = ctx.enter_context(nc.Block())

        @block.sync
        def _(sp):
            start_signals(sp, "sync")
            def load_weights(e, u):
                for n in range(LOADS):
                    dst, src = weights_part(e, u, n)
                    sp.dma_start(dst, src).then_inc(ew_in[u].sem, 16)

            def load_patches(i):
                sp.wait_ge(patch_lo.sem, patch_lo.before(i))
                sp.dma_start(patch_sb[:, :, :], patches[bass.ds(i, 1)].rearrange("a p k n -> p (a k) n")
                             ).then_inc(patches_in.sem, 16)

            def load_text(i):
                sp.wait_ge(h_kept.sem, h_kept.before(i))
                for u in range(2):
                    img = txt[bass.ds(2 * i + u, 1)].rearrange("a t d -> (a t) d")
                    sp.dma_start(h0[EMB:128, u, :], img[0:MAIN - EMB, :]).then_inc(txt_in.sem, 16)
                    sp.dma_start(h0[TAILS * u:TAILS * u + TAIL, 2, :], img[MAIN - EMB:TXT, :]).then_inc(txt_in.sem, 16)

            def store_pair(i):
                sp.wait_ge(h1_ready.sem, h1_ready.at(i, 3))
                for u in range(2):
                    sp.dma_start(token_rows(rows_h, 2 * i + u, 0, MAIN), h1[:, u, :]).then_inc(h_out.sem, 16)
                    sp.dma_start(token_rows(rows_h, 2 * i + u, MAIN, TAIL), h1[TAILS * u:TAILS * u + TAIL, 2, :]
                                 ).then_inc(h_out.sem, 16)
                sp.wait_ge(x2_hi.sem, x2_hi.at(i, 3))
                sp.wait_ge(x2_lo.sem, x2_lo.at(i, 3))
                for u in range(2):
                    sp.dma_start(token_rows(rows_x, 2 * i + u, 0, MAIN),
                                 x2_hl[:, u, :, :].rearrange("p a b -> p (a b)")).then_inc(rows_out.sem, 16)
                    sp.dma_start(token_rows(rows_x, 2 * i + u, MAIN, TAIL),
                                 x2_hl[TAILS * u:TAILS * u + TAIL, 2, :, :].rearrange("p a b -> p (a b)")
                                 ).then_inc(rows_out.sem, 16)

            load_patches(0)
            sp.dma_start(w_emb_sb[:, :, :], w_emb).then_inc(emb_w_in.sem, 16)
            sp.dma_start(cls_b_sb[:, :], cls_b).then_inc(emb_w_in.sem, 16)
            sp.dma_start(C[:, :], consts).then_inc(const_in.sem, 16)
            for u in range(2):
                sp.dma_start(pos_sb[TAILS * u:TAILS * u + EMB, :], pos).then_inc(pos_in.sem, 16)
            sp.wait_ge(filled.sem, filled.at(0, 1))
            load_text(0)
            for dst, src in ((wq_raw[:, :, :], w_qkv), (wo_raw[:, :, :], w_o), (rw_raw[:, :, :], router_w),
                             (rb_sb[:, :], router_b.broadcast_to((128, E))), (b1_all[:, :, :], b1)):
                sp.dma_start(dst, src).then_inc(w_in.sem, 16)
            load_patches(1)
            sp.dma_start(b2_e[0][:, :], b2[0:1, :].broadcast_to((HT, D))).then_inc(b2_in[0].sem, 16)
            load_weights(0, 0)
            with sp.Fori(0, PAIRS - 1) as i:
                load_text(i + 1)
                load_patches(i + 2)
                store_pair(i)
            sp.wait_ge(emb_ready.sem, emb_ready.at(PAIRS, 1))
            sp.wait_ge(p_hi.sem, p_hi.at(PAIRS - 1, 8))
            sp.wait_ge(p_lo.sem, p_lo.at(PAIRS - 1, 4))
            sp.wait_ge(p_lo_odd.sem, p_lo_odd.at(PAIRS - 1, 4))
            load_weights(1, 1)
            store_pair(PAIRS - 1)

            def tile_ids(e):
                lo = sp.value_load(table[0:1, bass.ds(e, 1)], min_val=0, max_val=E + MAXT)
                hi = sp.value_load(table[0:1, bass.ds(e + 1, 1)], min_val=1, max_val=E + MAXT)
                off = sp.value_load(table[0:1, bass.ds(e + E + 1, 1)], min_val=0, max_val=E * CAP)
                with sp.Fori(lo, hi) as g:
                    places = id_list[bass.ds(g * TT + off, TT), :].rearrange("(s p) a -> p (s a)", s=2)
                    with nc.allow_non_contiguous_dma(reason="ids, one to a partition"):
                        sp.wait_ge(g_turned.sem, g_turned.before(g))
                        sp.dma_start(idx_in[:, :], places).then_inc(idx_in_in.sem, 16)
                        sp.wait_ge(hb_done.sem, hb_done.before(g))
                        sp.dma_start(idx_h[:, :], places).then_inc(idx_h_in.sem, 16)

            sp.wait_ge(tabled.sem, tabled.at(0, 10))
            sp.wait_ge(ids_out.sem, ids_out.at(PAIRS - 1, 3))
            with sp.Fori(0, E) as e:
                tile_ids(e)
            last = sp.value_load(table[0:1, E:E + 1], min_val=E, max_val=E + MAXT)
            pad_places = id_list[0:TT, :].rearrange("(s p) a -> p (s a)", s=2)
            with nc.allow_non_contiguous_dma(reason="ids, one to a partition"):
                sp.wait_ge(g_turned.sem, g_turned.before(last))
                sp.dma_start(idx_in[:, :], pad_places).then_inc(idx_in_in.sem, 16)
                sp.wait_ge(hb_done.sem, hb_done.before(last))
                sp.dma_start(idx_h[:, :], pad_places).then_inc(idx_h_in.sem, 16)
            sp.wait_ge(out_done.sem, out_done.before(last))
            sp.sem_inc(passed.sem, 1)

        @block.gpsimd
        def _(pool):
            start_signals(pool, "gpsimd")
            def inverse_deviation(i, mvt, rs, moments, rsqrt):
                pool.wait_ge(moments.sem, moments.at(i, 6))
                pool.sem_inc(passed.sem, 1)
                pool.tensor_scalar(rs[:, :], mvt[:, :, 1], EPS, None, ALU.add).then_inc(rsqrt.sem, 1)
                pool.wait_ge(rsqrt.sem, rsqrt.at(i, 1))
                pool.tensor_tensor(rs[:, :], rs[:, :], minus_half[:, :], ALU.pow).then_inc(rsqrt.sem, 1)

            def low_patches(i):
                pool.wait_ge(patch_hi.sem, patch_hi.at(i, 1))
                pool.tensor_tensor(patch_l[:, :, :], patch_sb[:, :, :], patch_h[:, :, :], ALU.subtract
                                   ).then_inc(patch_lo.sem, 1)

            low_patches(0)
            for dst, value in ((pad_ids[:, :], NTOK), (zero_row[:, :], 0.0), (minus_half[:, :], -0.5),
                               (pack[:, :, :, :, :], 0.0), (QT_flat[:, 16 * S:], 0.0), (Pt_h_wide[:, :, :], 0.0),
                               (Pt_l_wide[:, :, :], 0.0), (Pq_h[:, :, :, :], 0.0), (Pq_l[:, :, :, :], 0.0)):
                pool.memset(dst, value).then_inc(filled_too.sem, 1)
            pool.wait_ge(filled_too.sem, filled_too.at(0, 9))
            def low_xn(i):
                for t in range(3):
                    pool.wait_ge(xn_hi.sem, xn_hi.at(i, t + 1))
                    pool.tensor_tensor(xn_l[:, t, :], xn[:, t, :], xn_h[:, t, :], ALU.subtract).then_inc(xn_lo.sem, 1)

            def low_pack(i, t):
                for m in range(2):
                    pool.wait_ge(pack_hi.sem, pack_hi.at(i, 2 * t + m + 1))
                    src = qk[:, t % 2, D * m:D * m + D].rearrange("p (h d) -> p h d", h=H)
                    dst = pack[:, t % 2, m, :, :]
                    at = DH * (2 - m)
                    pool.tensor_tensor(dst[:, :, at:at + DH], src, dst[:, :, 0:DH], ALU.subtract
                                       ).then_inc(pack_lo.sem, 1)

            def keep_h(i):
                pool.wait_ge(emb_added.sem, emb_added.at(i, 2))
                pool.wait_ge(ln2.sem, ln2.before(i))
                pool.wait_ge(h_out.sem, h_out.before(i))
                pool.wait_ge(ln1.sem, ln1.at(i, 9))
                pool.sem_inc(passed.sem, 1)
                pool.tensor_copy(h1[:, :, :], h0[:, :, :]).then_inc(h_kept.sem, 1)

            def low_p(i, n):
                u, (h, nj) = n // 3, score_heads(n % 3)
                pool.wait_ge(p_hi.sem, p_hi.at(i, n + 1))
                raw = P32_par(n % 2, nj)
                pool.tensor_tensor(by_parity(P_l[:, u, h:h + 2 * nj, :]), raw[:, :, :, 0:MAIN],
                                   by_parity(P_h[:, u, h:h + 2 * nj, :]), ALU.subtract)
                pool.tensor_tensor(by_parity(Pq_l[:, u, h:h + 2 * nj, 0:TAIL]), raw[:, :, :, MAIN:S],
                                   by_parity(Pq_h[:, u, h:h + 2 * nj, 0:TAIL]), ALU.subtract).then_inc(p_lo.sem, 1)

            def pair(i, following):
                if following:
                    inverse_deviation(i + 1, mv, rstd, ln1, rsqrt1)
                pool.wait_ge(ids_out.sem, ids_out.before(i))
                low_p(i, 0)
                if following:
                    low_xn(i + 1)
                low_p(i, 2)
                low_p(i, 4)
                rows = slice(0, TAIL)
                pool.wait_ge(p_hi.sem, p_hi.at(i, 7))
                pool.wait_ge(p_lo.sem, p_lo.at(i, 3))
                pool.tensor_tensor(by_parity(Pt_l[rows]), P32t[rows], by_parity(Pt_h[rows]), ALU.subtract
                                   ).then_inc(p_lo.sem, 1)
                pool.wait_ge(p_lo.sem, p_lo.at(i, 4))
                if following:
                    low_patches(i + 2)
                for t in range(3):
                    pool.wait_ge(o_hi.sem, o_hi.at(i, t + 1))
                    pool.tensor_tensor(O_l[:, t, :], O[:, t, :], O_h[:, t, :], ALU.subtract).then_inc(o_lo.sem, 1)
                if following:
                    for t in range(3):
                        low_pack(i + 1, t)
                inverse_deviation(i, mv2, rstd2, ln2, rsqrt2)
                for t in range(3):
                    pool.wait_ge(x2_hi.sem, x2_hi.at(i, t + 1))
                    pool.tensor_tensor(x2_hl[:, t, 1, :], xn2[:, t, :], x2_hl[:, t, 0, :], ALU.subtract
                                       ).then_inc(x2_lo.sem, 1)
                if following:
                    keep_h(i + 1)
                pool.wait_ge(route.sem, route.at(i, 14))
                pool.sem_inc(passed.sem, 1)
                for t in range(3):
                    pool.indirect_dma_start(
                        out=id_list[:, :], out_offset=bass.IndirectOffsetOnAxis(ap=place[:, t:t + 1], axis=0),
                        in_=ids[:, t:t + 1], in_offset=None, bounds_check=E * CAP - 1, oob_is_err=False,
                    ).then_inc(ids_out.sem, 16)

            inverse_deviation(0, mv, rstd, ln1, rsqrt1)
            low_xn(0)
            keep_h(0)
            for half in range(2):
                cols = slice(half * D, half * D + D)
                pool.dma_start(rows_x[NTOK:NTOK + 1, cols], zero_row[0:1, :].bitcast(F16)[:, cols]).then_inc(ids_out.sem, 16)
                cols = slice(half * D // 2, (half + 1) * D // 2)
                pool.dma_start(rows_h[NTOK:NTOK + 1, cols], zero_row[0:1, cols]).then_inc(out_done.sem, 16)
            pool.dma_start(id_list[0:E * CAP, :].rearrange("(p n) a -> p (n a)", p=128), pad_ids[:, :]).then_inc(ids_out.sem, 16)
            for t in range(3):
                low_pack(0, t)
            low_patches(1)
            with pool.Fori(0, PAIRS - 1) as i:
                pair(i, True)
            pair(PAIRS - 1, False)

            pool.wait_ge(tabled.sem, tabled.at(0, 10))
            pool.wait_ge(ids_out.sem, ids_out.at(PAIRS - 1, 3))
            pool.wait_ge(out_done.sem, out_done.before(0))
            pool.wait_ge(h_out.sem, h_out.at(PAIRS - 1, 4))
            pool.wait_ge(rows_out.sem, rows_out.at(PAIRS - 1, 4))

            def gather_x(g, s):
                if s == 0:
                    pool.wait_ge(idx_in_in.sem, idx_in_in.at(g, 1))
                    pool.sem_inc(passed.sem, 1)
                    pool.wait_ge(g_turned.sem, g_turned.before(g))
                    pool.sem_inc(passed.sem, 1)
                pool.indirect_dma_start(
                    out=Xg[:, s, :], out_offset=None, in_=rows_x[:, :],
                    in_offset=bass.IndirectOffsetOnAxis(ap=idx_in[:, s:s + 1], axis=0),
                    bounds_check=NTOK, oob_is_err=False).then_inc(x_in.sem, 16)

            def gather_h(g):
                pool.wait_ge(idx_h_in.sem, idx_h_in.at(g, 1))
                pool.sem_inc(passed.sem, 1)
                pool.wait_ge(hb_done.sem, hb_done.before(g))
                pool.sem_inc(passed.sem, 1)
                for s in range(2):
                    pool.indirect_dma_start(
                        out=Hg[:, s, :], out_offset=None, in_=rows_h[:, :],
                        in_offset=bass.IndirectOffsetOnAxis(ap=idx_h[:, s:s + 1], axis=0),
                        bounds_check=NTOK, oob_is_err=False).then_inc(h_in.sem, 16)

            gather_x(0, 0)
            gather_x(0, 1)
            gather_h(0)
            last = pool.value_load(table[0:1, E:E + 1], min_val=E, max_val=E + MAXT)
            with pool.Fori(0, last) as g:
                for k in range(8):
                    pool.wait_ge(u_hi.sem, u_hi.at(g, k + 1))
                    pool.tensor_tensor(u_l[:, k, :], u32[:, k % U32, :], u_h[:, k, :], ALU.subtract
                                       ).then_inc(u_lo.sem, 1)
                    if k in (1, 3):
                        gather_x(g + 1, k // 3)
                gather_h(g + 1)
                pool.wait_ge(idx_out_in.sem, idx_out_in.at(g, 1))
                for s in range(2):
                    pool.wait_ge(yo_ready.sem, yo_ready.at(g, s + 1))
                    pool.sem_inc(passed.sem, 1)
                    pool.indirect_dma_start(
                        out=out[:, :], out_offset=bass.IndirectOffsetOnAxis(ap=idx_out[:, s:s + 1], axis=0),
                        in_=yo[:, s, :], in_offset=None, bounds_check=NTOK - 1, oob_is_err=False,
                    ).then_inc(out_done.sem, 16)
            pool.wait_ge(x_in.sem, x_in.at(last, 2))
            pool.wait_ge(h_in.sem, h_in.at(last, 2))

        @block.scalar
        def _(act):
            start_signals(act, "scalar")
            def high_patches(i):
                act.wait_ge(patches_in.sem, patches_in.at(i, 1))
                act.wait_ge(emb_ready.sem, emb_ready.before(i))
                act.activation(patch_h[:, :, :], patch_sb[:, :, :], ACT.Copy).then_inc(patch_hi.sem, 1)

            high_patches(0)
            act.wait_ge(emb_w_in.sem, emb_w_in.at(0, 2))
            act.activation(w_emb_h[:, :, :], w_emb_sb[:, :, :], ACT.Copy, scale=WS).then_inc(w_emb_hi.sem, 1)
            act.wait_ge(w_in.sem, w_in.at(0, 5))
            for raw, hi_ in ((wq_raw, wq_h), (wo_raw, wo_h), (rw_raw, rw_h)):
                act.activation(hi_[:, :, :], raw[:, :, :], ACT.Copy, scale=WS).then_inc(split_h.sem, 1)
            act.wait_ge(const_ready.sem, const_ready.at(0, 11))
            act.wait_ge(filled_too.sem, filled_too.at(0, 9))

            def high_xn(i):
                for t in range(3):
                    act.wait_ge(ln1.sem, ln1.at(i, 7 + t))
                    act.wait_ge(xn_turned.sem, xn_turned.before(i))
                    act.activation(xn_h[:, t, :], xn[:, t, :], ACT.Copy).then_inc(xn_hi.sem, 1)

            def turned_xn(i):
                for tiles, bank, turned in ((slice(0, 2), X[:, 1, :], 2), (slice(2, 3), X[:, 0, 0:256], 3)):
                    act.wait_ge(xn_turned.sem, xn_turned.at(i, turned))
                    act.activation(xT[:, tiles].rearrange("p t a b c -> p (t a b c)"), bank.bitcast(F16), ACT.Copy
                                   ).then_inc(xT_ready.sem, 1)

            def high_v(i, t):
                act.wait_ge(qkv_ready.sem, qkv_ready.at(i, t + 1))
                act.activation(V_h[:, t, :, 0:DH], proj[t][:, 1, 0:D].rearrange("p (h d) -> p h d", h=H), ACT.Copy,
                               scale=1 / WS).then_inc(v_hi.sem, 1)

            def high_pack(i, t):
                act.wait_ge(qk_ready.sem, qk_ready.at(i, t + 1))
                if t >= 2:
                    act.wait_ge(pack_turned.sem, pack_turned.at(i, t - 1))
                else:
                    act.wait_ge(pack_turned.sem, pack_turned.before(i))
                for m in range(2):
                    src = qk[:, t % 2, D * m:D * m + D].rearrange("p (h a d) -> p h a d", h=H, a=1
                                                                  ).broadcast_to((128, H, 2, DH))
                    dst = pack[:, t % 2, m, :, :].rearrange("p h (s d) -> p h s d", d=DH)
                    dst = dst[:, :, 0:2, :] if m == 0 else dst[:, :, 0:3:2, :]
                    act.activation(dst, src, ACT.Copy).then_inc(pack_hi.sem, 1)

            def turned_q(i, t):
                act.wait_ge(pack_turned.sem, pack_turned.at(i, t + 1))
                src = halves(SC[1 - t % 2][:, 0, :])
                if t < 2:
                    act.activation(QT[:, t, :, 0:MAIN], src, ACT.Copy).then_inc(qT_ready.sem, 1)
                else:
                    act.activation(QT[:, :, :, MAIN:S], tail_cols(src), ACT.Copy).then_inc(qT_ready.sem, 1)

            def turned_tiles(i, turned, dst, ready):
                for t in range(3):
                    act.wait_ge(turned.sem, turned.at(i, t + 1))
                    act.activation(dst[:, t].rearrange("p a b c -> p (a b c)"), turn_banks[t].bitcast(F16)[:, 0:512], ACT.Copy
                                   ).then_inc(ready.sem, 1)

            def exponentials(i, items):
                for n in items:
                    act.wait_ge(st_ready.sem, st_ready.at(i, min(n, 6) + 1))
                    if n >= 6:
                        rows = slice(TAILS * (n - 6), TAILS * (n - 6) + TAIL)
                        act.activation(P32t[rows], SC[1][rows, :, 0:8 * TAIL].rearrange("p a (b q) -> p a b q", b=8),
                                       ACT.Exp, scale=DH ** -0.5).then_inc(exp_done.sem, 1)
                        continue
                    _, nj = score_heads(n % 3)
                    if n == 0:
                        act.wait_ge(p_lo.sem, p_lo.before(i))
                    elif n == 1:
                        act.wait_ge(p_lo_odd.sem, p_lo_odd.before(i))
                    elif n % 2 == 0:
                        act.wait_ge(p_lo.sem, p_lo.at(i, n // 2))
                    else:
                        act.wait_ge(p_lo_odd.sem, p_lo_odd.at(i, n // 2))
                    act.activation(P32_par(n % 2, nj),
                                   SC[(n + 7) % 2][:, :, 0:nj * S].rearrange("p a (b q) -> p a b q", b=nj),
                                   ACT.Exp, scale=DH ** -0.5).then_inc(exp_done.sem, 1)

            def pair(i, following):
                act.wait_ge(negm_turned.sem, negm_turned.at(i, 1))
                mt = X[:, 1, :].bitcast(F16)[:, 0:384].rearrange("p (t n) -> p t n", t=3)
                act.activation(mT[:, :, 0:MAIN], mt[:, 0:2, :], ACT.Copy).then_inc(mT_ready.sem, 1)
                act.activation(mT[:, :, MAIN:S], mt[:, 2, :].rearrange("p (u n) -> p u n", u=2)[:, :, 0:TAIL], ACT.Copy
                               ).then_inc(mT_ready.sem, 1)
                exponentials(i, range(0, 1))
                if following:
                    high_xn(i + 1)
                exponentials(i, range(1, 8))
                if following:
                    turned_xn(i + 1)
                    high_patches(i + 2)
                for c in range(2):
                    if c == 0:
                        act.wait_ge(ew_in[0].sem, ew_in[0].at(0, LOADS))
                    piece = bass.ds((2 * i + c) * PIECE, PIECE)
                    act.activation(w_hi[0][:, piece], w_raw[0][:, piece], ACT.Copy, scale=WS).then_inc(ew_hi.sem, 1)
                for t in range(3):
                    act.wait_ge(o_ready.sem, o_ready.at(i, t + 1 if t < 2 else 6))
                    act.activation(O_h[:, t, :], O[:, t, :], ACT.Copy).then_inc(o_hi.sem, 1)
                if following:
                    high_v(i + 1, 0)
                turned_tiles(i, o_turned, oT, oT_ready)
                if following:
                    high_pack(i + 1, 0)
                    high_v(i + 1, 1)
                    high_pack(i + 1, 1)
                    high_v(i + 1, 2)
                    turned_q(i + 1, 0)
                    high_pack(i + 1, 2)
                    turned_q(i + 1, 1)
                    turned_q(i + 1, 2)
                for t in range(3):
                    act.wait_ge(ln2.sem, ln2.at(i, 7 + t))
                    act.wait_ge(x2_turned.sem, x2_turned.before(i))
                    act.wait_ge(rows_out.sem, rows_out.before(i))
                    act.activation(x2_hl[:, t, 0, :], xn2[:, t, :], ACT.Copy).then_inc(x2_hi.sem, 1)
                turned_tiles(i, x2_turned, x2T, x2T_ready)

            high_xn(0)
            turned_xn(0)
            for t in range(3):
                high_v(0, t)
                if t == 2:
                    turned_q(0, 0)
                high_pack(0, t)
            turned_q(0, 1)
            turned_q(0, 2)
            high_patches(1)
            with act.Fori(0, PAIRS - 1) as i:
                pair(i, True)
            pair(PAIRS - 1, False)

            def turned_x(g):
                act.wait_ge(g_turned.sem, g_turned.at(g, 1))
                act.activation(gT[:, :, :, :].rearrange("p a b c -> p (a b c)"),
                               PV[:, 0, :].bitcast(F16)[:, 0:4 * TT], ACT.Copy).then_inc(gT_ready.sem, 1)

            def tile(g, off, u, load_part, split_piece):
                for k in range(8):
                    if k == 5:
                        act.wait_ge(out_done.sem, out_done.before(g))
                        with nc.allow_non_contiguous_dma(reason="ids, one to a partition"):
                            act.dma_start(idx_out[:, :], id_list[bass.ds(g * TT + off, TT), :].rearrange(
                                "(s p) a -> p (s a)", s=2)).then_inc(idx_out_in.sem, 16)
                    load_part(k)
                    act.wait_ge(up_ready.sem, up_ready.at(g, k + 1))
                    if k >= 2:
                        act.wait_ge(glu_done.sem, glu_done.at(g, k - 1))
                    else:
                        act.wait_ge(glu_done.sem, glu_done.before(g))
                    act.activation(sigm[:, k % 2, :], up_banks[k % 4][:, TT:2 * TT], ACT.Sigmoid,
                                   scale=1 / WS, bias=b1_gate[u][:, k:k + 1]).then_inc(sig_done.sem, 1)
                    if k % 2:
                        split_piece(k // 2)
                for n in range(4, PIECES):
                    if n == 8:
                        turned_x(g + 1)
                    load_part(4 + n)
                    split_piece(n)
                turned_x(g + 1)

            def expert(j, u, load, split):
                e = 2 * j + u
                lo = act.value_load(table[0:1, bass.ds(e, 1)], min_val=0, max_val=E + MAXT)
                hi = act.value_load(table[0:1, bass.ds(e + 1, 1)], min_val=1, max_val=E + MAXT)
                off = act.value_load(table[0:1, bass.ds(e + E + 1, 1)], min_val=0, max_val=E * CAP)

                def split_piece(n):
                    if n == 0:
                        act.wait_ge(ew_in[1 - u].sem, ew_in[1 - u].at(j + u, LOADS))
                        act.wait_ge(y_ready.sem, y_ready.before(lo))
                    piece = slice(n * PIECE, (n + 1) * PIECE)
                    act.activation(w_hi[1 - u][:, piece], w_raw[1 - u][:, piece], ACT.Copy, scale=WS
                                   ).then_inc(ew_hi.sem, 1)

                if split:
                    act.wait_ge(hb_done.sem, hb_done.before(lo))
                    act.dma_start(b2_e[1 - u][:, :], b2[bass.ds(e + 1, 1), :].broadcast_to((HT, D))
                                  ).then_inc(b2_in[1 - u].sem, 16)
                def load_part(n):
                    if n == 0:
                        act.wait_ge(ew_lo.sem, ew_lo.at(e, PIECES))
                    dst, src = weights_part(e + 2, u, n)
                    act.dma_start(dst, src).then_inc(ew_in[u].sem, 16)

                act.wait_ge(bias_ready.sem, bias_ready.at(e, 2))
                tile(lo, off, u, load_part if load else lambda n: None, split_piece if split else lambda n: None)
                with act.If(lo + 1 < hi):
                    with act.Fori(lo + 1, hi) as g:
                        tile(g, off, u, lambda n: None, lambda n: None)

            act.activation(sigm[0:1, 0, 0:1], zero_row[0:1, 0:1], ACT.Sigmoid)
            act.wait_ge(tabled.sem, tabled.at(0, 10))
            turned_x(0)
            with act.Fori(0, E // 2 - 1) as j:
                for u in range(2):
                    expert(j, u, True, True)
            for u in range(2):
                expert(E // 2 - 1, u, False, u == 0)

        @block.vector
        def _(dve):
            start_signals(dve, "vector")
            for dst, value in ((h0[:, :, :], 0.0), (neg_m[:, :, :, :], 0.0), (O[:, :, :], 0.0), (V_l[:, :, :, :], 0.0),
                               (V_h[:, :, :, :], 1.0)):
                dve.memset(dst, value).then_inc(filled.sem, 1)
            dve.wait_ge(w_emb_hi.sem, w_emb_hi.at(0, 1))
            dve.scalar_tensor_tensor(out=w_emb_l[:, :, :], in0=w_emb_sb[:, :, :], scalar=WS, in1=w_emb_h[:, :, :],
                                     op0=ALU.mult, op1=ALU.subtract).then_inc(w_emb_ready.sem, 1)
            dve.wait_ge(const_in.sem, const_in.at(0, 1))
            dve.memset(ones[:, :], 1.0).then_inc(const_ready.sem, 1)
            for dst, name in ((ident, "ident"), (identb, "ident"), (mask_main, "mask_main"), (mask_tail, "mask_tail"),
                              (mask_t_main, "mask_t_main"), (mask_t_tail, "mask_t_tail"),
                              (before, "before"), (base, "list_base"), (ids_f, "id0")):
                dve.tensor_copy(dst[:, :], const(name)).then_inc(const_ready.sem, 1)
            dve.tensor_copy(head_sel[:, :, :], const("head_rows").rearrange("p (h a) -> p h a", a=1
                                                                            ).broadcast_to((128, H, 128))
                            ).then_inc(const_ready.sem, 1)

            def moments(i, src, st, mvt, signal):
                for t in range(3):
                    dve.bn_stats(st[:, t, :], src[:, t, :]).then_inc(signal.sem, 1)
                for t in range(3):
                    dve.wait_ge(signal.sem, signal.at(i, t + 1))
                    dve.sem_inc(passed.sem, 1)
                    dve.bn_aggr(mvt[:, t, :], st[:, t, :]).then_inc(signal.sem, 1)

            def normed(i, src, dst, mvt, rs, signal, rsqrt):
                dve.wait_ge(rsqrt.sem, rsqrt.at(i, 2))
                for t in range(3):
                    dve.tensor_scalar(dst[:, t, :], src[:, t, :], mvt[:, t, 0:1], rs[:, t:t + 1],
                                      ALU.subtract, ALU.mult).then_inc(signal.sem, 1)

            def embedding(i):
                dve.wait_ge(emb_ready.sem, emb_ready.at(i, 1))
                dve.wait_ge(txt_in.sem, txt_in.at(i, 4))
                for u in range(2):
                    rows = slice(TAILS * u, TAILS * u + EMB)
                    dve.scalar_tensor_tensor(out=h0[0:EMB, u, :], in0=PV[rows, 1, 0:D], scalar=1 / WS, in1=pos_sb[rows, :],
                                             op0=ALU.mult, op1=ALU.add).then_inc(emb_added.sem, 1)
                dve.wait_ge(emb_added.sem, emb_added.at(i, 2))
                moments(i, h0, stats, mv, ln1)

            def first_norm(i):
                dve.wait_ge(xn_lo.sem, xn_lo.before(i))
                normed(i, h0, xn, mv, rstd, ln1, rsqrt1)

            def rotary(i, t):
                dve.wait_ge(qkv_ready.sem, qkv_ready.at(i, t + 1))
                ty = t // 2
                pair_of = proj[t][:, 0, :].rearrange("p (n a d) -> p n a d", a=2, d=8)
                a_of = rope_a[:, :].rearrange("p (n a d) -> p n a d", a=2, d=8)
                b_of = rope_b[:, :].rearrange("p (n a d) -> p n a d", a=2, d=8)
                cos = const("cos").rearrange("p (t n a d) -> p t n a d", t=2, n=1, a=2)[:, ty]
                sin = const("sin").rearrange("p (t n a d) -> p t n a d", t=2, n=1, a=2)[:, ty]
                if t:
                    dve.wait_ge(qk_ready.sem, qk_ready.at(i, t))
                else:
                    dve.wait_ge(qk_ready.sem, qk_ready.before(i))
                dve.tensor_tensor(a_of, pair_of, cos.broadcast_to((128, 2 * H, 2, 8)), ALU.mult
                                  ).then_inc(rope.sem, 1)
                for half in range(2):
                    dve.tensor_tensor(b_of[:, :, half, :], pair_of[:, :, 1 - half, :],
                                      sin[:, :, half, :].broadcast_to((128, 2 * H, 8)), ALU.mult
                                      ).then_inc(rope.sem, 1)
                dve.wait_ge(v_hi.sem, v_hi.at(i, t + 1))
                dve.scalar_tensor_tensor(out=V_l[:, t, :, 0:DH],
                                         in0=proj[t][:, 1, 0:D].rearrange("p (h d) -> p h d", h=H),
                                         scalar=1 / WS, in1=V_h[:, t, :, 0:DH], op0=ALU.mult, op1=ALU.subtract
                                         ).then_inc(v_lo.sem, 1)
                if t >= 2:
                    dve.wait_ge(pack_hi.sem, pack_hi.at(i, 2))
                    dve.wait_ge(pack_lo.sem, pack_lo.at(i, 2))
                elif t == 0:
                    dve.wait_ge(pack_hi.sem, pack_hi.before(i))
                    dve.wait_ge(pack_lo.sem, pack_lo.before(i))
                dve.wait_ge(rope.sem, rope.at(i, 3 * t + 3))
                dve.tensor_tensor(qk[:, t % 2, :], rope_a[:, :], rope_b[:, :], ALU.add).then_inc(qk_ready.sem, 1)

            def turned_k(i, t):
                dve.wait_ge(pack_turned.sem, pack_turned.at(i, t + 1))
                src = halves(SC[1 - t % 2][:, 1, :])
                if t < 2:
                    dve.tensor_copy(KT[:, t, :, 0:MAIN], src).then_inc(kT_ready.sem, 1)
                else:
                    dve.tensor_copy(KT[:, :, :, MAIN:S], tail_cols(src)).then_inc(kT_ready.sem, 1)

            def split_p(i, items):
                for n in items:
                    dve.wait_ge(exp_done.sem, exp_done.at(i, n + 1))
                    if n < 6:
                        u, (h, nj) = n // 3, score_heads(n % 3)
                        raw = P32_par(n % 2, nj)
                        hi_, lo_ = (by_parity(p[:, u, h:h + 2 * nj, :]) for p in (P_h, P_l))
                        hi_q, lo_q = (by_parity(p[:, u, h:h + 2 * nj, 0:TAIL]) for p in (Pq_h, Pq_l))
                        dve.tensor_copy(hi_, raw[:, :, :, 0:MAIN])
                        dve.tensor_copy(hi_q, raw[:, :, :, MAIN:S]).then_inc(p_hi.sem, 1)
                        if n % 2:
                            dve.wait_ge(p_hi.sem, p_hi.at(i, n + 1))
                            dve.tensor_tensor(lo_, raw[:, :, :, 0:MAIN], hi_, ALU.subtract)
                            dve.tensor_tensor(lo_q, raw[:, :, :, MAIN:S], hi_q, ALU.subtract).then_inc(p_lo_odd.sem, 1)
                        continue
                    rows = slice(TAILS * (n - 6), TAILS * (n - 6) + TAIL)
                    hi_, lo_, raw = by_parity(Pt_h[rows]), by_parity(Pt_l[rows]), P32t[rows]
                    dve.tensor_copy(hi_, raw).then_inc(p_hi.sem, 1)
                    if n % 2:
                        dve.wait_ge(p_hi.sem, p_hi.at(i, n + 1))
                        dve.tensor_tensor(lo_, raw, hi_, ALU.subtract).then_inc(p_lo_odd.sem, 1)

            def by_tile(ap):
                return ap.rearrange("p (t e) -> p t e", t=1).broadcast_to((128, 3, E))

            def by_expert(ap):
                return ap.rearrange("p (t e) -> p t e", e=1).broadcast_to((128, 3, E))

            def maxima(i, items):
                for n in items:
                    dve.wait_ge(s_ready.sem, s_ready.at(i, n + 1))
                    if n < 4:
                        tile, h, nj, width = n // 2, 8 * (n % 2), 4, MAIN
                    else:
                        (h, nj), tile, width = score_heads(n - 4), 2, S
                    dve.tensor_reduce(smax[:, tile, h:h + 2 * nj].rearrange("p (j a) -> p a j", a=2),
                                      SC[n % 2][:, :, 0:nj * width].rearrange("p a (j k) -> p a j k", j=nj),
                                      AX, ALU.max).then_inc(max_done.sem, 1)

            def choose(i):
                dve.wait_ge(logits_ready.sem, logits_ready.at(i, 1))
                dve.scalar_tensor_tensor(out=logit[:, :, :], in0=X[:, 0, 0:3 * E].rearrange("p (t e) -> p t e", t=3),
                                         scalar=1 / WS, in1=by_tile(rb_sb[:, :]), op0=ALU.mult, op1=ALU.add
                                         ).then_inc(route.sem, 1)
                dve.wait_ge(route.sem, route.at(i, 1))
                dve.tensor_reduce(lmax[:, :], logit[:, :, :], AX, ALU.max).then_inc(route.sem, 1)
                dve.wait_ge(route.sem, route.at(i, 2))
                dve.tensor_tensor(tie[:, :, :], logit[:, :, :], by_expert(lmax[:, :]), ALU.is_equal).then_inc(route.sem, 1)
                dve.wait_ge(route.sem, route.at(i, 3))
                dve.tensor_tensor(pick[:, :, :], tie[:, :, :], by_tile(const("expert_m8")), ALU.mult).then_inc(route.sem, 1)
                dve.wait_ge(route.sem, route.at(i, 4))
                dve.tensor_reduce(first[:, :], pick[:, :, :], AX, ALU.min).then_inc(route.sem, 1)
                dve.wait_ge(route.sem, route.at(i, 5))
                dve.tensor_tensor(onehot[:, :, :], by_tile(const("expert_m8")), by_expert(first[:, :]), ALU.is_equal
                                  ).then_inc(route.sem, 1)
                dve.wait_ge(route.sem, route.at(i, 6))
                dve.tensor_tensor(onehot16[:, :, :], onehot[:, :, :], by_expert(const("valid")), ALU.mult
                                  ).then_inc(route.sem, 1)

            def number(i):
                dve.wait_ge(ranks_ready.sem, ranks_ready.at(i, 1))
                dve.wait_ge(route.sem, route.at(i, 7))
                dve.tensor_tensor(place_e[:, :, :], X[:, 0, 0:3 * E].rearrange("p (t e) -> p t e", t=3),
                                  by_tile(base[:, :]), ALU.add).then_inc(route.sem, 1)
                dve.wait_ge(route.sem, route.at(i, 8))
                dve.tensor_tensor(place_e[:, :, :], place_e[:, :, :], onehot16[:, :, :], ALU.mult).then_inc(route.sem, 1)
                dve.wait_ge(route.sem, route.at(i, 9))
                dve.tensor_reduce(place_f[:, :], place_e[:, :, :], AX, ALU.add).then_inc(route.sem, 1)
                dve.wait_ge(route.sem, route.at(i, 10))
                dve.tensor_tensor(place[:, :], place_f[:, :], const("pad_place"), ALU.add).then_inc(route.sem, 1)
                dve.tensor_tensor(base[:, :], base[:, :], X[:, 0, 3 * E:4 * E], ALU.add).then_inc(route.sem, 1)
                dve.tensor_copy(ids[:, :], ids_f[:, :]).then_inc(route.sem, 1)
                dve.tensor_scalar(ids_f[:, :], ids_f[:, :], float(2 * S), None, ALU.add).then_inc(route.sem, 1)

            def pair(i, following):
                dve.wait_ge(max_done.sem, max_done.at(i, 7))
                nm = neg_m[:, :, :, 0:H]
                dve.tensor_scalar(nm, smax[:, :, :].rearrange("p t (a h) -> p t a h", a=1
                                                              ).broadcast_to((128, 3, 2, H)), -1.0, None, ALU.mult
                                  ).then_inc(negm_hi.sem, 1)
                dve.wait_ge(negm_hi.sem, negm_hi.at(i, 1))
                for d in range(2):
                    ins = dve.scalar_tensor_tensor(out=neg_m[:, :, d, H:2 * H], in0=smax[:, :, :], scalar=-1.0,
                                                   in1=neg_m[:, :, d, 0:H], op0=ALU.mult, op1=ALU.subtract)
                    ins.then_inc(negm_ready.sem, 1)


                if following:
                    embedding(i + 1)
                    first_norm(i + 1)
                split_p(i, range(0, 8))

                for c in range(2):
                    dve.wait_ge(ew_hi.sem, ew_hi.at(0, 2 * i + c + 1))
                    piece = bass.ds((2 * i + c) * PIECE, PIECE)
                    dve.scalar_tensor_tensor(out=w_lo[0][:, piece], in0=w_raw[0][:, piece], scalar=WS,
                                             in1=w_hi[0][:, piece], op0=ALU.mult, op1=ALU.subtract
                                             ).then_inc(ew_lo.sem, 1)

                dve.wait_ge(o_lo.sem, o_lo.before(i))
                for n in range(6):
                    dve.wait_ge(pv_ready.sem, pv_ready.at(i, n + 1 if n < 2 else n // 2 + 2))
                    if n < 2:
                        heads, rows, to, slot = slice(0, H), slice(0, 128), slice(0, 128), n
                        src = PV[:, n, 0:H * (DH + 1)].rearrange("p (h d) -> p h d", h=H)
                    else:
                        u, par = n // 2 - 1, n % 2
                        heads, slot = slice(par, H, 2), 2 + u
                        rows, to = slice(TAILS * par, TAILS * par + TAIL), slice(TAILS * u, TAILS * u + TAIL)
                        src = X[rows, u, 0:H * (DH + 1)].rearrange("p (h d) -> p h d", h=H)[:, heads, :]
                    inv = rinv[rows, slot, heads]
                    dve.reciprocal(inv, src[:, :, DH]).then_inc(o_rinv.sem, 1)
                    dve.wait_ge(o_rinv.sem, o_rinv.at(i, n + 1))
                    dve.tensor_tensor(O[to, min(n, 2), :].rearrange("p (h d) -> p h d", h=H)[:, heads, :], src[:, :, 0:DH],
                                      inv.rearrange("p (h a) -> p h a", a=1
                                                    ).broadcast_to((rows.stop - rows.start, src.shape[1], DH)), ALU.mult
                                      ).then_inc(o_ready.sem, 1)

                if following:
                    rotary(i + 1, 0)
                    rotary(i + 1, 1)
                dve.wait_ge(h_kept.sem, h_kept.at(i, 1))
                for t in range(3):
                    dve.wait_ge(wo_ready.sem, wo_ready.at(i, t + 1))
                    dve.scalar_tensor_tensor(out=h1[:, t, :], in0=wo_banks[t][:, 0:D], scalar=1 / WS, in1=h1[:, t, :],
                                             op0=ALU.mult, op1=ALU.add).then_inc(h1_ready.sem, 1)
                dve.wait_ge(h1_ready.sem, h1_ready.at(i, 3))
                if following:
                    rotary(i + 1, 2)
                moments(i, h1, stats2, mv2, ln2)
                if following:
                    for t in range(3):
                        turned_k(i + 1, t)
                dve.wait_ge(x2_lo.sem, x2_lo.before(i))
                normed(i, h1, xn2, mv2, rstd2, ln2, rsqrt2)
                if following:
                    maxima(i + 1, range(0, 4))
                choose(i)
                if following:
                    maxima(i + 1, range(4, 6))
                number(i)
                if following:
                    maxima(i + 1, range(6, 7))

            dve.wait_ge(filled.sem, filled.at(0, 5))
            dve.wait_ge(pos_in.sem, pos_in.at(0, 2))
            embedding(0)
            dve.wait_ge(w_in.sem, w_in.at(0, 5))
            for n, (raw, hi_, lo_) in enumerate(((wq_raw, wq_h, wq_l), (wo_raw, wo_h, wo_l), (rw_raw, rw_h, rw_l))):
                dve.wait_ge(split_h.sem, split_h.at(0, n + 1))
                dve.scalar_tensor_tensor(out=lo_[:, :, :], in0=raw[:, :, :], scalar=WS, in1=hi_[:, :, :],
                                         op0=ALU.mult, op1=ALU.subtract).then_inc(w_ready.sem, 1)
            first_norm(0)
            for t in range(3):
                rotary(0, t)
            for t in range(3):
                turned_k(0, t)
            maxima(0, range(7))
            with dve.Fori(0, PAIRS - 1) as i:
                pair(i, True)
            pair(PAIRS - 1, False)

            steps = [0]

            def step(ins):
                steps[0] += 1
                ins.then_inc(tabled.sem, 1)
                dve.wait_ge(tabled.sem, tabled.at(0, steps[0]))

            dve.wait_ge(route.sem, route.at(PAIRS - 1, 14))
            step(dve.tensor_tensor(count[:, :], base[:, :], const("list_base"), ALU.subtract))
            step(dve.tensor_tensor(above[:, :, :], count[:, :].rearrange("p (e a) -> p e a", a=1
                                                                         ).broadcast_to((128, E, MAXT - 1)),
                                   const("tile_edges").rearrange("p (a n) -> p a n", a=1
                                                                 ).broadcast_to((128, E, MAXT - 1)), ALU.is_gt))
            step(dve.tensor_reduce(tiles[:, :], above[:, :, :], AX, ALU.add))
            step(dve.tensor_scalar(tiles[:, :], tiles[:, :], 1.0, None, ALU.add))
            step(dve.tensor_tensor(cum_all[:, :, :], const("lower").rearrange("p (e n) -> p e n", e=E),
                                   tiles[:, :].rearrange("p (a n) -> p a n", a=1).broadcast_to((128, E, E)), ALU.mult))
            step(dve.tensor_reduce(cum[:, :], cum_all[:, :, :], AX, ALU.add))
            step(dve.tensor_copy(table_f[:, 0:E], cum[:, :]))
            step(dve.tensor_tensor(table_f[:, E:E + 1], cum[:, E - 1:E], tiles[:, E - 1:E], ALU.add))
            step(dve.scalar_tensor_tensor(out=table_f[:, E + 1:2 * E + 1], in0=cum[:, :], scalar=-float(TT),
                                          in1=const("list_base"), op0=ALU.mult, op1=ALU.add))
            step(dve.tensor_copy(table[:, :], table_f[:, :]))

            def tile(g, u, split_piece):
                dve.wait_ge(h_in.sem, h_in.at(g, 2))
                dve.wait_ge(yo_ready.sem, yo_ready.before(g))
                dve.tensor_tensor(hb[:, :, :], Hg[:, :, :], b2_e[u][:, :].rearrange("p (a d) -> p a d", a=1
                                                                               ).broadcast_to((HT, 2, D)),
                                  ALU.add).then_inc(hb_done.sem, 1)
                for k in range(8):
                    dve.wait_ge(sig_done.sem, sig_done.at(g, k + 1))
                    if k >= U32:
                        dve.wait_ge(u_lo.sem, u_lo.at(g, k - U32 + 1))
                    elif k == 0:
                        dve.wait_ge(u_lo.sem, u_lo.before(g))
                    dve.scalar_tensor_tensor(out=u32[:, k % U32, :], in0=up_banks[k % 4][:, 0:TT],
                                             scalar=b1_lin[u][:, k:k + 1], in1=sigm[:, k % 2, :],
                                             op0=ALU.add, op1=ALU.mult).then_inc(glu_done.sem, 1)
                    dve.wait_ge(glu_done.sem, glu_done.at(g, k + 1))
                    dve.tensor_copy(u_h[:, k, :], u32[:, k % U32, :]).then_inc(u_hi.sem, 1)
                    if k % 2:
                        split_piece(k // 2)
                for n in range(4, PIECES):
                    split_piece(n)
                dve.wait_ge(hb_done.sem, hb_done.at(g, 1))
                dve.wait_ge(out_done.sem, out_done.before(g))
                for s in range(2):
                    dve.wait_ge(y_ready.sem, y_ready.at(g, s + 1))
                    dve.scalar_tensor_tensor(out=yo[:, s, :], in0=y_banks[s][0:HT, 0:D], scalar=1 / (WS * WS),
                                             in1=hb[:, s, :], op0=ALU.mult, op1=ALU.add
                                             ).then_inc(yo_ready.sem, 1)

            def biases(e, u):
                b1_of = b1_all[:, bass.ds(e, 1), :].rearrange("p a c -> p (a c)")
                dve.tensor_scalar(b1_lin[u][:, :], b1_of[:, 0:8], WS, None, ALU.mult).then_inc(bias_ready.sem, 1)
                dve.tensor_copy(b1_gate[u][:, :], b1_of[:, 8:16]).then_inc(bias_ready.sem, 1)

            def expert(j, u, split):
                e = 2 * j + u
                lo = dve.value_load(table[0:1, bass.ds(e, 1)], min_val=0, max_val=E + MAXT)
                hi = dve.value_load(table[0:1, bass.ds(e + 1, 1)], min_val=1, max_val=E + MAXT)

                def split_piece(n):
                    dve.wait_ge(ew_hi.sem, ew_hi.at(e + 1, n + 1))
                    piece = slice(n * PIECE, (n + 1) * PIECE)
                    dve.scalar_tensor_tensor(out=w_lo[1 - u][:, piece], in0=w_raw[1 - u][:, piece], scalar=WS,
                                             in1=w_hi[1 - u][:, piece], op0=ALU.mult, op1=ALU.subtract
                                             ).then_inc(ew_lo.sem, 1)

                dve.wait_ge(bias_ready.sem, bias_ready.at(e, 2))
                dve.sem_inc(passed.sem, 1)
                dve.wait_ge(b2_in[u].sem, b2_in[u].at(j, 1))
                dve.sem_inc(passed.sem, 1)
                def next_expert(n):
                    split_piece(n)
                    if n == PIECES - 1:
                        biases(e + 1, 1 - u)

                tile(lo, u, next_expert if split else lambda n: None)
                with dve.If(lo + 1 < hi):
                    with dve.Fori(lo + 1, hi) as g:
                        tile(g, u, lambda n: None)

            biases(0, 0)
            with dve.Fori(0, E // 2 - 1) as j:
                for u in range(2):
                    expert(j, u, True)
            for u in range(2):
                expert(E // 2 - 1, u, u == 0)

        @block.tensor
        def _(pe):
            start_signals(pe, "tensor")

            def split_product(dst, pairs_h, pairs_l):
                terms = []
                for (ah, al), (bh, bl) in zip(pairs_h, pairs_l):
                    terms += [(ah, bh), (ah, bl), (al, bh)]
                for n, (a, b) in enumerate(terms):
                    ins = pe.matmul(dst, a, b, start=(n == 0), stop=(n == len(terms) - 1))
                return ins

            def turn(t, hl_of, src_ready, rnd, signal):
                dst = turn_banks[t].bitcast(F16)
                for hl in range(2):
                    pe.wait_ge(src_ready[hl].sem, src_ready[hl].at(rnd, t + 1))
                    for c in range(2):
                        n = 2 * hl + c
                        ins = pe.transpose(dst[:, 128 * n:128 * n + 128], hl_of(hl)[:, 128 * c:128 * c + 128], ident[:, :])
                ins.then_inc(signal.sem, 1)

            def tokens(buf, t):
                return [(buf[:, t, 0, c, :], buf[:, t, 1, c, :]) for c in range(2)]

            def embed(i, chunks):
                if 0 in chunks:
                    pe.wait_ge(patch_lo.sem, patch_lo.at(i, 1))
                for c in chunks:
                    wh, wl = w_emb_h[:, c, :], w_emb_l[:, c, :]
                    for n, (a, w) in enumerate(((patch_h, wh), (patch_h, wl), (patch_l, wh))):
                        pe.matmul(PV[0:PR, 1, 0:D], a[:, c, :], w, start=(c == 0 and n == 0), stop=False,
                                  skip_group_check=True)
                if KP - 1 in chunks:
                    pe.matmul(PV[0:PR, 1, 0:D], const("emb_rows", 2), cls_b_sb[:, :], start=False, stop=True,
                              skip_group_check=True).then_inc(emb_ready.sem, 1)

            def turn_xn(i):
                pe.wait_ge(emb_added.sem, emb_added.at(i, 2))
                for t in range(3):
                    for hl, (src, ready) in enumerate(((xn_h, xn_hi), (xn_l, xn_lo))):
                        pe.wait_ge(ready.sem, ready.at(i, t + 1))
                        for c in range(2):
                            n = 2 * hl + c
                            ins = pe.transpose(xn_banks[t].bitcast(F16)[:, 128 * n:128 * n + 128],
                                               src[:, t, 128 * c:128 * c + 128], ident[:, :])
                    ins.then_inc(xn_turned.sem, 1)

            def project(i, t):
                pe.wait_ge(xT_ready.sem, xT_ready.at(i, 1 if t < 2 else 2))
                if t == 2:
                    pe.wait_ge(v_lo.sem, v_lo.at(i, 1))
                    pe.wait_ge(rope.sem, rope.at(i, 3))
                split_product(proj[t][:, 0, :], tokens(xT, t),
                              [(wq_h[:, c, 0:2 * D], wq_l[:, c, 0:2 * D]) for c in range(2)])
                split_product(proj[t][:, 1, 0:D], tokens(xT, t),
                              [(wq_h[:, c, 2 * D:3 * D], wq_l[:, c, 2 * D:3 * D]) for c in range(2)]
                              ).then_inc(qkv_ready.sem, 1)

            def turn_pack(i, t):
                pe.wait_ge(pack_hi.sem, pack_hi.at(i, 2 * t + 2))
                pe.wait_ge(pack_lo.sem, pack_lo.at(i, 2 * t + 2))
                if t < 2:
                    pe.wait_ge(v_lo.sem, v_lo.at(i, t + 2))
                    pe.wait_ge(rope.sem, rope.at(i, 3 * t + 6))
                else:
                    pe.wait_ge(qT_ready.sem, qT_ready.at(i, 1))
                    pe.wait_ge(kT_ready.sem, kT_ready.at(i, 1))
                for m in range(2):
                    src = pack[:, t % 2, m, :, :].rearrange("p h s -> p (h s)")
                    dst = halves(SC[1 - t % 2][:, m, :])
                    for b in range(8):
                        ins = pe.transpose(dst[:, b, :], src[:, 128 * b:128 * b + 128], ident[:, :])
                ins.then_inc(pack_turned.sem, 1)

            def scores(i, items):
                if 0 in items:
                    pe.wait_ge(qT_ready.sem, qT_ready.at(i, 3))
                    pe.wait_ge(kT_ready.sem, kT_ready.at(i, 3))
                for n in items:
                    if n >= 2:
                        pe.wait_ge(max_done.sem, max_done.at(i, n - 1))
                    dst = SC[n % 2]
                    if n >= 4:
                        pe.sem_inc(passed.sem, 1)
                    for par in range(2):
                        rows = slice(64 * par, 64 * par + 64)
                        if n < 4:
                            u, q = n // 2, n % 2
                            pe.matmul(dst[:, par, :], identb[:, :], mask_main[:, :].rearrange("p (a k) -> p a k", a=1
                                                                        ).broadcast_to((128, 4, MAIN)),
                                      start=True, stop=False, skip_group_check=True)
                            for j in range(4):
                                ins = pe.matmul(dst[:, par, MAIN * j:MAIN * j + MAIN], QT[rows, u, 4 * q + j, 0:MAIN],
                                                KT[rows, u, 4 * q + j, 0:MAIN], start=False, stop=True,
                                                skip_group_check=True)
                        else:
                            h, nj = score_heads(n - 4)
                            for u in range(2):
                                for j in range(nj):
                                    q_at = (8 * u + h // 2 + j) * S + MAIN
                                    pe.matmul(dst[TAILS * u:TAILS * u + TAILS, par, S * j:S * j + S],
                                              QT_flat[rows, q_at:q_at + TAILS], KT[rows, u, h // 2 + j, :],
                                              start=(j == 0), stop=False, skip_group_check=True)
                            ins = pe.matmul(dst[:, par, 0:nj * S].rearrange("p (j k) -> p j k", k=S)[:, :, MAIN:S], identb[:, :],
                                            mask_tail[:, MAIN:S].rearrange("p (a k) -> p a k", a=1).broadcast_to((128, nj, TAIL)),
                                            start=False, stop=True, skip_group_check=True)
                    ins.then_inc(s_ready.sem, 1)

            def turn_x2(i):
                for t in range(3):
                    if t == 0:
                        pe.wait_ge(h1_ready.sem, h1_ready.at(i, 3))
                    turn(t, lambda hl: x2_hl[:, t, hl, :], (x2_hi, x2_lo), i, x2_turned)

            def route_logits(i):
                for t in range(3):
                    pe.wait_ge(x2T_ready.sem, x2T_ready.at(i, t + 1))
                    ins = split_product(X[:, 0, E * t:E * t + E], tokens(x2T, t),
                                        [(rw_h[:, c, :], rw_l[:, c, :]) for c in range(2)])
                ins.then_inc(logits_ready.sem, 1)

            def route_counts(i):
                pe.wait_ge(route.sem, route.at(i, 7))
                for t in range(4):
                    terms = [(ones, s) for s in range(min(t, 3))] + ([(before, t)] if t < 3 else [])
                    for n, (a, s) in enumerate(terms):
                        ins = pe.matmul(X[:, 0, E * t:E * t + E], a[:, :], onehot16[:, s, :], start=(n == 0),
                                        stop=(n == len(terms) - 1))
                ins.then_inc(ranks_ready.sem, 1)

            def pair(i, following):
                pe.wait_ge(negm_ready.sem, negm_ready.at(i, 2))
                for t in range(3):
                    ins = pe.transpose(X[:, 1, :].bitcast(F16)[:, 128 * t:128 * t + 128],
                                       neg_m[:, t, :, :].rearrange("p a b -> p (a b)"), ident[:, :])
                ins.then_inc(negm_turned.sem, 1)
                pe.wait_ge(mT_ready.sem, mT_ready.at(i, 2))

                for n in range(7):
                    if n < 2:
                        pe.wait_ge(max_done.sem, max_done.at(i, 6 + n))
                    else:
                        pe.wait_ge(exp_done.sem, exp_done.at(i, n - 1))
                    pe.sem_inc(passed.sem, 1)
                    dst = SC[(n + 7) % 2]
                    if n < 6:
                        (h, nj), us, keys, queries, width = score_heads(n % 3), [n // 3], slice(0, MAIN), slice(0, S), S
                    else:
                        h, nj, us, keys, queries, width = 0, 8, [0, 1], slice(MAIN, S), slice(MAIN, S), TAIL
                    nk = keys.stop - keys.start
                    for par in range(2):
                        if n == 6:
                            pe.matmul(dst[0:PR, par, 0:nj * TAIL], identb[:, 0:PR], mask_t_tail[:, :].rearrange(
                                "p (a k) -> p a k", a=1).broadcast_to((128, nj, TAIL)),
                                start=True, stop=False, skip_group_check=True)
                    for u in us:
                        at = 0 if n < 6 else TAILS * u
                        for par in range(2):
                            rows = slice(64 * par, 64 * par + 64)
                            for j in range(nj):
                                to = dst[at:at + nk, par, width * j:width * j + width]
                                pe.matmul(to, head_sel[:, h + 2 * j + par, 0:nk], mT[:, u, queries],
                                          start=(n < 6 and j == 0), stop=False, skip_group_check=True)
                                ins = pe.matmul(to, KT[rows, u, h // 2 + j, keys], QT[rows, u, h // 2 + j, queries],
                                                start=False, stop=(n == 6), skip_group_check=True)
                            if n < 6:
                                ins = pe.matmul(dst[:, par, 0:nj * S].rearrange("p (j q) -> p j q", q=S)[:, :, 0:MAIN],
                                                identb[:, :], mask_t_main[:, 0:MAIN].rearrange("p (a q) -> p a q", a=1
                                                                                               ).broadcast_to((128, nj, MAIN)),
                                                start=False, stop=True, skip_group_check=True)
                    ins.then_inc(st_ready.sem, 1)

                if following:
                    pe.wait_ge(route.sem, route.before(i))
                    turn_xn(i + 1)

                for u in range(2):
                    pe.wait_ge(p_lo.sem, p_lo.at(i, 2 + u))
                    pe.wait_ge(p_lo_odd.sem, p_lo_odd.at(i, 1 + 2 * u))
                    for h in range(H):
                        ins = split_product(PV[:, u, (DH + 1) * h:(DH + 1) * (h + 1)],
                                            [(P_h[:, u, h, 0:MAIN], P_l[:, u, h, 0:MAIN])],
                                            [(V_h[:, u, h, :], V_l[:, u, h, :])])
                    ins.then_inc(pv_ready.sem, 1)
                if following:
                    pe.wait_ge(xT_ready.sem, xT_ready.at(i + 1, 2))
                for u in range(2):
                    if u == 0:
                        pe.wait_ge(p_lo.sem, p_lo.at(i, 4))
                    else:
                        pe.wait_ge(p_lo_odd.sem, p_lo_odd.at(i, 4))
                    rows = slice(TAILS * u, TAILS * u + TAIL)
                    for h in range(0, H, 2):
                        main = [p[:, u, h:h + 2, :].rearrange("p a q -> p (a q)") for p in (Pq_h, Pq_l)]
                        tail = [t[rows, h:h + 2, :].rearrange("p a q -> p (a q)") for t in (Pt_h_wide, Pt_l_wide)]
                        ins = split_product(X[:, u, (DH + 1) * h:(DH + 1) * (h + 2)], [main, tail],
                                            [[v[:, u, h:h + 2, :].rearrange("p h d -> p (h d)") for v in (V_h, V_l)],
                                             [v[rows, 2, h:h + 2, :].rearrange("p h d -> p (h d)") for v in (V_h, V_l)]])
                    ins.then_inc(pv_ready.sem, 1)

                if following:
                    pe.wait_ge(exp_done.sem, exp_done.at(i, 6))
                    project(i + 1, 0)
                pe.wait_ge(o_ready.sem, o_ready.at(i, 6))
                for t in range(3):
                    turn(t, lambda hl: (O_h, O_l)[hl][:, t, :], (o_hi, o_lo), i, o_turned)
                if following:
                    pe.wait_ge(exp_done.sem, exp_done.at(i, 8))
                    project(i + 1, 1)
                for t in range(3):
                    pe.wait_ge(oT_ready.sem, oT_ready.at(i, t + 1))
                    split_product(wo_banks[t][:, 0:D], tokens(oT, t),
                                  [(wo_h[:, c, :], wo_l[:, c, :]) for c in range(2)]).then_inc(wo_ready.sem, 1)
                if following:
                    project(i + 1, 2)
                    pe.wait_ge(h1_ready.sem, h1_ready.at(i, 1))
                    for t in range(3):
                        turn_pack(i + 1, t)
                        embed(i + 2, range(2 * t, 2 * t + 2))
                    for n in range(7):
                        scores(i + 1, [n])
                        if n == 2:
                            turn_x2(i)
                        if n == 3:
                            route_logits(i)
                        if n == 5:
                            route_counts(i)
                else:
                    turn_x2(i)
                    route_logits(i)
                    route_counts(i)

            pe.wait_ge(w_emb_ready.sem, w_emb_ready.at(0, 1))
            pe.wait_ge(const_in.sem, const_in.at(0, 1))
            embed(0, range(KP))
            pe.wait_ge(const_ready.sem, const_ready.at(0, 11))
            pe.wait_ge(filled.sem, filled.at(0, 5))
            pe.wait_ge(filled_too.sem, filled_too.at(0, 9))
            turn_xn(0)
            pe.wait_ge(w_ready.sem, w_ready.at(0, 3))
            for t in range(3):
                project(0, t)
            for t in range(3):
                turn_pack(0, t)
            scores(0, range(7))
            embed(1, range(KP))
            with pe.Fori(0, PAIRS - 1) as i:
                pair(i, True)
            pair(PAIRS - 1, False)

            def turn_x(g):
                pe.wait_ge(x_in.sem, x_in.at(g, 2))
                for n in range(8):
                    hl, c, s = n // 4, n // 2 % 2, n % 2
                    ins = pe.transpose(PV[:, 0, :].bitcast(F16)[:, HT * n:HT * n + HT],
                                       Xg[:, s, D * hl + 128 * c:D * hl + 128 * c + 128], ident[0:HT, 0:HT])
                ins.then_inc(g_turned.sem, 1)

            pe.wait_ge(tabled.sem, tabled.at(0, 10))
            turn_x(0)
            with pe.Fori(0, E // 2) as j:
                for u in range(2):
                    e = 2 * j + u
                    lo = pe.value_load(table[0:1, bass.ds(e, 1)], min_val=0, max_val=E + MAXT)
                    hi = pe.value_load(table[0:1, bass.ds(e + 1, 1)], min_val=1, max_val=E + MAXT)
                    pe.wait_ge(ew_lo.sem, ew_lo.at(e, PIECES))
                    pe.sem_inc(passed.sem, 1)
                    with pe.Fori(lo, hi) as g:
                        pe.wait_ge(gT_ready.sem, gT_ready.at(g, 1))
                        for k in range(8):
                            if k >= 4:
                                pe.wait_ge(glu_done.sem, glu_done.at(g, k - 3))
                            else:
                                pe.wait_ge(glu_done.sem, glu_done.at(g - 1, k + 5))
                            for part in range(2):
                                at = HID * part + 128 * k
                                ins = split_product(up_banks[k % 4][:, TT * part:TT * part + TT],
                                                    [(w1_h[u][:, c, at:at + 128], w1_l[u][:, c, at:at + 128]) for c in range(2)],
                                                    [(gT[:, 0, c, :], gT[:, 1, c, :]) for c in range(2)])
                            ins.then_inc(up_ready.sem, 1)
                        pe.wait_ge(yo_ready.sem, yo_ready.before(g))
                        for k in range(8):
                            pe.wait_ge(u_lo.sem, u_lo.at(g, k + 1))
                            for s in range(2):
                                uh, ul = (x[:, k, HT * s:HT * s + HT] for x in (u_h, u_l))
                                wh, wl = w2_h[u][:, k, :], w2_l[u][:, k, :]
                                for n, (a, b) in enumerate(((uh, wh), (uh, wl), (ul, wh))):
                                    ins = pe.matmul(y_banks[s][0:HT, 0:D], a, b, start=(k == 0 and n == 0),
                                                    stop=(k == 7 and n == 2))
                                if k == 7:
                                    ins.then_inc(y_ready.sem, 1)
                            if k == 3:
                                turn_x(g + 1)


def by_parity(ap):
    return ap.rearrange("p (j a) n -> p a j n", a=2)


def halves(bank):
    return bank.bitcast(F16).rearrange("p (b n) -> p b n", b=8)


def tail_cols(blocks):
    return blocks.rearrange("p b (u n) -> p u b n", u=2)[:, :, :, 0:TAIL]


def kernel(**inputs):
    import concourse.bacc as bacc
    from concourse.bass_utils import run_bass_kernel_spmd

    def get(name):
        return np.ascontiguousarray(inputs[name])

    x = get("x").reshape(PAIRS, 2, 3, 6, 16, 6, 16).transpose(0, 2, 4, 6, 1, 3, 5).reshape(PAIRS, KP, 128, 2, NPATCH)
    patches = np.zeros((PAIRS + 1, 128, KP, PR), x.dtype)
    for u in range(2):
        patches[:PAIRS, :, :, TAILS * u + 1:TAILS * u + EMB] = x[:, :, :, u].transpose(0, 2, 1, 3)
    qkv = get("L0_attn_W_qkv")
    turned = qkv[:2 * D].reshape(2 * H, DH // 2, 2, D).transpose(0, 2, 1, 3).reshape(2 * D, D)
    qkv = np.concatenate([turned, qkv[2 * D:]], 0)

    def chunks(w):
        return np.ascontiguousarray(w.reshape(-1, 128, w.shape[1]).transpose(1, 0, 2))

    arrays = {
        "patches": patches,
        "txt": get("txt"),
        "w_emb": chunks(get("L0_tok_w").T),
        "cls_b": np.stack([get("L0_tok_cls_token"), get("L0_tok_b")]),
        "pos": get("L0_tok_pos"),
        "w_qkv": chunks(qkv.T),
        "w_o": chunks(get("L0_attn_W_o").T),
        "router_w": chunks(get("L0_ffn_router_w")),
        "router_b": get("L0_ffn_router_b").reshape(1, E),
        "w1": get("L0_ffn_w1"),
        "b1": np.ascontiguousarray(get("L0_ffn_b1").reshape(E, 16, 128).transpose(2, 0, 1)),
        "w2": get("L0_ffn_w2"),
        "b2": get("L0_ffn_b2"),
        "consts": constants(),
    }
    nc = bacc.Bacc("TRN2", target_bir_lowering=False, num_devices=1)
    args = [nc.dram_tensor(f"in_{n}", a.shape, mybir.dt.from_np(a.dtype), kind="ExternalInput").ap()
            for n, a in arrays.items()]
    out = nc.dram_tensor("out", (NTOK, D), F32, kind="ExternalOutput").ap()
    build(nc, *args, out)
    r = run_bass_kernel_spmd(nc, [{f"in_{n}": a for n, a in arrays.items()}], core_ids=[0])
    return r.results[0]["out"].reshape(B, S, D)
```
